# Optimizing a Trainium2 kernel written in Bass

```python
import numpy as np
import jax
import jax.numpy as jnp

def _softmax(x, axis=-1):
    return jax.nn.softmax(x, axis=axis)

def _gelu(x):
    return jax.nn.gelu(x, approximate=True)

def _silu(x):
    return jax.nn.silu(x)

def _sigmoid(x):
    return jax.nn.sigmoid(x)

def _layernorm(x, axis=-1, eps=1e-05):
    m = jnp.mean(x, axis=axis, keepdims=True)
    v = jnp.var(x, axis=axis, keepdims=True)
    return (x - m) / jnp.sqrt(v + eps)

def _scatter_add(tgt, idx, src, axis=0):
    return tgt.at[idx].add(src)

def _segment_sum(src, seg, n):
    return jax.ops.segment_sum(src, seg, n)
kernel_name = 'mk_gnn_preln_d4_gnn_r8_d1b04e'

def setup_inputs(seed: int=0):
    np.random.seed(seed)
    _w = jnp.asarray

    def _rec_inputs():
        import jax
        import jax.numpy as jnp
        _gk = jax.random.key(seed)
        x = -0.0001006 + 1 * jax.random.normal(jax.random.fold_in(_gk, 1), (6250, 96), jnp.float32)
        _s = jax.random.randint(jax.random.fold_in(_gk, 2), (100000,), 0, 6250, jnp.int32)
        _d = jax.random.randint(jax.random.fold_in(_gk, 3), (100000,), 0, 6250, jnp.int32)
        _loop = jnp.arange(6250, dtype=jnp.int32)
        src = jnp.concatenate([_s, _d, _loop])
        dst = jnp.concatenate([_d, _s, _loop])
        _o = jnp.argsort(dst, stable=True)
        src = src[_o]
        dst = dst[_o]
        edge_attr_32 = 0.000196303 + 1.00016 * jax.random.normal(jax.random.fold_in(_gk, 12), (206250, 32), jnp.float32)
        edge_attr_96 = -4.21973e-05 + 0.999841 * jax.random.normal(jax.random.fold_in(_gk, 13), (206250, 96), jnp.float32)
        return (x, src, dst, edge_attr_32, edge_attr_96)
    x, src, dst, edge_attr_32, edge_attr_96 = _rec_inputs()

    def _L0_gnn_setup():
        import jax, jax.numpy as jnp
        import numpy as np
        N_NODES = 6250
        N_EDGES = 100000
        EMB = 96
        HID = 2 * EMB
        key = jax.random.key(seed)
        ks = jax.random.split(key, 8)
        h = jax.random.normal(ks[0], (N_NODES, EMB), dtype=jnp.float32)
        edge_attr = jax.random.normal(ks[1], (N_EDGES, EMB), dtype=jnp.float32)
        src = jax.random.randint(ks[2], (N_EDGES,), 0, N_NODES, dtype=jnp.int32)
        dst = jax.random.randint(ks[3], (N_EDGES,), 0, N_NODES, dtype=jnp.int32)
        W1 = jax.random.normal(ks[4], (EMB, HID), dtype=jnp.float32) * (1.0 / np.sqrt(EMB))
        b1 = jnp.zeros((HID,), dtype=jnp.float32)
        W2 = jax.random.normal(ks[5], (HID, EMB), dtype=jnp.float32) * (1.0 / np.sqrt(HID))
        b2 = jnp.zeros((EMB,), dtype=jnp.float32)
        eps = jnp.zeros((1,), dtype=jnp.float32)
        return {'h': h, 'edge_attr': edge_attr, 'src': src, 'dst': dst, 'W1': W1, 'b1': b1, 'W2': W2, 'b2': b2, 'eps': eps}
    _L0_gnn_all = _L0_gnn_setup()
    _L0_gnn_in = {k: v for k, v in _L0_gnn_all.items() if k in ('W1', 'b1', 'W2', 'b2', 'eps')}
    del _L0_gnn_all

    def _L1_gnn_setup():
        import jax, jax.numpy as jnp
        import numpy as np
        N_NODES = 6250
        N_EDGES = 100000
        IN_DIM = 96
        OUT_DIM = 96
        EDGE_DIM = 32
        BN_EPS = 1e-05
        key = jax.random.key(seed)
        ks = jax.random.split(key, 12)
        x = jax.random.normal(ks[0], (N_NODES, IN_DIM), dtype=jnp.float32)
        edge_index = jax.random.randint(ks[1], (2, N_EDGES), 0, N_NODES, dtype=jnp.int64)
        edge_attr = jax.random.normal(ks[2], (N_EDGES, EDGE_DIM), dtype=jnp.float32)
        We = jax.random.normal(ks[3], (EDGE_DIM, IN_DIM), dtype=jnp.float32) / np.sqrt(EDGE_DIM)
        be = jnp.zeros((IN_DIM,), dtype=jnp.float32)
        W1 = jax.random.normal(ks[4], (IN_DIM, OUT_DIM), dtype=jnp.float32) / np.sqrt(IN_DIM)
        b1 = jnp.zeros((OUT_DIM,), dtype=jnp.float32)
        W2 = jax.random.normal(ks[5], (OUT_DIM, OUT_DIM), dtype=jnp.float32) / np.sqrt(OUT_DIM)
        b2 = jnp.zeros((OUT_DIM,), dtype=jnp.float32)
        gamma = jnp.ones((OUT_DIM,), dtype=jnp.float32)
        beta = jnp.zeros((OUT_DIM,), dtype=jnp.float32)
        return {'x': x, 'edge_index': edge_index, 'edge_attr': edge_attr, 'We': We, 'be': be, 'W1': W1, 'b1': b1, 'W2': W2, 'b2': b2, 'gamma': gamma, 'beta': beta}
    _L1_gnn_all = _L1_gnn_setup()
    _L1_gnn_in = {k: v for k, v in _L1_gnn_all.items() if k in ('We', 'be', 'W1', 'b1', 'W2', 'b2', 'gamma', 'beta')}
    del _L1_gnn_all

    def _L2_gnn_setup():
        import jax, jax.numpy as jnp
        import numpy as np
        N_NODES = 6250
        N_EDGES = 100000
        D = 96
        N_LAYERS = 3
        key = jax.random.key(seed)
        ks = jax.random.split(key, 8)
        s = 1.0 / np.sqrt(D)
        x = jax.random.normal(ks[0], (N_NODES, D), dtype=jnp.float32)
        edge_index = jax.random.randint(ks[1], (2, N_EDGES), 0, N_NODES, dtype=jnp.int32)
        W_in = jax.random.normal(ks[2], (D, D), dtype=jnp.float32) * s
        b_in = jnp.zeros((D,), dtype=jnp.float32)
        gcn_W = jax.random.normal(ks[3], (N_LAYERS, D, D), dtype=jnp.float32) * s
        gcn_b = jnp.zeros((N_LAYERS, D), dtype=jnp.float32)
        W_out = jax.random.normal(ks[4], (D, D), dtype=jnp.float32) * s
        b_out = jnp.zeros((D,), dtype=jnp.float32)
        return {'x': x, 'edge_index': edge_index, 'W_in': W_in, 'b_in': b_in, 'gcn_W': gcn_W, 'gcn_b': gcn_b, 'W_out': W_out, 'b_out': b_out}
    _L2_gnn_all = _L2_gnn_setup()
    _L2_gnn_in = {k: v for k, v in _L2_gnn_all.items() if k in ('W_in', 'b_in', 'gcn_W', 'gcn_b', 'W_out', 'b_out')}
    del _L2_gnn_all

    def _L3_gnn_setup():
        import jax, jax.numpy as jnp
        import numpy as np
        N_NODES = 6250
        N_EDGES = 100000
        DIM = 96
        HEADS = 4
        LAYERS = 3
        NEG_SLOPE = 0.2

        def _gat_layer(x, src, dst, W, a_src, a_dst, b):
            N = x.shape[0]
            H, C = a_src.shape
            h = (x @ W).reshape(N, H, C)
            alpha_s = jnp.einsum('nhc,hc->nh', h, a_src)
            alpha_d = jnp.einsum('nhc,hc->nh', h, a_dst)
            e = jax.nn.leaky_relu(alpha_s[src] + alpha_d[dst], NEG_SLOPE)
            m = jax.ops.segment_max(e, dst, num_segments=N)
            m = jnp.where(jnp.isfinite(m), m, 0.0)
            ex = jnp.exp(e - m[dst])
            den = jax.ops.segment_sum(ex, dst, num_segments=N)
            alpha = ex / (den[dst] + 1e-16)
            msg = h[src] * alpha[:, :, None]
            out = jax.ops.segment_sum(msg, dst, num_segments=N)
            return out.reshape(N, H * C) + b
        key = jax.random.key(seed)
        ks = jax.random.split(key, 6)
        C = DIM // HEADS
        x = jax.random.normal(ks[0], (N_NODES, DIM), dtype=jnp.float32)
        edge_index = jax.random.randint(ks[1], (2, N_EDGES), 0, N_NODES, dtype=jnp.int32)
        W = jax.random.normal(ks[2], (LAYERS, DIM, DIM), dtype=jnp.float32) * (1.0 / np.sqrt(DIM))
        att_src = jax.random.normal(ks[3], (LAYERS, HEADS, C), dtype=jnp.float32) * (1.0 / np.sqrt(C))
        att_dst = jax.random.normal(ks[4], (LAYERS, HEADS, C), dtype=jnp.float32) * (1.0 / np.sqrt(C))
        bias = jnp.zeros((LAYERS, DIM), dtype=jnp.float32)
        return {'x': x, 'edge_index': edge_index, 'W': W, 'att_src': att_src, 'att_dst': att_dst, 'bias': bias}
    _L3_gnn_all = _L3_gnn_setup()
    _L3_gnn_in = {k: v for k, v in _L3_gnn_all.items() if k in ('W', 'att_src', 'att_dst', 'bias')}
    del _L3_gnn_all
    return {'x': x, 'src': src, 'dst': dst, 'edge_attr_32': edge_attr_32, 'edge_attr_96': edge_attr_96, 'L0_gnn_W1': _L0_gnn_in['W1'], 'L0_gnn_b1': _L0_gnn_in['b1'], 'L0_gnn_W2': _L0_gnn_in['W2'], 'L0_gnn_b2': _L0_gnn_in['b2'], 'L0_gnn_eps': _L0_gnn_in['eps'], 'L1_gnn_We': _L1_gnn_in['We'], 'L1_gnn_be': _L1_gnn_in['be'], 'L1_gnn_W1': _L1_gnn_in['W1'], 'L1_gnn_b1': _L1_gnn_in['b1'], 'L1_gnn_W2': _L1_gnn_in['W2'], 'L1_gnn_b2': _L1_gnn_in['b2'], 'L1_gnn_gamma': _L1_gnn_in['gamma'], 'L1_gnn_beta': _L1_gnn_in['beta'], 'L2_gnn_W_in': _L2_gnn_in['W_in'], 'L2_gnn_b_in': _L2_gnn_in['b_in'], 'L2_gnn_gcn_W': _L2_gnn_in['gcn_W'], 'L2_gnn_gcn_b': _L2_gnn_in['gcn_b'], 'L2_gnn_W_out': _L2_gnn_in['W_out'], 'L2_gnn_b_out': _L2_gnn_in['b_out'], 'L3_gnn_W': _L3_gnn_in['W'], 'L3_gnn_att_src': _L3_gnn_in['att_src'], 'L3_gnn_att_dst': _L3_gnn_in['att_dst'], 'L3_gnn_bias': _L3_gnn_in['bias']}

def reference(x, src, dst, edge_attr_32, edge_attr_96, L0_gnn_W1, L0_gnn_b1, L0_gnn_W2, L0_gnn_b2, L0_gnn_eps, L1_gnn_We, L1_gnn_be, L1_gnn_W1, L1_gnn_b1, L1_gnn_W2, L1_gnn_b2, L1_gnn_gamma, L1_gnn_beta, L2_gnn_W_in, L2_gnn_b_in, L2_gnn_gcn_W, L2_gnn_gcn_b, L2_gnn_W_out, L2_gnn_b_out, L3_gnn_W, L3_gnn_att_src, L3_gnn_att_dst, L3_gnn_bias):
    import jax
    import jax.numpy as jnp

    def _L0_gnn_ref(h, edge_attr, src, dst, W1, b1, W2, b2, eps):
        import jax, jax.numpy as jnp
        import numpy as np
        N_NODES = 6250
        N_EDGES = 100000
        EMB = 96
        HID = 2 * EMB
        m = h[src] + edge_attr
        aggr = jax.ops.segment_sum(m, dst, num_segments=N_NODES)
        hidden = jax.nn.relu(aggr @ W1 + b1)
        mlp_out = hidden @ W2 + b2
        out = (1.0 + eps[0]) * h + mlp_out
        return out

    def _L1_gnn_ref(x, edge_index, edge_attr, We, be, W1, b1, W2, b2, gamma, beta):
        import jax, jax.numpy as jnp
        import numpy as np
        N_NODES = 6250
        N_EDGES = 100000
        IN_DIM = 96
        OUT_DIM = 96
        EDGE_DIM = 32
        BN_EPS = 1e-05
        src = edge_index[0]
        dst = edge_index[1]
        msg = jax.nn.relu(x[src] + edge_attr @ We + be)
        aggr = jax.ops.segment_sum(msg, dst, num_segments=x.shape[0])
        h = x + aggr
        h = jax.nn.relu(h @ W1 + b1) @ W2 + b2
        mean = jnp.mean(h, axis=0)
        var = jnp.mean(jnp.square(h - mean), axis=0)
        h = (h - mean) * jax.lax.rsqrt(var + BN_EPS) * gamma + beta
        return jax.nn.relu(h)

    def _L2_gnn_ref(x, edge_index, W_in, b_in, gcn_W, gcn_b, W_out, b_out):
        import jax, jax.numpy as jnp
        import numpy as np
        N_NODES = 6250
        N_EDGES = 100000
        D = 96
        N_LAYERS = 3
        N = x.shape[0]
        loop = jnp.arange(N, dtype=edge_index.dtype)
        row = jnp.concatenate([edge_index[0], loop])
        col = jnp.concatenate([edge_index[1], loop])
        deg = jax.ops.segment_sum(jnp.ones_like(col, dtype=x.dtype), col, num_segments=N)
        dinv = jnp.where(deg > 0, jax.lax.rsqrt(deg), 0.0)
        norm = (dinv[row] * dinv[col])[:, None]

        def gcn_conv(h, W, b):
            hw = h @ W.T
            msg = norm * hw[row]
            out = jax.ops.segment_sum(msg, col, num_segments=N)
            return out + b
        h = jax.nn.relu(x @ W_in.T + b_in)
        for l in range(N_LAYERS):
            h = h + jax.nn.relu(gcn_conv(h, gcn_W[l], gcn_b[l]))
        return h @ W_out.T + b_out

    def _L3_gnn_ref(x, edge_index, W, att_src, att_dst, bias):
        import jax, jax.numpy as jnp
        import numpy as np
        N_NODES = 6250
        N_EDGES = 100000
        DIM = 96
        HEADS = 4
        LAYERS = 3
        NEG_SLOPE = 0.2

        def _gat_layer(x, src, dst, W, a_src, a_dst, b):
            N = x.shape[0]
            H, C = a_src.shape
            h = (x @ W).reshape(N, H, C)
            alpha_s = jnp.einsum('nhc,hc->nh', h, a_src)
            alpha_d = jnp.einsum('nhc,hc->nh', h, a_dst)
            e = jax.nn.leaky_relu(alpha_s[src] + alpha_d[dst], NEG_SLOPE)
            m = jax.ops.segment_max(e, dst, num_segments=N)
            m = jnp.where(jnp.isfinite(m), m, 0.0)
            ex = jnp.exp(e - m[dst])
            den = jax.ops.segment_sum(ex, dst, num_segments=N)
            alpha = ex / (den[dst] + 1e-16)
            msg = h[src] * alpha[:, :, None]
            out = jax.ops.segment_sum(msg, dst, num_segments=N)
            return out.reshape(N, H * C) + b
        src = edge_index[0]
        dst = edge_index[1]
        for l in range(W.shape[0]):
            x = jax.nn.relu(_gat_layer(x, src, dst, W[l], att_src[l], att_dst[l], bias[l]))
        return x
    edge_index = jnp.stack([src, dst])
    h = jnp.maximum(_layernorm(x, axis=-1), 0.0)
    x = x + _L0_gnn_ref(h, edge_attr_96, src, dst, L0_gnn_W1, L0_gnn_b1, L0_gnn_W2, L0_gnn_b2, L0_gnn_eps)
    h = jnp.maximum(_layernorm(x, axis=-1), 0.0)
    x = x + _L1_gnn_ref(h, edge_index, edge_attr_32, L1_gnn_We, L1_gnn_be, L1_gnn_W1, L1_gnn_b1, L1_gnn_W2, L1_gnn_b2, L1_gnn_gamma, L1_gnn_beta)
    h = jnp.maximum(_layernorm(x, axis=-1), 0.0)
    x = x + _L2_gnn_ref(h, edge_index, L2_gnn_W_in, L2_gnn_b_in, L2_gnn_gcn_W, L2_gnn_gcn_b, L2_gnn_W_out, L2_gnn_b_out)
    h = jnp.maximum(_layernorm(x, axis=-1), 0.0)
    x = x + _L3_gnn_ref(h, edge_index, L3_gnn_W, L3_gnn_att_src, L3_gnn_att_dst, L3_gnn_bias)
    return x

_drawn_inputs = setup_inputs


def setup_inputs(seed=0):
    import zlib

    import numpy as np

    out = dict(_drawn_inputs(seed))
    spreads = {'L0_gnn_b1': (0.0, 0.8),
     'L0_gnn_b2': (0.0, 0.8),
     'L1_gnn_be': (0.0, 0.8),
     'L1_gnn_b1': (0.0, 0.8),
     'L1_gnn_b2': (0.0, 0.8),
     'L1_gnn_gamma': (1.0, 0.6),
     'L1_gnn_beta': (0.0, 0.8),
     'L2_gnn_b_in': (0.0, 0.662),
     'L2_gnn_gcn_b': (0.0, 0.563),
     'L2_gnn_b_out': (0.0, 0.8),
     'L3_gnn_bias': (0.0, 0.8)}
    factors = {'L3_gnn_W': 2.9, 'L3_gnn_att_src': 8.0, 'L3_gnn_att_dst': 8.0}
    for name, (base, spread) in spreads.items():
        noise = np.random.default_rng([zlib.crc32(name.encode()), seed]).standard_normal(out[name].shape)
        drawn = base * np.exp(spread * noise) if base else spread * noise
        out[name] = jnp.asarray(drawn.astype(out[name].dtype))
    for name, factor in factors.items():
        out[name] = (out[name] * factor).astype(out[name].dtype)
    return out
```

```python
import concourse.bass as bass
from concourse import mybir
from contextlib import ExitStack


def gnn_kernel(nc, x, src, dst, edge_attr_32, edge_attr_96, L0_W1, L0_b1, L0_W2, L0_b2, L0_eps,
               L1_We, L1_be, L1_W1, L1_b1, L1_W2, L1_b2, L1_gamma, L1_beta,
               L2_W_in, L2_b_in, L2_gcn_W, L2_gcn_b, L2_W_out, L2_b_out,
               L3_W, L3_att_src, L3_att_dst, L3_bias, out):
    f32, i32, bf16 = mybir.dt.float32, mybir.dt.int32, mybir.dt.bfloat16
    ALU, ACT, AX = mybir.AluOpType, mybir.ActivationFunctionType, mybir.AxisListType
    DVE, PE, SP, ACTE = (mybir.EngineType.DVE, mybir.EngineType.PE, mybir.EngineType.SP,
                         mybir.EngineType.Activation)
    ds = bass.ds

    P = 128
    N, D = x.shape
    E = src.shape[0]
    DE = edge_attr_32.shape[1]
    LAYERS, HEADS, C = L3_att_src.shape
    WT = D + HEADS
    NB = -(-N // P)
    Q = 4
    NG = -(-NB // Q)
    NBP = NG * Q
    FULL = N // P
    REST = N - FULL * P
    U = 8
    LANES = P // HEADS
    STEPS = -(-(-(-E // P) + NB) // P) * P
    GROUPS = STEPS // U
    ITERS = GROUPS // 2
    LT = STEPS // LANES
    JG = LT // Q
    BIG = 1.0e30
    LN_EPS = BN_EPS = 1e-5
    SLOPE = 0.2
    EP = max(d for d in range(1, P + 1) if E % d == 0)
    EF = E // EP
    ET = -(-E // P)
    KC = -(-STEPS // P)
    assert STEPS % P == 0 and LT % Q == 0 and GROUPS % 2 == 0 and NG == JG and STEPS <= 4 * 512

    ctx = ExitStack()
    with ctx:
        def sb(name, shape, dt=f32):
            return ctx.enter_context(nc.sbuf_tensor("sb_" + name, shape, dt))

        def sem(name):
            return ctx.enter_context(nc.semaphore(name))

        def dram(name, shape, dt):
            return nc.dram_tensor(name, shape, dt, kind="Internal").ap()

        table = dram("feature_table", [NBP * P, D], f32)
        gat_table = dram("attention_table", [NBP * P, WT], f32)
        stage = dram("gathered_rows", [P, STEPS, WT], f32)
        src_rows = dram("src_rows", [ET, P], i32)
        dst_rows = dram("dst_rows", [ET, P], i32)

        X = sb("X", [P, NBP, D])
        H = sb("H", [P, NBP, D])
        ACC = sb("ACC", [P, NBP, WT])
        S = sb("S", [P, STEPS, HEADS])
        DL = sb("DL", [P, STEPS, HEADS])
        LN = sb("LN", [P, LT * P])
        CUT = sb("CUT", [P, LT * P + 1], bf16)
        IDX = sb("IDX", [P, STEPS], i32)
        REL = sb("REL", [P, STEPS], bf16)
        EB = sb("EB", [65, STEPS], i32)
        HOT = sb("HOT", [P, 2, U, P])
        G = sb("G", [P, 2, U, WT])
        EA = sb("EA", [P, 2, U * D])
        NOW = sb("NOW", [P, 2, U], i32)
        iota_row = sb("iota_row", [P, P])
        iota_col = sb("iota_col", [P, 1])
        ident = sb("ident", [P, P])
        ones = sb("ones", [P, P])
        WTS = sb("WTS", [D, 14, D])
        WE = sb("WE", [P, P // DE, D])
        ROWS = sb("ROWS", [P, 7 + 4 * LAYERS, D])
        BCOL = sb("BCOL", [D, 3])
        DD = sb("DD", [P, NBP, HEADS])
        dinv = sb("dinv", [P, NBP])
        stat = sb("stat", [P, 2, NBP])
        epsp = sb("epsp", [P, 1])
        valid = sb("valid", [P, 1])
        plan = sb("plan", [P, 8])
        tiles_i = sb("tiles_i", [P, 3], i32)
        row_i = sb("row_i", [P, KC], i32)
        crow = EB[0:1, 0:8 * P].bitcast(f32).rearrange("p (a b) -> p a b", a=8)
        ccol = sb("ccol", [P, 4])

        zb = HOT[:, 0, 0:4, :].rearrange("p a b -> p (a b)")
        zT = HOT[:, 0, 4:8, :].rearrange("p a b -> p (a b)")
        hid = HOT[:, 1, :, :].rearrange("p (q a) b -> p q (a b)", q=2)
        tmp = HOT[:, 1, 0:4, :].rearrange("p a b -> p (a b)")
        ST = EA[:, :, :].rearrange("p a b -> p (a b)")[:, 0:U * P].rearrange("p (a b) -> p a b", a=U)
        S_flat = S[:, :, :].rearrange("p k h -> p (k h)")
        D_flat = DL[:, :, :].rearrange("p k h -> p (k h)")
        ind = S_flat[:, 0:STEPS]
        dabs = S_flat[:, 0:STEPS]
        first = S_flat[:, STEPS:2 * STEPS]
        keep = S_flat[:, 2 * STEPS:3 * STEPS]
        block_of = S_flat[:, 3 * STEPS:4 * STEPS]
        win_i = [D_flat[:, n * STEPS:(n + 1) * STEPS].bitcast(i32) for n in range(2)]
        win_f = [D_flat[:, (n + 2) * STEPS:(n + 3) * STEPS] for n in range(2)]
        iota_k = LN[:, 3 * STEPS:4 * STEPS]
        dst_i = LN[0:EP, 0:EF].bitcast(i32)
        dst_f = LN[0:EP, EF:2 * EF]
        upper = LN[0:NB, 2 * EF:2 * EF + P][:, 0:NB]
        step_of = LN[0:NB, 2 * EF + P:2 * EF + 2 * P][:, 0:NB]
        edge_dv = LN[0:NB, 2 * EF + 2 * P:2 * EF + 3 * P]
        cnt = LN[:, 2 * EF + 3 * P:2 * EF + 3 * P + NB + 1]
        assert 2 * EF + 4 * P <= 3 * STEPS and NB < P
        less = ACC[:, :, :].rearrange("p b d -> p (b d)")[0:EP, 0:EF]
        ACCF = ACC[:, :, 0:D]
        scratch = ACC[:, :, :].rearrange("p b d -> p (b d)")[:, 0:LT * P // 2]
        S_strands = S[:, :, :].rearrange("p (i j) h -> p j i h", j=LT)
        D_strands = DL[:, :, :].rearrange("p (i j) h -> p j i h", j=LT)
        dabs_strands = dabs.rearrange("p (i j) -> p j i", j=LT)

        sums = [ctx.enter_context(nc.psum_tensor(f"sums{j}", [P, 2, 512], f32)) for j in range(2)]
        psA, psB, psC, psD = (ctx.enter_context(nc.psum_tensor(f"ps{c}", [P, 512], f32)) for c in "ABCD")

        def row(n):
            return ROWS[:, n:n + 1, :]
        R_L0B2, R_BE, R_L1B2, R_GAMMA, R_BETA, R_BIN, R_BOUT = range(7)
        R_GCNB, R_GATB, R_ASRC, R_ADST = 7, 7 + LAYERS, 7 + 2 * LAYERS, 7 + 3 * LAYERS
        W_L0A, W_L0B, W_L0C, W_L0D, W_L11, W_L12, W_IN, W_GCN, W_OUT = 0, 1, 2, 3, 4, 5, 6, 7, 10
        W_GAT = 11
        TURNED = [W_IN, W_GCN, W_GCN + 1, W_GCN + 2, W_OUT]

        x_in, dst_in, const_in, weights_in = sem("x_in"), sem("dst_in"), sem("const_in"), sem("weights_in")
        iota_done, consts_done = sem("iota_done"), sem("consts_done")
        setup_operand, setup_product = sem("setup_operand"), sem("setup_product")
        plan_ready = sem("plan_ready")
        rows_in, windows_in = sem("rows_in"), sem("windows_in")
        chain = sem("chain")
        var_ready, root_ready = sem("var_ready"), sem("root_ready")
        table_ready, table_stored = sem("table_ready"), sem("table_stored")
        z_ready = sem("z_ready")
        carry_operand, carry_product = sem("carry_operand"), sem("carry_product")
        weights_ready, exp_done = sem("weights_ready"), sem("exp_done")
        strands_ready = sem("strands_ready")
        idx_seen = sem("idx_seen")
        result_ready, out_done = sem("result_ready"), sem("out_done")

        NAMES = ["idx_ready", "attr_in0", "attr_in1", "hot_built", "rows_ready",
                 "seg_done", "acc_step", "ea_flipped", "ea_lifted", "ea_product", "summed",
                 "hot_read", "st_ready", "d_product", "d_copied", "s_copied", "stored0", "stored1",
                 "stage_in0", "stage_in1", "w_copied",
                 "staged", "flipped", "lifted", "hid_product", "hid_ready", "made", "taken",
                 "leaky_done", "logit_done"]
        SEM = {n: sem(n) for n in NAMES}
        START = {"seg_done": 2, "acc_step": 2 * U} | {n: 1 for n in (
            "flipped", "lifted", "taken", "hid_ready", "ea_lifted", "summed", "st_ready", "d_product",
            "d_copied", "logit_done")}
        gather = {"idx_ready": GROUPS}
        segment = {"hot_built": GROUPS, "seg_done": GROUPS, "acc_step": STEPS}
        attrs = {"attr_in0": ITERS * U * 16, "attr_in1": ITERS * U * 16, "rows_ready": GROUPS}
        dense = {n: NG for n in ("staged", "flipped", "lifted", "made", "taken")}
        MOVES = {
            "sum_attr": gather | segment | attrs,
            "sum_relu": gather | segment | attrs | {"ea_flipped": GROUPS, "ea_lifted": GROUPS,
                                                    "ea_product": 2 * GROUPS, "summed": 2 * GROUPS},
            "sum": gather | segment,
            "fetch": gather | {n: GROUPS for n in ("hot_built", "hot_read", "st_ready", "d_product",
                                                   "d_copied", "s_copied")}
                     | {"stored0": ITERS * 16, "stored1": ITERS * 16},
            "weigh": segment | {"stage_in0": ITERS * 16, "stage_in1": ITERS * 16,
                                "rows_ready": GROUPS, "w_copied": GROUPS},
            "dense": dense,
            "mlp1": dense | {"hid_product": NG, "hid_ready": NG},
            "mlp2": dense | {"hid_product": 2 * NG, "hid_ready": 2 * NG},
            "strand": {n: JG for n in ("staged", "flipped", "lifted")},
            "unstrand": {n: JG for n in ("staged", "made", "taken", "leaky_done", "logit_done")},
        }
        PLAN = [("flags", "strand"), ("L0", "sum_attr"), ("L0mlp", "mlp2"), ("L1", "sum_relu"),
                ("L1mlp", "mlp1"), ("in", "dense")]
        for l in range(LAYERS):
            PLAN += [(f"gcn{l}", "dense"), (f"gcnsum{l}", "sum")]
        PLAN += [("out", "dense")]
        for l in range(LAYERS):
            PLAN += [(f"gat{l}", "dense"), (f"fetch{l}", "fetch"), (f"strand{l}", "strand"),
                     (f"unstrand{l}", "unstrand"), (f"weigh{l}", "weigh")]

        GATHERED = {name: [sem(f"gathered{half}_{name}") for half in range(2)]
                    for name, kind in PLAN if "idx_ready" in MOVES[kind]}

        class Stage:
            def __init__(self, name):
                n = [a for a, _ in PLAN].index(name)
                self.base = {s: START.get(s, 0) + sum(MOVES[k].get(s, 0) for _, k in PLAN[:n]) for s in NAMES}
                self.gathered = GATHERED.get(name)
                self.end = {s: self.base[s] + MOVES[PLAN[n][1]].get(s, 0) for s in NAMES}

        def firsts(k, n, engine):
            return nc.values_load_multi_w_load_instructions(
                EB[32:33, ds(k, n)], engines=(engine,), min_val=0, max_val=E - P,
                skip_runtime_bounds_check_because="the plan clips them")[1]

        def blocks(k, n, engine):
            return nc.values_load_multi_w_load_instructions(
                EB[64:65, ds(k, n)], engines=(engine,), min_val=0, max_val=NB - 1,
                skip_runtime_bounds_check_because="the plan clips them")[1]

        block = ctx.enter_context(nc.Block())

        @block.sync
        def _(sp):
            for to, of in ((src_rows, src), (dst_rows, dst)):
                sp.dma_start(to[0:ET - 1, :], of[0:(ET - 1) * P].rearrange("(r e) -> r e", e=P)).then_inc(rows_in, 16)
                sp.dma_start(to[ET - 1:ET, :], of[E - P:E].unsqueeze(0)).then_inc(rows_in, 16)
            sp.dma_start(dst_i, dst.rearrange("(p f) -> p f", p=EP)).then_inc(dst_in, 16)
            sp.dma_start(X[:, 0:FULL, :], x[0:FULL * P, :].rearrange("(b p) d -> p b d", p=P)).then_inc(x_in, 16)
            sp.wait_ge(consts_done, 2)
            sp.dma_start(X[0:REST, FULL, :], x[FULL * P:N, :]).then_inc(x_in, 16)
            vectors = [(R_L0B2, L0_b2), (R_BE, L1_be), (R_L1B2, L1_b2), (R_GAMMA, L1_gamma),
                       (R_BETA, L1_beta), (R_BIN, L2_b_in), (R_BOUT, L2_b_out)]
            for n, v in vectors:
                sp.dma_start(ROWS[:, n, :], v.partition_broadcast(P)).then_inc(const_in, 16)
            for n, m in [(R_GCNB, L2_gcn_b), (R_GATB, L3_bias),
                         (R_ASRC, L3_att_src.rearrange("l h c -> l (h c)")),
                         (R_ADST, L3_att_dst.rearrange("l h c -> l (h c)"))]:
                sp.dma_start(ROWS[:, n:n + LAYERS, :], m.partition_broadcast(P)).then_inc(const_in, 16)
            sp.dma_start(epsp[:, :], L0_eps.partition_broadcast(P)).then_inc(const_in, 16)
            with nc.allow_non_contiguous_dma(reason="three short columns"):
                sp.dma_start(BCOL[:, 0:2], L0_b1.rearrange("(q d) -> d q", q=2)).then_inc(const_in, 16)
                sp.dma_start(BCOL[:, 2:3], L1_b1.rearrange("(d a) -> d a", a=1)).then_inc(const_in, 16)
            sp.dma_start(WTS[:, W_L0A:W_L0B + 1, :], L0_W1.rearrange("k (q n) -> k q n", q=2)).then_inc(weights_in, 16)
            sp.dma_start(WTS[:, W_L0C:W_L0D + 1, :], L0_W2.rearrange("(q k) n -> k q n", q=2)).then_inc(weights_in, 16)
            sp.dma_start(WTS[:, W_L11, :], L1_W1).then_inc(weights_in, 16)
            sp.dma_start(WTS[:, W_L12, :], L1_W2).then_inc(weights_in, 16)
            sp.dma_start(WTS[:, W_IN, :], L2_W_in).then_inc(weights_in, 16)
            sp.dma_start(WTS[:, W_GCN:W_GCN + LAYERS, :], L2_gcn_W.rearrange("l a b -> a l b")).then_inc(weights_in, 16)
            sp.dma_start(WTS[:, W_OUT, :], L2_W_out).then_inc(weights_in, 16)
            sp.dma_start(WTS[:, W_GAT:W_GAT + LAYERS, :], L3_W.rearrange("l a b -> a l b")).then_inc(weights_in, 16)
            for r in range(P // DE):
                sp.dma_start(WE[r * DE:(r + 1) * DE, r, :], L1_We).then_inc(weights_in, 16)

            tables = [0]

            def store_table(to, of):
                tables[0] += 1
                sp.wait_ge(table_ready, tables[0])
                sp.dma_start(to.rearrange("(b p) d -> p b d", p=P), of).then_inc(table_stored, 16)

            def load_attrs(t, attr, width, freed):
                at, name = t.base[freed], SEM[freed]
                for half in range(2):
                    e = firsts(half * U, U, SP)
                    for n in range(U):
                        sp.dma_start(EA[:, half, n * width:(n + 1) * width],
                                     attr[ds(e[n], P), :]).then_inc(SEM[f"attr_in{half}"], 16)
                with sp.Fori(1, ITERS) as it:
                    e = firsts(2 * U * it, 2 * U, SP)
                    for half in range(2):
                        sp.wait_ge(name, 2 * it + (at + half - 1))
                        for n in range(U):
                            sp.dma_start(EA[:, half, n * width:(n + 1) * width],
                                         attr[ds(e[half * U + n], P), :]).then_inc(SEM[f"attr_in{half}"], 16)

            store_table(table, H[:, :, :])
            load_attrs(Stage("L0"), edge_attr_96, D, "rows_ready")
            store_table(table, ACCF)
            sp.wait_ge(table_stored, 32)
            load_attrs(Stage("L1"), edge_attr_32, DE, "ea_flipped")
            for l in range(LAYERS):
                store_table(table, ACCF)
            for l in range(LAYERS):
                store_table(gat_table, ACC[:, :, :])
                t = Stage(f"fetch{l}")
                with sp.Fori(0, ITERS) as it:
                    for half in range(2):
                        sp.wait_ge(t.gathered[half], 16 * U * it + 16 * U)
                        sp.dma_start(stage[:, ds(2 * U * it + U * half, U), :],
                                     G[:, half, :, :]).then_inc(SEM[f"stored{half}"], 16)
                for half in range(2):
                    sp.wait_ge(SEM[f"stored{half}"], t.end[f"stored{half}"])
                sp.wait_ge(SEM["s_copied"], t.end["s_copied"])
                t = Stage(f"weigh{l}")
                with sp.Fori(0, ITERS) as it:
                    for half in range(2):
                        sp.wait_ge(SEM["seg_done"], 2 * it + (t.base["seg_done"] + half - 1))
                        sp.dma_start(G[:, half, :, :], stage[:, ds(2 * U * it + U * half, U), :])\
                          .then_inc(SEM[f"stage_in{half}"], 16)
            sp.wait_ge(result_ready, 1)
            sp.dma_start(out[0:FULL * P, :].rearrange("(b p) d -> p b d", p=P), X[:, 0:FULL, :]).then_inc(out_done, 16)
            sp.dma_start(out[FULL * P:N, :], X[0:REST, FULL, :]).then_inc(out_done, 16)
            sp.wait_ge(out_done, 32)

        @block.gpsimd
        def _(pool):
            nc.gpsimd.iota(iota_row[:, :], [[1, P]], base=0, channel_multiplier=0,
                           allow_small_or_imprecise_dtypes=True).then_inc(iota_done, 1)
            nc.gpsimd.iota(iota_col[:, :], [[0, 1]], base=0, channel_multiplier=1,
                           allow_small_or_imprecise_dtypes=True).then_inc(iota_done, 1)
            nc.gpsimd.iota(iota_k, [[1, STEPS]], base=0, channel_multiplier=0,
                           allow_small_or_imprecise_dtypes=True).then_inc(iota_done, 1)

            pool.wait_ge(rows_in, 64)
            pool.wait_ge(plan_ready, 2)
            for n, rows in enumerate((src_rows, dst_rows)):
                for c in range(KC):
                    pool.indirect_dma_start(win_i[n][:, c * P:(c + 1) * P], None, rows,
                                            bass.IndirectOffsetOnAxis(ap=row_i[:, c:c + 1], axis=0)).then_inc(windows_in, 16)

            def gathers(t, rows, width):
                with pool.Fori(0, ITERS) as it:
                    for half in range(2):
                        pool.wait_ge(SEM["seg_done"], 2 * it + (t.base["seg_done"] + half - 1))
                        pool.tensor_copy(NOW[:, half, :], IDX[:, ds(2 * U * it + U * half, U)]).then_inc(SEM["idx_ready"], 1)
                        pool.wait_ge(SEM["idx_ready"], 2 * it + (t.base["idx_ready"] + half + 1))
                        pool.sem_inc(idx_seen, 1)
                        for n in range(U):
                            pool.indirect_dma_start(
                                G[:, half, n, 0:width], None, rows,
                                bass.IndirectOffsetOnAxis(ap=NOW[:, half, n:n + 1], axis=0))\
                                .then_inc(t.gathered[half], 16)

            def fetches(t):
                def group(k, half, n):
                    pool.tensor_copy(NOW[:, half, :], IDX[:, ds(k, U)]).then_inc(SEM["idx_ready"], 1)
                    pool.wait_ge(SEM["idx_ready"], n)
                    pool.sem_inc(idx_seen, 1)
                    for n in range(U):
                        pool.indirect_dma_start(
                            G[:, half, n, :], None, gat_table,
                            bass.IndirectOffsetOnAxis(ap=NOW[:, half, n:n + 1], axis=0))\
                            .then_inc(t.gathered[half], 16)
                for half in range(2):
                    group(half * U, half, t.base["idx_ready"] + half + 1)
                with pool.Fori(1, ITERS) as it:
                    for half in range(2):
                        pool.wait_ge(SEM[f"stored{half}"], 16 * it + t.base[f"stored{half}"])
                        pool.wait_ge(SEM["s_copied"], 2 * it + (t.base["s_copied"] + half - 1))
                        group(2 * U * it + U * half, half, 2 * it + (t.base["idx_ready"] + half + 1))

            def sums_of(t):
                gathers(t, table, D)

            zs = [0]

            def stage_blocks(t, z):
                zs[0] += 1
                pool.wait_ge(z_ready, zs[0])
                with pool.Fori(0, NG) as g:
                    pool.wait_ge(SEM["flipped"], g + t.base["flipped"])
                    pool.tensor_copy(zb[:, 0:Q * D].rearrange("p (b d) -> p b d", b=Q),
                                     z[:, ds(Q * g, Q), 0:D]).then_inc(SEM["staged"], 1)

            def stage_strands(t, of):
                zs[0] += 1
                pool.wait_ge(z_ready, zs[0])
                with pool.Fori(0, JG) as g:
                    pool.wait_ge(SEM["flipped"], g + t.base["flipped"])
                    for q in range(Q):
                        ins = pool.tensor_copy(
                            zb[:, q * P:(q + 1) * P].rearrange("p (i h) -> p i h", h=HEADS),
                            of(Q * g + q))
                    ins.then_inc(SEM["staged"], 1)

            stage_strands(Stage("flags"),
                          lambda j: dabs_strands[:, ds(j, 1), :].squeeze(1).unsqueeze(2).broadcast_to([P, LANES, HEADS]))
            pool.wait_ge(table_stored, 16)
            sums_of(Stage("L0"))
            stage_blocks(Stage("L0mlp"), ACC)
            pool.wait_ge(table_stored, 32)
            sums_of(Stage("L1"))
            stage_blocks(Stage("L1mlp"), ACC)
            stage_blocks(Stage("in"), H)
            for l in range(LAYERS):
                stage_blocks(Stage(f"gcn{l}"), H)
                pool.wait_ge(table_stored, 16 * (3 + l))
                sums_of(Stage(f"gcnsum{l}"))
            stage_blocks(Stage("out"), H)
            for l in range(LAYERS):
                stage_blocks(Stage(f"gat{l}"), H)
                pool.wait_ge(table_stored, 16 * (3 + LAYERS + l))
                fetches(Stage(f"fetch{l}"))
                stage_strands(Stage(f"strand{l}"), lambda j: S_strands[:, ds(j, 1), :, :].squeeze(1))
                t = Stage(f"unstrand{l}")
                pool.wait_ge(strands_ready, l + 1)
                with pool.Fori(0, JG) as g:
                    pool.wait_ge(SEM["made"], g + t.base["made"])
                    pool.tensor_copy(zb, LN[:, ds(Q * P * g, Q * P)]).then_inc(SEM["staged"], 1)

        @block.scalar
        def _(act):
            roots = [0]

            def root(to, of):
                roots[0] += 1
                act.wait_ge(var_ready, roots[0])
                nc.scalar.activation(to, of, ACT.Sqrt).then_inc(root_ready, 1)

            def lift(t, of, to):
                with act.Fori(0, NG) as g:
                    act.wait_ge(SEM["flipped"], g + (t.base["flipped"] + 1))
                    nc.scalar.activation(to(g), of, ACT.Copy).then_inc(SEM["lifted"], 1)

            def lift_mlp(t, halves, bias):
                with act.Fori(0, NG) as g:
                    act.wait_ge(SEM["flipped"], g + (t.base["flipped"] + 1))
                    nc.scalar.activation(zT[0:D, :], psA[0:D, :], ACT.Copy).then_inc(SEM["lifted"], 1)
                    for q in range(halves):
                        act.wait_ge(SEM["hid_product"], halves * g + (t.base["hid_product"] + q + 1))
                        nc.scalar.activation(hid[0:D, q, :], (psB, psC)[q][0:D, :], ACT.Relu,
                                             bias=BCOL[:, bias + q:bias + q + 1]).then_inc(SEM["hid_ready"], 1)

            lift(Stage("flags"), psA[:, :], lambda g: LN[:, ds(Q * P * g, Q * P)])
            root(stat[:, 1, :], stat[:, 0, :])
            root(dinv[:, :], dinv[:, :])
            act.wait_ge(const_in, 14 * 16)
            lift_mlp(Stage("L0mlp"), 2, 0)
            root(stat[:, 1, :], stat[:, 0, :])

            t = Stage("L1")

            def lift_attrs(half, at):
                act.wait_ge(SEM["ea_flipped"], at)
                nc.scalar.activation(EA[:, half, U * DE:U * DE + 2 * P], psA[:, 0:2 * P], ACT.Copy)\
                  .then_inc(SEM["ea_lifted"], 1)

            def relu(half, at):
                act.wait_ge(SEM["summed"], at)
                nc.scalar.activation(G[:, half, :, 0:D], G[:, half, :, 0:D], ACT.Relu).then_inc(SEM["rows_ready"], 1)

            lift_attrs(0, t.base["ea_flipped"] + 1)
            with act.Fori(0, ITERS - 1) as it:
                for half in range(2):
                    lift_attrs(1 - half, 2 * it + (t.base["ea_flipped"] + half + 2))
                    relu(half, 4 * it + (t.base["summed"] + 2 * half + 2))
            lift_attrs(1, t.end["ea_flipped"])
            relu(0, t.end["summed"] - 2)
            relu(1, t.end["summed"])

            lift_mlp(Stage("L1mlp"), 1, 2)
            root(HOT[:, 0, 1, 0:D], HOT[:, 0, 1, 0:D])
            for name in ["in"] + [f"gcn{l}" for l in range(LAYERS)] + ["out"]:
                if name == "in":
                    root(stat[:, 1, :], stat[:, 0, :])
                lift(Stage(name), psA[0:D, :], lambda g: zT[0:D, :])
            root(stat[:, 1, :], stat[:, 0, :])
            for l in range(LAYERS):
                lift(Stage(f"gat{l}"), psA[0:D, :], lambda g: zT[0:D, :])
                t = Stage(f"fetch{l}")
                with act.Fori(0, ITERS) as it:
                    for half in range(2):
                        k = 2 * U * it + U * half
                        act.wait_ge(SEM["hot_read"], 2 * it + (t.base["hot_read"] + half + 1))
                        act.wait_ge(SEM["d_product"], 2 * it + (t.base["d_product"] + half))
                        nc.scalar.activation(ST[:, 0:4, :], psA[:, :].rearrange("p (a b) -> p a b", a=4), ACT.Copy)
                        nc.scalar.activation(ST[:, 4:8, :], psB[:, :].rearrange("p (a b) -> p a b", a=4), ACT.Copy)\
                          .then_inc(SEM["st_ready"], 1)
                        act.wait_ge(SEM["d_product"], 2 * it + (t.base["d_product"] + half + 1))
                        nc.scalar.activation(DL[:, ds(k, U), :], psC[:, 0:U * HEADS].rearrange("p (k h) -> p k h", k=U),
                                             ACT.Copy).then_inc(SEM["d_copied"], 1)
                        act.wait_ge(t.gathered[half], 16 * U * it + 16 * U)
                        nc.scalar.activation(S[:, ds(k, U), :], G[:, half, :, D:WT], ACT.Copy).then_inc(SEM["s_copied"], 1)
                lift(Stage(f"strand{l}"), psA[:, :], lambda g: LN[:, ds(Q * P * g, Q * P)])
                act.wait_ge(weights_ready, l + 1)
                nc.scalar.activation(S_flat, S_flat, ACT.Exp).then_inc(exp_done, 1)
                act.wait_ge(exp_done, l + 1)
                t = Stage(f"weigh{l}")
                with act.Fori(0, ITERS) as it:
                    for half in range(2):
                        act.wait_ge(SEM[f"stage_in{half}"], 16 * it + (t.base[f"stage_in{half}"] + 16))
                        nc.scalar.activation(G[:, half, :, D:WT], S[:, ds(2 * U * it + U * half, U), :], ACT.Copy)\
                          .then_inc(SEM["w_copied"], 1)

        @block.tensor
        def _(pe):
            for name, value in START.items():
                if name != "acc_step":
                    pe.sem_inc(SEM[name], value)
            given = [0]

            def give(ins):
                given[0] += 1
                ins.then_inc(setup_product, 1)
            pe.wait_ge(setup_operand, 1)
            nc.tensor.matmul(psA[0:NB, 0:1], cnt[0:EP, 0:NB], ones[0:EP, 0:1], start=True, stop=True)
            give(nc.tensor.matmul(psA[0:NB, 1:2], cnt[0:EP, 1:NB + 1], ones[0:EP, 0:1], start=True, stop=True))
            pe.wait_ge(setup_operand, 2)
            give(nc.tensor.matmul(psA[0:NB, 2:3], upper[:, :], plan[0:NB, 3:4], start=True, stop=True))
            pe.wait_ge(setup_operand, 3)
            give(nc.tensor.matmul(psA[0:NB, 3:4], step_of[:, :], plan[0:NB, 5:6], start=True, stop=True))
            pe.wait_ge(setup_operand, 4)
            quarter = STEPS // 4
            for c in range(4):
                part = ind[0:NB, c * quarter:(c + 1) * quarter]
                nc.tensor.matmul(sums[c // 2][:, c % 2, 0:quarter], edge_dv[:, :], part, start=True, stop=True)
                last = nc.tensor.matmul((psA, psB, psC, psD)[c][:, 0:quarter], ones[0:NB, :], part, start=True, stop=True)
            give(last)
            pe.wait_ge(setup_operand, 5)
            pe.wait_ge(weights_in, (8 + P // DE) * 16)
            for n, w in enumerate(TURNED):
                last = nc.tensor.transpose(psA[0:D, n * D:(n + 1) * D], WTS[:, w, :], ident[0:D, 0:D])
            give(last)
            pe.wait_ge(setup_operand, 6)
            for c in range(KC):
                part = slice(c % 4 * P, (c % 4 + 1) * P)
                nc.tensor.transpose(sums[c // 8][:, c // 4 % 2, part], win_f[0][:, c * P:(c + 1) * P], ident[:, :])
                last = nc.tensor.transpose((psA, psB, psC, psD)[c // 4][:, part], win_f[1][:, c * P:(c + 1) * P], ident[:, :])
            give(last)

            def flip_strands(t):
                with pe.Fori(0, JG) as g:
                    pe.wait_ge(SEM["staged"], g + (t.base["staged"] + 1))
                    pe.wait_ge(SEM["lifted"], g + t.base["lifted"])
                    for q in range(Q):
                        last = nc.tensor.transpose(psA[:, q * P:(q + 1) * P], zb[:, q * P:(q + 1) * P], ident[:, :])
                    last.then_inc(SEM["flipped"], 1)

            def flip_blocks(t, g):
                pe.wait_ge(SEM["staged"], g + (t.base["staged"] + 1))
                pe.wait_ge(SEM["lifted"], g + t.base["lifted"])
                for q in range(Q):
                    last = nc.tensor.transpose(psA[0:D, q * P:(q + 1) * P], zb[:, q * D:(q + 1) * D], ident[:, :])
                last.then_inc(SEM["flipped"], 1)
                pe.wait_ge(SEM["lifted"], g + (t.base["lifted"] + 1))

            def dense_stage(t, w):
                with pe.Fori(0, NG) as g:
                    flip_blocks(t, g)
                    pe.wait_ge(SEM["taken"], g + t.base["taken"])
                    for q in range(Q):
                        last = nc.tensor.matmul(psD[:, q * D:(q + 1) * D], zT[0:D, q * P:(q + 1) * P], WTS[:, w, :],
                                                start=True, stop=True)
                    last.then_inc(SEM["made"], 1)

            def mlp_stage(t, halves, w1, w2):
                with pe.Fori(0, NG) as g:
                    flip_blocks(t, g)
                    pe.wait_ge(SEM["hid_ready"], halves * g + t.base["hid_ready"])
                    for h in range(halves):
                        nc.tensor.matmul((psB, psC)[h][0:D, :], WTS[:, w1 + h, :], zT[0:D, :],
                                         start=True, stop=True).then_inc(SEM["hid_product"], 1)
                    pe.wait_ge(SEM["hid_ready"], halves * g + (t.base["hid_ready"] + halves))
                    pe.wait_ge(SEM["taken"], g + t.base["taken"])
                    for q in range(Q):
                        for h in range(halves):
                            last = nc.tensor.matmul(psD[:, q * D:(q + 1) * D], hid[0:D, h, q * P:(q + 1) * P],
                                                    WTS[:, w2 + h, :], start=(h == 0), stop=(h == halves - 1))
                    last.then_inc(SEM["made"], 1)

            def segment_group(t, it, half, width):
                pe.wait_ge(SEM["acc_step"], 2 * U * it + (t.base["acc_step"] + U * half - U))
                for n in range(U):
                    last = nc.tensor.matmul(sums[half][:, n // 4, n % 4 * width:(n % 4 + 1) * width],
                                            HOT[:, half, n, :], G[:, half, n, 0:width], start=True, stop=True)
                last.then_inc(SEM["seg_done"], 1)

            def sum_stage(t, width, *ready):
                with pe.Fori(0, ITERS) as it:
                    for half in range(2):
                        pe.wait_ge(SEM["hot_built"], 2 * it + (t.base["hot_built"] + half + 1))
                        for name in ready:
                            if name in ("gathered",):
                                pe.wait_ge(t.gathered[half], 16 * U * it + 16 * U)
                            else:
                                pe.wait_ge(SEM[name], 2 * it + (t.base[name] + half + 1))
                        segment_group(t, it, half, width)

            flip_strands(Stage("flags"))
            pe.wait_ge(carry_operand, 1)
            for n in range(3):
                last = nc.tensor.transpose(psC[0:1, n * P:(n + 1) * P], ccol[:, n:n + 1], ident[:, :])
            last.then_inc(carry_product, 1)

            sum_stage(Stage("L0"), D + 1, "rows_ready")
            mlp_stage(Stage("L0mlp"), 2, W_L0A, W_L0C)

            t = Stage("L1")

            def attr_product(half, attr_at, g1, g0):
                pe.wait_ge(SEM[f"attr_in{half}"], attr_at)
                pe.wait_ge(SEM["ea_lifted"], t.base["ea_lifted"] + g0)
                for q in range(2):
                    last = nc.tensor.transpose(psA[:, q * P:(q + 1) * P], EA[:, half, q * P:(q + 1) * P], ident[:, :])
                last.then_inc(SEM["ea_flipped"], 1)
                pe.wait_ge(SEM["ea_lifted"], t.base["ea_lifted"] + g1)
                pe.wait_ge(SEM["summed"], t.base["summed"] + g0 * 2)
                for q in range(2):
                    nc.tensor.matmul((psB, psC)[q][:, 0:4 * D], EA[:, half, U * DE + q * P:U * DE + (q + 1) * P],
                                     WE[:, :, :].rearrange("p a b -> p (a b)"), start=True, stop=True)\
                      .then_inc(SEM["ea_product"], 1)

            def relu_sum(it, half, rows_at, hot_at):
                pe.wait_ge(SEM["hot_built"], hot_at)
                pe.wait_ge(SEM["rows_ready"], rows_at)
                segment_group(t, it, half, D)

            attr_product(0, t.base["attr_in0"] + 16 * U, 1, 0)
            with pe.Fori(0, ITERS - 1) as it:
                attr_product(1, 16 * U * it + (t.base["attr_in1"] + 16 * U), 2 * it + 2, 2 * it + 1)
                relu_sum(it, 0, 2 * it + (t.base["rows_ready"] + 1), 2 * it + (t.base["hot_built"] + 1))
                attr_product(0, 16 * U * it + (t.base["attr_in0"] + 32 * U), 2 * it + 3, 2 * it + 2)
                relu_sum(it, 1, 2 * it + (t.base["rows_ready"] + 2), 2 * it + (t.base["hot_built"] + 2))
            attr_product(1, t.end["attr_in1"], GROUPS, GROUPS - 1)
            relu_sum(ITERS - 1, 0, t.end["rows_ready"] - 1, t.end["hot_built"] - 1)
            relu_sum(ITERS - 1, 1, t.end["rows_ready"], t.end["hot_built"])

            mlp_stage(Stage("L1mlp"), 1, W_L11, W_L12)
            for n in range(2):
                pe.wait_ge(carry_operand, 2 + n)
                nc.tensor.matmul(psB[:, n * D:(n + 1) * D], ones[:, :], HOT[:, 0, n, 0:D],
                                 start=True, stop=True).then_inc(carry_product, 1)
            dense_stage(Stage("in"), W_IN)
            for l in range(LAYERS):
                dense_stage(Stage(f"gcn{l}"), W_GCN + l)
                sum_stage(Stage(f"gcnsum{l}"), D, "gathered")
            dense_stage(Stage("out"), W_OUT)
            for l in range(LAYERS):
                dense_stage(Stage(f"gat{l}"), W_GAT + l)
                t2 = Stage(f"fetch{l}")
                with pe.Fori(0, ITERS) as it:
                    for half in range(2):
                        pe.wait_ge(SEM["hot_built"], 2 * it + (t2.base["hot_built"] + half + 1))
                        pe.wait_ge(SEM["st_ready"], 2 * it + (t2.base["st_ready"] + half))
                        for n in range(U):
                            last = nc.tensor.transpose((psA, psB)[n // 4][:, n % 4 * P:(n % 4 + 1) * P],
                                                       HOT[:, half, n, :], ident[:, :])
                        last.then_inc(SEM["hot_read"], 1)
                        b = blocks(2 * U * it + U * half, U, PE)
                        pe.wait_ge(SEM["st_ready"], 2 * it + (t2.base["st_ready"] + half + 1))
                        pe.wait_ge(SEM["d_copied"], 2 * it + (t2.base["d_copied"] + half))
                        for n in range(U):
                            last = nc.tensor.matmul(psC[:, n * HEADS:(n + 1) * HEADS], ST[:, n, :],
                                                    DD[:, ds(b[n], 1), :].squeeze(1), start=True, stop=True)
                        last.then_inc(SEM["d_product"], 1)
                flip_strands(Stage(f"strand{l}"))
                for n in range(4):
                    pe.wait_ge(carry_operand, 4 + 4 * l + n)
                    if n % 2 == 0:
                        last = nc.tensor.transpose(psC[0:1, 0:P], ccol[:, 3:4], ident[:, :])
                    else:
                        last = nc.tensor.matmul(psD[:, 0:1], crow[0:1, 7, :], ones[0:1, 0:1], start=True, stop=True)
                    last.then_inc(carry_product, 1)
                t2 = Stage(f"unstrand{l}")
                with pe.Fori(0, JG) as g:
                    pe.wait_ge(SEM["staged"], g + (t2.base["staged"] + 1))
                    pe.wait_ge(SEM["taken"], g + t2.base["taken"])
                    for q in range(Q):
                        last = nc.tensor.transpose(psA[:, q * P:(q + 1) * P], zb[:, q * P:(q + 1) * P], ident[:, :])
                    last.then_inc(SEM["made"], 1)
                sum_stage(Stage(f"weigh{l}"), WT, "rows_ready", "w_copied")

        @block.vector
        def _(dve):
            done = [0]
            v = nc.vector

            def link(ins):
                done[0] += 1
                ins.then_inc(chain, 1)
                dve.wait_ge(chain, done[0])

            asked = [0]

            def ask(ins):
                asked[0] += 1
                ins.then_inc(setup_operand, 1)
                dve.wait_ge(setup_product, asked[0])

            v.memset(X[:, FULL:NBP, :], 0.0).then_inc(consts_done, 1)
            link(v.memset(ones[:, :], 1.0))
            v.memset(WE[:, :, :], 0.0).then_inc(consts_done, 1)
            link(v.memset(G[:, :, :, :], 1.0))
            v.memset(ACC[:, :, :], 0.0).then_inc(SEM["acc_step"], START["acc_step"])
            dve.wait_ge(SEM["acc_step"], START["acc_step"])
            link(v.memset(plan[:, :], 0.0))
            dve.wait_ge(iota_done, 3)
            link(v.tensor_scalar(ident[:, :], iota_row[:, :], iota_col[:, 0:1], None, ALU.is_equal))
            link(v.tensor_scalar(upper[:, :], iota_row[0:NB, 0:NB], iota_col[0:NB, 0:1], None, ALU.is_gt))
            link(v.tensor_scalar(plan[0:P, 0:1], iota_col[:, 0:1], 1.0, None, ALU.add))
            link(v.tensor_scalar(step_of[:, :], iota_row[0:NB, 0:NB], plan[0:NB, 0:1], None, ALU.is_equal))
            link(v.tensor_tensor(step_of[:, :], ident[0:NB, 0:NB], step_of[:, :], ALU.subtract))
            link(v.tensor_scalar(valid[:, :], iota_col[:, 0:1], float(REST), None, ALU.is_lt))

            dve.wait_ge(dst_in, 16)
            link(v.tensor_copy(dst_f, dst_i))
            link(v.memset(cnt[:, 0:1], 0.0))
            link(v.memset(cnt[:, NB:NB + 1], float(EF)))
            for b in range(1, NB):
                link(v.tensor_scalar(less, dst_f, float(b * P), None, ALU.is_lt, ALU.add, accum_out=cnt[0:EP, b:b + 1]))
            ask(v.memset(plan[:, 7:8], 0.0))
            link(v.tensor_copy(plan[0:NB, 1:3], psA[0:NB, 0:2]))
            link(v.tensor_copy(tiles_i[0:NB, 0:1], plan[0:NB, 1:2]))
            link(v.tensor_scalar(tiles_i[0:NB, 1:2], plan[0:NB, 2:3], float(P - 1), None, ALU.add))
            link(v.tensor_scalar(tiles_i[0:NB, 0:2], tiles_i[0:NB, 0:2], P.bit_length() - 1, None,
                                 ALU.logical_shift_right))
            link(v.tensor_tensor(plan[0:NB, 3:4], tiles_i[0:NB, 1:2], tiles_i[0:NB, 0:1], ALU.subtract))
            link(v.tensor_tensor(plan[0:NB, 6:7], plan[0:NB, 2:3], plan[0:NB, 1:2], ALU.is_gt))
            ask(v.tensor_tensor(plan[0:NB, 3:4], plan[0:NB, 3:4], plan[0:NB, 6:7], ALU.mult))
            link(v.tensor_copy(plan[0:NB, 4:5], psA[0:NB, 2:3]))
            ask(v.tensor_tensor(plan[0:NB, 5:6], tiles_i[0:NB, 0:1], plan[0:NB, 4:5], ALU.subtract))
            link(v.tensor_copy(plan[0:NB, 6:7], psA[0:NB, 3:4]))
            link(v.tensor_scalar(edge_dv[:, :], ones[0:NB, :], plan[0:NB, 6:7], None, ALU.mult))
            ask(v.tensor_scalar(ind[0:NB, :], iota_k[0:NB, :], plan[0:NB, 4:5], None, ALU.is_ge))
            quarter = STEPS // 4
            for c in range(4):
                part = slice(c * quarter, (c + 1) * quarter)
                link(v.tensor_tensor(first[:, part], iota_k[:, part], sums[c // 2][:, c % 2, 0:quarter], ALU.add))
                link(v.tensor_scalar(block_of[:, part], (psA, psB, psC, psD)[c][:, 0:quarter], -1.0, None, ALU.add))
            by_chunk = [a.rearrange("p (c k) -> p c k", k=P) for a in (ind, keep)]
            link(v.tensor_scalar(ind, first, float(ET - 1), None, ALU.min))
            link(v.tensor_tensor(by_chunk[1], by_chunk[0], ident[:, :].unsqueeze(1).broadcast_to([P, KC, P]), ALU.mult))
            link(v.tensor_reduce(stat[:, 0, 0:KC], by_chunk[1], AX.X, ALU.add))
            v.tensor_copy(row_i[:, :], stat[:, 0, 0:KC]).then_inc(plan_ready, 1)
            link(v.tensor_scalar(first, first, float(P), None, ALU.mult))
            link(v.tensor_scalar(ind, first, float(E - P), None, ALU.min))
            v.tensor_copy(EB[32:33, :], ind[32:33, :])
            v.tensor_copy(EB[64:65, :], block_of[64:65, :]).then_inc(plan_ready, 1)
            link(v.tensor_tensor(keep, first, ind, ALU.subtract))
            link(v.tensor_scalar(keep, keep, iota_col[:, 0:1], None, ALU.is_le))
            ask(v.memset(plan[:, 7:8], 0.0))
            link(v.tensor_copy(WTS[:, W_IN:W_OUT + 1, :], psA[0:D, 0:5 * D].rearrange("p (w d) -> p w d", w=5)))

            roots = [0]

            def root(ins):
                roots[0] += 1
                ins.then_inc(var_ready, 1)
                dve.wait_ge(root_ready, roots[0])

            def over_blocks(vec):
                return vec.broadcast_to([P, NBP, D])

            def over_features(col):
                return col.unsqueeze(2).broadcast_to([P, NBP, D])

            def normalise():
                link(v.tensor_reduce(stat[:, 0, :], X[:, :, :], AX.X, ALU.add))
                link(v.tensor_scalar(stat[:, 0, :], stat[:, 0, :], 1.0 / D, None, ALU.mult))
                link(v.tensor_tensor(H[:, :, :], X[:, :, :], over_features(stat[:, 0, :]), ALU.subtract))
                link(v.tensor_tensor(ACCF, H[:, :, :], H[:, :, :], ALU.mult))
                link(v.tensor_reduce(stat[:, 0, :], ACCF, AX.X, ALU.add))
                root(v.tensor_scalar(stat[:, 0, :], stat[:, 0, :], 1.0 / D, LN_EPS, ALU.mult, ALU.add))
                link(v.reciprocal(stat[:, 0, :], stat[:, 1, :]))
                link(v.scalar_tensor_tensor(H[:, :, :], H[:, :, :], 0.0, over_features(stat[:, 0, :]), ALU.max, ALU.mult))

            dve.wait_ge(windows_in, 2 * KC * 16)
            link(v.tensor_copy(win_f[0], win_i[0]))
            ask(v.tensor_copy(win_f[1], win_i[1]))
            for c in range(0, STEPS, 512):
                n = min(512, STEPS - c)
                part = slice(c, c + n)
                link(v.tensor_copy(IDX[:, part], sums[c // 1024][:, c // 512 % 2, 0:n]))
                got = (psA, psB, psC, psD)[c // 512][:, 0:n]
                link(v.scalar_tensor_tensor(dabs[:, part], got, 1.0, keep[:, part], ALU.add, ALU.mult))
                link(v.tensor_scalar(dabs[:, part], dabs[:, part], -1.0, None, ALU.add))
                link(v.scalar_tensor_tensor(first[:, part], block_of[:, part], -float(P), got, ALU.mult, ALU.add))
                link(v.scalar_tensor_tensor(first[:, part], first[:, part], 1.0, keep[:, part], ALU.add, ALU.mult))
                link(v.tensor_scalar(REL[:, part], first[:, part], -1.0, None, ALU.add))
            v.memset(plan[:, 7:8], 0.0).then_inc(z_ready, 1)
            dve.wait_ge(SEM["lifted"], Stage("flags").end["lifted"])
            T = LT * P
            link(v.memset(CUT[:, :], 0.0))
            link(v.tensor_tensor(CUT[:, 1:T], LN[:, 1:T], LN[:, 0:T - 1], ALU.not_equal))
            link(v.tensor_scalar(CUT[:, 1:T], CUT[:, 1:T], -BIG, None, ALU.mult))
            link(v.tensor_copy(ccol[:, 0:1], LN[:, 0:1]))
            link(v.tensor_copy(ccol[:, 1:2], LN[:, T - 1:T]))
            link(v.tensor_reduce(ccol[:, 2:3], CUT[:, 1:T], AX.X, ALU.min))
            v.tensor_scalar(ccol[:, 2:3], ccol[:, 2:3], 0.0, None, ALU.is_equal).then_inc(carry_operand, 1)
            dve.wait_ge(carry_product, 1)
            HS = HEADS
            link(v.memset(crow[:, :, :], 0.0))
            link(v.tensor_copy(crow[:, 3:6, :], psC[0:1, 0:3 * P].rearrange("p (a b) -> p a b", a=3)))
            link(v.tensor_tensor(crow[:, 6, HS:P], crow[:, 3, HS:P], crow[:, 4, 0:P - HS], ALU.is_equal))
            link(v.tensor_tensor(crow[:, 1, HS:P], crow[:, 6, HS:P], crow[:, 5, 0:P - HS], ALU.mult))
            link(v.tensor_tensor(crow[:, 2, HS:P], crow[:, 6, HS:P], crow[:, 5, HS:P], ALU.mult))
            link(v.tensor_copy(crow[:, 0, :], crow[:, 6, :]))
            link(v.tensor_scalar(crow[:, 0:3, :], crow[:, 0:3, :], -1.0, BIG, ALU.add, ALU.mult))

            dve.wait_ge(x_in, 32)
            dve.wait_ge(const_in, 14 * 16)
            normalise()
            link(v.memset(ACC[:, :, :], 0.0))
            v.memset(plan[:, 7:8], 0.0).then_inc(table_ready, 1)

            def build_hot(half, k):
                v.tensor_tensor(HOT[:, half, :, :], iota_row[:, :].unsqueeze(1).broadcast_to([P, U, P]),
                                REL[:, ds(k, U)].unsqueeze(2).broadcast_to([P, U, P]), ALU.is_equal)\
                 .then_inc(SEM["hot_built"], 1)

            def add_up(t, half, it, width, more=0):
                b = blocks(2 * U * it + U * half, U, DVE)
                dve.wait_ge(SEM["seg_done"], 2 * it + (t.base["seg_done"] + half + 1))
                for n in range(U):
                    to = ACC[:, ds(b[n], 1), 0:width].squeeze(1)
                    v.tensor_tensor(to, to, sums[half][:, n // 4, n % 4 * width:(n % 4 + 1) * width], ALU.add)\
                     .then_inc(SEM["acc_step"], 1)
                    dve.wait_ge(SEM["acc_step"], 2 * U * it + (t.base["acc_step"] + U * half + n + 1))

            def sum_stage(t, width, prepare):
                def ready(it, half):
                    dve.wait_ge(SEM["seg_done"], 2 * it + (t.base["seg_done"] + half - 1))
                    build_hot(half, 2 * U * it + U * half)
                    if prepare:
                        prepare(it, half)
                ready(0, 0)
                with dve.Fori(0, ITERS - 1) as it:
                    ready(it, 1)
                    add_up(t, 0, it, width)
                    ready(it + 1, 0)
                    add_up(t, 1, it, width)
                ready(ITERS - 1, 1)
                add_up(t, 0, ITERS - 1, width)
                add_up(t, 1, ITERS - 1, width)

            def take(t, use):
                with dve.Fori(0, NG) as g:
                    dve.wait_ge(SEM["made"], g + (t.base["made"] + 1))
                    use(g, psD[:, 0:Q * D].rearrange("p (b d) -> p b d", b=Q)).then_inc(SEM["taken"], 1)
                dve.wait_ge(SEM["taken"], t.end["taken"])

            def z_is_ready():
                v.memset(plan[:, 7:8], 0.0).then_inc(z_ready, 1)

            t0 = Stage("L0")

            def add_attr(it, half):
                dve.wait_ge(t0.gathered[half], 16 * U * it + 16 * U)
                dve.wait_ge(SEM[f"attr_in{half}"], 16 * U * it + (t0.base[f"attr_in{half}"] + 16 * U))
                v.tensor_tensor(G[:, half, :, 0:D], G[:, half, :, 0:D],
                                EA[:, half, :].rearrange("p (k d) -> p k d", k=U), ALU.add)\
                 .then_inc(SEM["rows_ready"], 1)
            sum_stage(t0, D + 1, add_attr)
            root(v.tensor_scalar(dinv[:, :], ACC[:, :, D], 1.0, None, ALU.add))
            link(v.reciprocal(dinv[:, :], dinv[:, :]))
            z_is_ready()
            link(v.tensor_scalar(epsp[:, :], epsp[:, :], 1.0, None, ALU.add))
            link(v.scalar_tensor_tensor(X[:, :, :], H[:, :, :], epsp[:, 0:1], X[:, :, :], ALU.mult, ALU.add))
            link(v.tensor_tensor(X[:, :, :], X[:, :, :], over_blocks(row(R_L0B2)), ALU.add))
            take(Stage("L0mlp"), lambda g, p: v.tensor_tensor(X[:, ds(Q * g, Q), :], p, X[:, ds(Q * g, Q), :], ALU.add))
            normalise()

            link(v.tensor_tensor(ACCF, H[:, :, :], over_blocks(row(R_BE)), ALU.add))
            v.memset(plan[:, 7:8], 0.0).then_inc(table_ready, 1)
            dve.wait_ge(table_stored, 32)
            link(v.tensor_copy(ACCF, H[:, :, :]))
            t1 = Stage("L1")

            def add_product(it, half):
                dve.wait_ge(t1.gathered[half], 16 * U * it + 16 * U)
                for q in range(2):
                    dve.wait_ge(SEM["ea_product"], 4 * it + (t1.base["ea_product"] + 2 * half + q + 1))
                    v.tensor_tensor(G[:, half, 4 * q:4 * q + 4, 0:D], G[:, half, 4 * q:4 * q + 4, 0:D],
                                    (psB, psC)[q][:, 0:4 * D].rearrange("p (k d) -> p k d", k=4), ALU.add)\
                     .then_inc(SEM["summed"], 1)
            sum_stage(t1, D, add_product)
            z_is_ready()
            take(Stage("L1mlp"), lambda g, p: v.tensor_tensor(
                H[:, ds(Q * g, Q), :], p, row(R_L1B2).broadcast_to([P, Q, D]), ALU.add))
            hot0, hot1 = HOT[:, 0, 0, 0:D], HOT[:, 0, 1, 0:D]
            by_feature = H[:, 0:NB, :].rearrange("p b d -> p d b")
            link(v.tensor_scalar(H[:, NB - 1, :], H[:, NB - 1, :], valid[:, 0:1], None, ALU.mult))
            v.tensor_reduce(hot0, by_feature, AX.X, ALU.add).then_inc(carry_operand, 1)
            dve.wait_ge(carry_product, 2)
            link(v.tensor_scalar(hot0, psB[:, 0:D], 1.0 / N, None, ALU.mult))
            link(v.tensor_tensor(H[:, :, :], H[:, :, :], over_blocks(HOT[:, 0, 0:1, 0:D]), ALU.subtract))
            link(v.tensor_scalar(H[:, NB - 1, :], H[:, NB - 1, :], valid[:, 0:1], None, ALU.mult))
            link(v.tensor_tensor(ACCF, H[:, :, :], H[:, :, :], ALU.mult))
            v.tensor_reduce(hot1, ACC[:, 0:NB, 0:D].rearrange("p b d -> p d b"), AX.X, ALU.add).then_inc(carry_operand, 1)
            dve.wait_ge(carry_product, 3)
            hot2 = HOT[:, 0, 2, 0:D]
            link(v.tensor_scalar(hot2, psB[:, D:2 * D], 1.0 / N, BN_EPS, ALU.mult, ALU.add))
            root(v.tensor_copy(hot1, hot2))
            link(v.reciprocal(hot0, hot1))
            link(v.tensor_tensor(hot0, hot0, ROWS[:, R_GAMMA, :], ALU.mult))
            link(v.tensor_tensor(H[:, :, :], H[:, :, :], over_blocks(HOT[:, 0, 0:1, 0:D]), ALU.mult))
            link(v.tensor_tensor(H[:, :, :], H[:, :, :], over_blocks(row(R_BETA)), ALU.add))
            link(v.scalar_tensor_tensor(X[:, :, :], H[:, :, :], 0.0, X[:, :, :], ALU.max, ALU.add))
            normalise()

            z_is_ready()
            take(Stage("in"), lambda g, p: v.tensor_tensor(
                H[:, ds(Q * g, Q), :], p, row(R_BIN).broadcast_to([P, Q, D]), ALU.add))
            link(v.tensor_scalar(H[:, :, :], H[:, :, :], 0.0, None, ALU.max))
            for l in range(LAYERS):
                z_is_ready()
                take(Stage(f"gcn{l}"), lambda g, p: v.tensor_tensor(
                    ACC[:, ds(Q * g, Q), 0:D], p, dinv[:, ds(Q * g, Q)].unsqueeze(2).broadcast_to([P, Q, D]), ALU.mult))
                v.memset(plan[:, 7:8], 0.0).then_inc(table_ready, 1)
                dve.wait_ge(table_stored, 16 * (3 + l))
                sum_stage(Stage(f"gcnsum{l}"), D, None)
                link(v.tensor_tensor(ACCF, ACCF, over_features(dinv[:, :]), ALU.mult))
                link(v.tensor_tensor(ACCF, ACCF, over_blocks(row(R_GCNB + l)), ALU.add))
                link(v.scalar_tensor_tensor(H[:, :, :], ACCF, 0.0, H[:, :, :], ALU.max, ALU.add))
            z_is_ready()
            link(v.tensor_tensor(X[:, :, :], X[:, :, :], over_blocks(row(R_BOUT)), ALU.add))
            take(Stage("out"), lambda g, p: v.tensor_tensor(X[:, ds(Q * g, Q), :], p, X[:, ds(Q * g, Q), :], ALU.add))
            normalise()

            for l in range(LAYERS):
                z_is_ready()
                take(Stage(f"gat{l}"), lambda g, p: v.tensor_copy(ACC[:, ds(Q * g, Q), 0:D], p))
                for r, to in ((R_ASRC, ACC[:, :, D:WT]), (R_ADST, DD[:, :, :])):
                    link(v.tensor_tensor(H[:, :, :], ACCF, over_blocks(row(r + l)), ALU.mult))
                    link(v.tensor_reduce(to, H[:, :, :].rearrange("p b (h c) -> p b h c", h=HEADS), AX.X, ALU.add))
                v.memset(plan[:, 7:8], 0.0).then_inc(table_ready, 1)

                t = Stage(f"fetch{l}")
                build_hot(0, 0)
                build_hot(1, U)
                with dve.Fori(1, ITERS) as it:
                    for half in range(2):
                        dve.wait_ge(SEM["hot_read"], 2 * it + (t.base["hot_read"] + half - 1))
                        build_hot(half, 2 * U * it + U * half)
                dve.wait_ge(SEM["s_copied"], t.end["s_copied"])
                z_is_ready()

                dve.wait_ge(SEM["lifted"], Stage(f"strand{l}").end["lifted"])
                link(v.tensor_tensor(S_flat, S_flat, D_flat, ALU.add))
                link(v.scalar_tensor_tensor(S_flat, S_flat, SLOPE, S_flat, ALU.mult, ALU.max))
                half_t = T // 2
                carried = [3 + 4 * l]

                def swap(ins):
                    carried[0] += 1
                    ins.then_inc(carry_operand, 1)
                    dve.wait_ge(carry_product, carried[0])

                link(v.tensor_tensor_scan(scratch, CUT[:, 0:half_t], LN[:, 0:half_t], -BIG, ALU.add, ALU.max))
                link(v.tensor_copy(ccol[:, 0:1], scratch[:, half_t - 1:half_t]))
                link(v.tensor_tensor_scan(scratch, CUT[:, half_t:T], LN[:, half_t:T], ccol[:, 0:1], ALU.add, ALU.max))
                swap(v.tensor_copy(ccol[:, 3:4], scratch[:, half_t - 1:half_t]))
                link(v.memset(crow[:, 6:8, :], -BIG))
                link(v.tensor_tensor(crow[:, 6, HS:P], psC[0:1, 0:P - HS], crow[:, 0, HS:P], ALU.add))
                for h in range(HS):
                    last = v.tensor_tensor_scan(crow[:, 7, h:P:HS], crow[:, 1, h:P:HS], crow[:, 6, h:P:HS], -BIG,
                                                ALU.add, ALU.max)
                    if h < HS - 1:
                        link(last)
                swap(last)
                link(v.tensor_copy(ccol[:, 1:2], psD[:, 0:1]))
                link(v.tensor_tensor_scan(LN[:, :], CUT[:, 0:T], LN[:, :], ccol[:, 1:2], ALU.add, ALU.max))
                link(v.tensor_tensor_scan(scratch[:, ::-1], CUT[:, T:half_t:-1], LN[:, T - 1:half_t - 1:-1], -BIG,
                                          ALU.add, ALU.max))
                link(v.tensor_copy(ccol[:, 0:1], scratch[:, 0:1]))
                link(v.tensor_tensor_scan(scratch[:, ::-1], CUT[:, half_t:0:-1], LN[:, 0:half_t][:, ::-1], ccol[:, 0:1],
                                          ALU.add, ALU.max))
                swap(v.tensor_copy(ccol[:, 3:4], scratch[:, 0:1]))
                link(v.memset(crow[:, 6:8, :], -BIG))
                link(v.memset(crow[:, 3, :], -BIG))
                link(v.tensor_tensor(crow[:, 6, 0:P - HS], psC[0:1, HS:P], crow[:, 0, HS:P], ALU.add))
                link(v.tensor_copy(crow[:, 3, 0:P - HS], crow[:, 2, HS:P]))
                for h in range(HS):
                    back = slice(P - HS + h, None, -HS)
                    last = v.tensor_tensor_scan(crow[:, 7, back], crow[:, 3, back], crow[:, 6, back], -BIG,
                                                ALU.add, ALU.max)
                    if h < HS - 1:
                        link(last)
                swap(last)
                link(v.tensor_copy(ccol[:, 1:2], psD[:, 0:1]))
                v.tensor_tensor_scan(LN[:, ::-1], CUT[:, T:0:-1], LN[:, ::-1], ccol[:, 1:2], ALU.add, ALU.max)\
                 .then_inc(strands_ready, 1)
                dve.wait_ge(strands_ready, l + 1)

                t = Stage(f"unstrand{l}")
                with dve.Fori(0, JG) as g:
                    dve.wait_ge(SEM["made"], g + (t.base["made"] + 1))
                    dve.wait_ge(SEM["logit_done"], g + t.base["logit_done"])
                    view = tmp.rearrange("p (j i h) -> p j i h", j=Q, h=HEADS)
                    v.tensor_tensor(view, psA[:, :].rearrange("p (j i h) -> p j i h", j=Q, h=HEADS),
                                    D_strands[:, ds(Q * g, Q), :, :], ALU.add).then_inc(SEM["taken"], 1)
                    dve.wait_ge(SEM["taken"], g + (t.base["taken"] + 1))
                    v.scalar_tensor_tensor(tmp, tmp, SLOPE, tmp, ALU.mult, ALU.max).then_inc(SEM["leaky_done"], 1)
                    dve.wait_ge(SEM["leaky_done"], g + (t.base["leaky_done"] + 1))
                    part = S_strands[:, ds(Q * g, Q), :, :]
                    v.tensor_tensor(part, part, view, ALU.subtract).then_inc(SEM["logit_done"], 1)
                dve.wait_ge(SEM["logit_done"], t.end["logit_done"])
                v.memset(ACC[:, :, :], 0.0).then_inc(weights_ready, 1)
                dve.wait_ge(weights_ready, l + 1)
                dve.wait_ge(exp_done, l + 1)

                t = Stage(f"weigh{l}")

                def weigh(it, half):
                    dve.wait_ge(SEM[f"stage_in{half}"], 16 * it + (t.base[f"stage_in{half}"] + 16))
                    rows = G[:, half, :, 0:D].rearrange("p k (h c) -> p k h c", h=HEADS)
                    v.tensor_tensor(rows, rows, S[:, ds(2 * U * it + U * half, U), :].unsqueeze(3)
                                    .broadcast_to([P, U, HEADS, C]), ALU.mult).then_inc(SEM["rows_ready"], 1)
                sum_stage(t, WT, weigh)
                link(v.tensor_scalar(ACC[:, :, D:WT], ACC[:, :, D:WT], 1e-16, None, ALU.add))
                link(v.reciprocal(ACC[:, :, D:WT], ACC[:, :, D:WT]))
                for h in range(HEADS):
                    part = ACC[:, :, h * C:(h + 1) * C]
                    link(v.tensor_tensor(part, part, ACC[:, :, D + h:D + h + 1].broadcast_to([P, NBP, C]), ALU.mult))
                link(v.tensor_tensor(ACCF, ACCF, over_blocks(row(R_GATB + l)), ALU.add))
                if l < LAYERS - 1:
                    link(v.tensor_scalar(H[:, :, :], ACCF, 0.0, None, ALU.max))
            v.scalar_tensor_tensor(X[:, :, :], ACCF, 0.0, X[:, :, :], ALU.max, ALU.add).then_inc(result_ready, 1)


_INS = ["x", "src", "dst", "edge_attr_32", "edge_attr_96", "L0_gnn_W1", "L0_gnn_b1", "L0_gnn_W2", "L0_gnn_b2",
        "L0_gnn_eps", "L1_gnn_We", "L1_gnn_be", "L1_gnn_W1", "L1_gnn_b1", "L1_gnn_W2", "L1_gnn_b2", "L1_gnn_gamma",
        "L1_gnn_beta", "L2_gnn_W_in", "L2_gnn_b_in", "L2_gnn_gcn_W", "L2_gnn_gcn_b", "L2_gnn_W_out", "L2_gnn_b_out",
        "L3_gnn_W", "L3_gnn_att_src", "L3_gnn_att_dst", "L3_gnn_bias"]


def kernel(**inputs):
    import numpy as _np
    import concourse.bacc as _bacc
    from concourse import mybir as _mybir
    from concourse.bass_utils import run_bass_kernel_spmd as _run

    nc = _bacc.Bacc("TRN2", target_bir_lowering=False, num_devices=1)
    arrays, args = {}, []
    for name in _INS:
        a = _np.ascontiguousarray(inputs[name])
        arrays[f"in_{name}_dram"] = a
        args.append(nc.dram_tensor(f"in_{name}_dram", a.shape, _mybir.dt.from_np(a.dtype), kind="ExternalInput").ap())
    shape = arrays["in_x_dram"].shape
    result = nc.dram_tensor("out_0_dram", shape, _mybir.dt.float32, kind="ExternalOutput").ap()
    gnn_kernel(nc, *args, result)
    r = _run(nc, [arrays], core_ids=[0])
    return r.results[0]["out_0_dram"]
```

```python
import concourse.bass as bass
from concourse import mybir
from contextlib import ExitStack


def gnn_kernel(nc, x, src, dst, edge_attr_32, edge_attr_96, L0_W1, L0_b1, L0_W2, L0_b2, L0_eps,
               L1_We, L1_be, L1_W1, L1_b1, L1_W2, L1_b2, L1_gamma, L1_beta,
               L2_W_in, L2_b_in, L2_gcn_W, L2_gcn_b, L2_W_out, L2_b_out,
               L3_W, L3_att_src, L3_att_dst, L3_bias, out):
    f32, i32, bf16 = mybir.dt.float32, mybir.dt.int32, mybir.dt.bfloat16
    ALU, ACT, AX = mybir.AluOpType, mybir.ActivationFunctionType, mybir.AxisListType
    DVE, PE, SP, ACTE = (mybir.EngineType.DVE, mybir.EngineType.PE, mybir.EngineType.SP,
                         mybir.EngineType.Activation)
    ds = bass.ds

    P = 128
    N, D = x.shape
    E = src.shape[0]
    DE = edge_attr_32.shape[1]
    LAYERS, HEADS, C = L3_att_src.shape
    WT = D + HEADS
    NB = -(-N // P)
    Q = 4
    NG = -(-NB // Q)
    NBP = NG * Q
    FULL = N // P
    REST = N - FULL * P
    U = 8
    BT = P // HEADS
    STEPS = -(-(-(-E // P) + NB) // P) * P
    GROUPS = STEPS // U
    ITERS = GROUPS // 2
    UN = 4
    ROUNDS = GROUPS // UN
    BATCHES = STEPS // BT
    BG = BT // U
    JG = BATCHES // Q
    BIG = 1.0e30
    LN_EPS = BN_EPS = 1e-5
    SLOPE = 0.2
    PARTS = 3
    EP = max(d for d in range(1, P + 1) if E % d == 0)
    EF = E // EP
    ET = -(-E // P)
    REM = E - (ET - 1) * P
    KC = -(-STEPS // P)
    assert BATCHES % 2 == 0 and UN == BG == 4 and NG == JG and STEPS <= 4 * 512 and 0 < REM < P

    ctx = ExitStack()
    with ctx:
        def sb(name, shape, dt=f32):
            return ctx.enter_context(nc.sbuf_tensor("sb_" + name, shape, dt))

        def sem(name):
            return ctx.enter_context(nc.semaphore(name))

        def dram(name, shape, dt):
            return nc.dram_tensor(name, shape, dt, kind="Internal").ap()

        table = dram("feature_table", [NBP * P, D], f32)
        gat_table = dram("attention_table", [NBP * P, WT], f32)
        src_rows = dram("src_rows", [ET, P], i32)
        dst_rows = dram("dst_rows", [ET, P], i32)

        X = sb("X", [P, NBP, D])
        H = sb("H", [P, NBP, D])
        ACC = sb("ACC", [P, NBP, WT])
        CUT = sb("CUT", [P, BATCHES, P + 1], bf16)
        FORE = sb("FORE", [P, BATCHES, P + HEADS], bf16)
        AFT = sb("AFT", [P, BATCHES, P], bf16)
        JOIN = sb("JOIN", [1, BATCHES])
        IDX = sb("IDX", [P, STEPS], i32)
        REL = sb("REL", [P, STEPS], bf16)
        OUT = sb("OUT", [P, STEPS], bf16)
        EB = sb("EB", [65, STEPS], i32)
        HOT = sb("HOT", [P, 8, U, P])
        G = sb("G", [P, 8, U, WT])
        EA = sb("EA", [P, 2, U * D])
        NOW = sb("NOW", [P, 2, BT], i32)
        SB = sb("SB", [P, P])
        LW = sb("LW", [P, 4, P + HEADS])
        WB = sb("WB", [P, BT, HEADS])
        scales = sb("scales", [P, HEADS])
        cut_now = sb("cut_now", [P, P + 1], bf16)
        lone = sb("lone", [P, 8])
        iota_row = sb("iota_row", [P, P])
        iota_col = sb("iota_col", [P, 1])
        ident = sb("ident", [P, P])
        ones = sb("ones", [P, P])
        WTS = sb("WTS", [D, 14, D])
        WE = sb("WE", [P, P // DE, D])
        ROWS = sb("ROWS", [P, 7 + 4 * LAYERS, D])
        BCOL = sb("BCOL", [D, 3])
        DD = sb("DD", [P, NBP, HEADS])
        DDP = sb("DDP", [P, NBP, PARTS, HEADS], bf16)
        dinv = sb("dinv", [P, NBP])
        stat = sb("stat", [P, 2, NBP])
        epsp = sb("epsp", [P, 1])
        valid = sb("valid", [P, 1])
        plan = sb("plan", [P, 8])
        tiles_i = sb("tiles_i", [P, 3], i32)
        row_i = sb("row_i", [P, KC], i32)
        H_flat = H[:, :, :].rearrange("p b d -> p (b d)")
        ACC_flat = ACC[:, :, :].rearrange("p b d -> p (b d)")
        G_flat = G[:, :, :, :].rearrange("p s k d -> p (s k d)")
        HOT_flat = HOT[:, :, :, :].rearrange("p s k n -> p (s k n)")
        EA_flat = EA[:, :, :].rearrange("p a b -> p (a b)")
        ST = EA_flat[:, 0:U * P // 2].bitcast(bf16).rearrange("p (k e) -> p k e", k=U)
        DL = EA_flat[:, U * P // 2:U * P // 2 + 2 * PARTS * P].rearrange("p (b a) -> p b a", b=2)
        spare = 2 * STEPS
        zb = G_flat[:, spare:spare + 512]
        zT = G_flat[:, spare + 512:spare + 1024]
        hid = G_flat[:, spare + 1024:spare + 2048].rearrange("p (q a) -> p q a", q=2)
        assert spare + 2048 <= 8 * U * WT and BATCHES * P <= 8 * U * P
        win_i = [H_flat[:, n * STEPS:(n + 1) * STEPS].bitcast(i32) for n in range(2)]
        win_f = [H_flat[:, 2 * STEPS:3 * STEPS], G_flat[:, 0:STEPS]]
        ind = dabs = ACC_flat[:, 0:STEPS]
        first = ACC_flat[:, STEPS:2 * STEPS]
        keep = ACC_flat[:, 2 * STEPS:3 * STEPS]
        block_of = G_flat[:, STEPS:2 * STEPS]
        begins, ends, chained = (H_flat[:, n * STEPS:(n + 1) * STEPS] for n in range(3))
        lanes = HOT_flat[:, 0:BATCHES * P]
        iota_k = HOT_flat[:, 3 * STEPS:4 * STEPS]
        dst_i = HOT_flat[0:EP, 0:EF].bitcast(i32)
        dst_f = HOT_flat[0:EP, EF:2 * EF]
        upper = HOT_flat[0:NB, 2 * EF:2 * EF + P][:, 0:NB]
        step_of = HOT_flat[0:NB, 2 * EF + P:2 * EF + 2 * P][:, 0:NB]
        edge_dv = HOT_flat[0:NB, 2 * EF + 2 * P:2 * EF + 3 * P]
        cnt = HOT_flat[:, 2 * EF + 3 * P:2 * EF + 3 * P + NB + 1]
        assert 2 * EF + 4 * P <= 3 * STEPS and NB < P
        less = ACC_flat[0:EP, 0:EF]
        ACCF = ACC[:, :, 0:D]
        SB3 = SB[:, :].rearrange("p (t h) -> p t h", h=HEADS)

        heads = EA_flat[:, 0:2 * P].bitcast(i32)
        edge_of = EA_flat[:, 2 * P:3 * P]

        sums = [ctx.enter_context(nc.psum_tensor(f"sums{j}", [P, 2, 512], f32)) for j in range(2)]
        psA, psB, psC, psD = (ctx.enter_context(nc.psum_tensor(f"ps{c}", [P, 512], f32)) for c in "ABCD")

        def row(n):
            return ROWS[:, n:n + 1, :]
        R_L0B2, R_BE, R_L1B2, R_GAMMA, R_BETA, R_BIN, R_BOUT = range(7)
        R_GCNB, R_GATB, R_ASRC, R_ADST = 7, 7 + LAYERS, 7 + 2 * LAYERS, 7 + 3 * LAYERS
        W_L0A, W_L0B, W_L0C, W_L0D, W_L11, W_L12, W_IN, W_GCN, W_OUT = 0, 1, 2, 3, 4, 5, 6, 7, 10
        W_GAT = 11
        TURNED = [W_IN, W_GCN, W_GCN + 1, W_GCN + 2, W_OUT]

        x_in, dst_in, const_in, weights_in = sem("x_in"), sem("dst_in"), sem("const_in"), sem("weights_in")
        iota_done, consts_done = sem("iota_done"), sem("consts_done")
        setup_operand, setup_product = sem("setup_operand"), sem("setup_product")
        plan_ready = sem("plan_ready")
        rows_in, windows_in = sem("rows_in"), sem("windows_in")
        chain = sem("chain")
        var_ready, root_ready = sem("var_ready"), sem("root_ready")
        table_ready, table_stored = sem("table_ready"), sem("table_stored")
        z_ready = sem("z_ready")
        feature_sums, feature_totals = sem("feature_sums"), sem("feature_totals")
        heads_in = sem("heads_in")
        idx_seen = sem("idx_seen")
        result_ready, out_done = sem("result_ready"), sem("out_done")

        NAMES = ["idx_ready", "attr_in0", "attr_in1", "hot_built", "rows_ready",
                 "seg_done", "acc_step", "ea_flipped", "ea_lifted", "ea_product", "summed",
                 "hot_read", "st_ready", "d_product", "d_copied",
                 "lane_step", "lane_ask", "lane_reply", "exponent", "exp_made",
                 "staged", "flipped", "lifted", "hid_product", "hid_ready", "made", "taken"]
        SEM = {n: sem(n) for n in NAMES}
        START = {"seg_done": 8, "acc_step": 2 * U} | {n: 1 for n in (
            "flipped", "lifted", "taken", "hid_ready", "ea_lifted", "summed", "st_ready", "d_product",
            "d_copied")}
        LANE_STEPS, LANE_ASKS = 22, 5
        HEAD_STEPS, HEAD_ASKS = 11, 4
        gather = {"idx_ready": GROUPS // 2}
        segment = {"hot_built": GROUPS, "seg_done": GROUPS, "acc_step": STEPS}
        attrs = {"attr_in0": ITERS * U * 16, "attr_in1": ITERS * U * 16, "rows_ready": GROUPS}
        dense = {n: NG for n in ("staged", "flipped", "lifted", "made", "taken")}
        MOVES = {
            "sum_attr": gather | segment | attrs,
            "sum_relu": gather | segment | attrs | {"ea_flipped": GROUPS, "ea_lifted": GROUPS,
                                                    "ea_product": 2 * GROUPS, "summed": 2 * GROUPS},
            "sum": gather | segment,
            "attend": segment | {"idx_ready": BATCHES, "rows_ready": GROUPS, "lane_step": LANE_STEPS * BATCHES,
                                 "lane_ask": LANE_ASKS * BATCHES, "lane_reply": LANE_ASKS * BATCHES,
                                 "exponent": 2 * BATCHES, "exp_made": 2 * BATCHES}
                      | {n: GROUPS for n in ("hot_read", "st_ready", "d_product", "d_copied")},
            "dense": dense,
            "mlp1": dense | {"hid_product": NG, "hid_ready": NG},
            "mlp2": dense | {"hid_product": 2 * NG, "hid_ready": 2 * NG},
            "lanes": {n: JG for n in ("staged", "flipped", "lifted")},
        }
        PLAN = [("flags", "lanes"), ("L0", "sum_attr"), ("L0mlp", "mlp2"), ("L1", "sum_relu"),
                ("L1mlp", "mlp1"), ("in", "dense")]
        for l in range(LAYERS):
            PLAN += [(f"gcn{l}", "dense"), (f"gcnsum{l}", "sum")]
        PLAN += [("out", "dense")]
        for l in range(LAYERS):
            PLAN += [(f"gat{l}", "dense"), (f"attend{l}", "attend")]

        GATHERED = {name: [sem(f"gathered{slot}_{name}") for slot in range(UN if kind != "attend" else 8)]
                    for name, kind in PLAN if "idx_ready" in MOVES[kind]}

        class Stage:
            def __init__(self, name):
                n = [a for a, _ in PLAN].index(name)
                self.base = {s: START.get(s, 0) + sum(MOVES[k].get(s, 0) for _, k in PLAN[:n]) for s in NAMES}
                self.gathered = GATHERED.get(name)
                self.end = {s: self.base[s] + MOVES[PLAN[n][1]].get(s, 0) for s in NAMES}

        def freed(t, slots):
            return t.base["seg_done"] - slots

        def firsts(k, n, engine):
            return nc.values_load_multi_w_load_instructions(
                EB[32:33, ds(k, n)], engines=(engine,), min_val=0, max_val=E - P,
                skip_runtime_bounds_check_because="the plan clips them")[1]

        def blocks(k, n, engine):
            return nc.values_load_multi_w_load_instructions(
                EB[64:65, ds(k, n)], engines=(engine,), min_val=0, max_val=NB - 1,
                skip_runtime_bounds_check_because="the plan clips them")[1]

        block = ctx.enter_context(nc.Block())

        @block.sync
        def _(sp):
            for to, of in ((src_rows, src), (dst_rows, dst)):
                sp.dma_start(to[0:ET - 1, :], of[0:(ET - 1) * P].rearrange("(r e) -> r e", e=P)).then_inc(rows_in, 16)
            sp.dma_start(src_rows[ET - 1:ET, :], src[E - P:E].unsqueeze(0)).then_inc(rows_in, 16)
            sp.dma_start(dst_rows[ET - 1:ET, P - REM:P], dst[E - REM:E].unsqueeze(0)).then_inc(rows_in, 16)
            with nc.allow_non_contiguous_dma(reason="one number, repeated"):
                sp.dma_start(dst_rows[ET - 1, 0:P - REM].unsqueeze(1),
                             dst[E - REM:E - REM + 1].partition_broadcast(P - REM)).then_inc(rows_in, 16)
            sp.dma_start(dst_i, dst.rearrange("(p f) -> p f", p=EP)).then_inc(dst_in, 16)
            sp.dma_start(X[:, 0:FULL, :], x[0:FULL * P, :].rearrange("(b p) d -> p b d", p=P)).then_inc(x_in, 16)
            sp.wait_ge(consts_done, 2)
            sp.dma_start(X[0:REST, FULL, :], x[FULL * P:N, :]).then_inc(x_in, 16)
            vectors = [(R_L0B2, L0_b2), (R_BE, L1_be), (R_L1B2, L1_b2), (R_GAMMA, L1_gamma),
                       (R_BETA, L1_beta), (R_BIN, L2_b_in), (R_BOUT, L2_b_out)]
            for n, v in vectors:
                sp.dma_start(ROWS[:, n, :], v.partition_broadcast(P)).then_inc(const_in, 16)
            for n, m in [(R_GCNB, L2_gcn_b), (R_GATB, L3_bias),
                         (R_ASRC, L3_att_src.rearrange("l h c -> l (h c)")),
                         (R_ADST, L3_att_dst.rearrange("l h c -> l (h c)"))]:
                sp.dma_start(ROWS[:, n:n + LAYERS, :], m.partition_broadcast(P)).then_inc(const_in, 16)
            sp.dma_start(epsp[:, :], L0_eps.partition_broadcast(P)).then_inc(const_in, 16)
            with nc.allow_non_contiguous_dma(reason="three short columns"):
                sp.dma_start(BCOL[:, 0:2], L0_b1.rearrange("(q d) -> d q", q=2)).then_inc(const_in, 16)
                sp.dma_start(BCOL[:, 2:3], L1_b1.rearrange("(d a) -> d a", a=1)).then_inc(const_in, 16)
            sp.dma_start(WTS[:, W_L0A:W_L0B + 1, :], L0_W1.rearrange("k (q n) -> k q n", q=2)).then_inc(weights_in, 16)
            sp.dma_start(WTS[:, W_L0C:W_L0D + 1, :], L0_W2.rearrange("(q k) n -> k q n", q=2)).then_inc(weights_in, 16)
            sp.dma_start(WTS[:, W_L11, :], L1_W1).then_inc(weights_in, 16)
            sp.dma_start(WTS[:, W_L12, :], L1_W2).then_inc(weights_in, 16)
            sp.dma_start(WTS[:, W_IN, :], L2_W_in).then_inc(weights_in, 16)
            sp.dma_start(WTS[:, W_GCN:W_GCN + LAYERS, :], L2_gcn_W.rearrange("l a b -> a l b")).then_inc(weights_in, 16)
            sp.dma_start(WTS[:, W_OUT, :], L2_W_out).then_inc(weights_in, 16)
            sp.dma_start(WTS[:, W_GAT:W_GAT + LAYERS, :], L3_W.rearrange("l a b -> a l b")).then_inc(weights_in, 16)
            for r in range(P // DE):
                sp.dma_start(WE[r * DE:(r + 1) * DE, r, :], L1_We).then_inc(weights_in, 16)

            tables = [0]

            def store_table(to, of):
                tables[0] += 1
                sp.wait_ge(table_ready, tables[0])
                sp.dma_start(to.rearrange("(b p) d -> p b d", p=P), of).then_inc(table_stored, 16)

            def load_attrs(t, attr, width, freed):
                at, name = t.base[freed], SEM[freed]
                for half in range(2):
                    e = firsts(half * U, U, SP)
                    for n in range(U):
                        sp.dma_start(EA[:, half, n * width:(n + 1) * width],
                                     attr[ds(e[n], P), :]).then_inc(SEM[f"attr_in{half}"], 16)
                with sp.Fori(1, ITERS) as it:
                    e = firsts(2 * U * it, 2 * U, SP)
                    for half in range(2):
                        sp.wait_ge(name, 2 * it + (at + half - 1))
                        for n in range(U):
                            sp.dma_start(EA[:, half, n * width:(n + 1) * width],
                                         attr[ds(e[half * U + n], P), :]).then_inc(SEM[f"attr_in{half}"], 16)

            store_table(table, H[:, :, :])
            load_attrs(Stage("L0"), edge_attr_96, D, "rows_ready")
            store_table(table, ACCF)
            sp.wait_ge(table_stored, 32)
            load_attrs(Stage("L1"), edge_attr_32, DE, "ea_flipped")
            for l in range(LAYERS):
                store_table(table, ACCF)
            for l in range(LAYERS):
                store_table(gat_table, ACC[:, :, :])
            sp.wait_ge(result_ready, 1)
            sp.dma_start(out[0:FULL * P, :].rearrange("(b p) d -> p b d", p=P), X[:, 0:FULL, :]).then_inc(out_done, 16)
            sp.dma_start(out[FULL * P:N, :], X[0:REST, FULL, :]).then_inc(out_done, 16)
            sp.wait_ge(out_done, 32)

        @block.gpsimd
        def _(pool):
            nc.gpsimd.iota(iota_row[:, :], [[1, P]], base=0, channel_multiplier=0,
                           allow_small_or_imprecise_dtypes=True).then_inc(iota_done, 1)
            nc.gpsimd.iota(iota_col[:, :], [[0, 1]], base=0, channel_multiplier=1,
                           allow_small_or_imprecise_dtypes=True).then_inc(iota_done, 1)
            nc.gpsimd.iota(heads[:, 0:P], [[1, P]], base=0, channel_multiplier=0).then_inc(heads_in, 1)
            nc.gpsimd.iota(heads[:, P:P + 1], [[0, 1]], base=0, channel_multiplier=1).then_inc(heads_in, 1)
            nc.gpsimd.iota(iota_k, [[1, STEPS]], base=0, channel_multiplier=0,
                           allow_small_or_imprecise_dtypes=True).then_inc(iota_done, 1)

            pool.wait_ge(rows_in, 5 * 16)
            pool.wait_ge(plan_ready, 2)
            for n, rows in enumerate((src_rows, dst_rows)):
                for c in range(KC):
                    pool.indirect_dma_start(win_i[n][:, c * P:(c + 1) * P], None, rows,
                                            bass.IndirectOffsetOnAxis(ap=row_i[:, c:c + 1], axis=0)).then_inc(windows_in, 16)

            def row_of(to, index, rows, landed):
                pool.indirect_dma_start(to, None, rows, bass.IndirectOffsetOnAxis(ap=index, axis=0)).then_inc(landed, 16)

            def sums_of(t):
                with pool.Fori(0, ROUNDS) as it:
                    for pair in range(UN // 2):
                        pool.wait_ge(SEM["seg_done"], UN * it + (freed(t, UN) + 2 * pair + 2))
                        pool.tensor_copy(NOW[:, pair, 0:2 * U], IDX[:, ds(UN * U * it + 2 * U * pair, 2 * U)])\
                            .then_inc(SEM["idx_ready"], 1)
                        pool.wait_ge(SEM["idx_ready"], UN // 2 * it + (t.base["idx_ready"] + pair + 1))
                        pool.sem_inc(idx_seen, 1)
                        for n in range(2 * U):
                            slot = 2 * pair + n // U
                            row_of(G[:, slot, n % U, 0:D], NOW[:, pair, n:n + 1], table, t.gathered[slot])

            def attention_rows(t):
                with pool.Fori(0, BATCHES // 2) as it:
                    for half in range(2):
                        for q in range(BG):
                            pool.wait_ge(SEM["seg_done"], 8 * it + (freed(t, 8) + BG * half + q + 1))
                            if q == 0:
                                pool.tensor_copy(NOW[:, half, :], IDX[:, ds(2 * BT * it + BT * half, BT)])\
                                    .then_inc(SEM["idx_ready"], 1)
                                pool.wait_ge(SEM["idx_ready"], 2 * it + (t.base["idx_ready"] + half + 1))
                            pool.sem_inc(idx_seen, 1)
                            for n in range(U):
                                row_of(G[:, BG * half + q, n, :], NOW[:, half, q * U + n:q * U + n + 1], gat_table,
                                       t.gathered[BG * half + q])

            zs = [0]

            def stage_blocks(t, z):
                zs[0] += 1
                pool.wait_ge(z_ready, zs[0])
                with pool.Fori(0, NG) as g:
                    pool.wait_ge(SEM["flipped"], g + t.base["flipped"])
                    pool.tensor_copy(zb[:, 0:Q * D].rearrange("p (b d) -> p b d", b=Q),
                                     z[:, ds(Q * g, Q), 0:D]).then_inc(SEM["staged"], 1)

            zs[0] += 1
            pool.wait_ge(z_ready, zs[0])
            t = Stage("flags")
            with pool.Fori(0, JG) as g:
                pool.wait_ge(SEM["flipped"], g + t.base["flipped"])
                pool.tensor_copy(zb.rearrange("p (k h) -> p k h", h=HEADS),
                                 dabs[:, ds(P * g, P)].unsqueeze(2).broadcast_to([P, P, HEADS])).then_inc(SEM["staged"], 1)
            pool.wait_ge(table_stored, 16)
            sums_of(Stage("L0"))
            stage_blocks(Stage("L0mlp"), ACC)
            pool.wait_ge(table_stored, 32)
            sums_of(Stage("L1"))
            stage_blocks(Stage("L1mlp"), ACC)
            stage_blocks(Stage("in"), H)
            for l in range(LAYERS):
                stage_blocks(Stage(f"gcn{l}"), H)
                pool.wait_ge(table_stored, 16 * (3 + l))
                sums_of(Stage(f"gcnsum{l}"))
            stage_blocks(Stage("out"), H)
            for l in range(LAYERS):
                stage_blocks(Stage(f"gat{l}"), H)
                pool.wait_ge(table_stored, 16 * (3 + LAYERS + l))
                attention_rows(Stage(f"attend{l}"))

        @block.scalar
        def _(act):
            roots = [0]

            def root(to, of):
                roots[0] += 1
                act.wait_ge(var_ready, roots[0])
                nc.scalar.activation(to, of, ACT.Sqrt).then_inc(root_ready, 1)

            def lift(t, of, to):
                with act.Fori(0, NG) as g:
                    act.wait_ge(SEM["flipped"], g + (t.base["flipped"] + 1))
                    nc.scalar.activation(to(g), of, ACT.Copy).then_inc(SEM["lifted"], 1)

            def lift_mlp(t, halves, bias):
                with act.Fori(0, NG) as g:
                    act.wait_ge(SEM["flipped"], g + (t.base["flipped"] + 1))
                    nc.scalar.activation(zT[0:D, :], psA[0:D, :], ACT.Copy).then_inc(SEM["lifted"], 1)
                    for q in range(halves):
                        act.wait_ge(SEM["hid_product"], halves * g + (t.base["hid_product"] + q + 1))
                        nc.scalar.activation(hid[0:D, q, :], (psB, psC)[q][0:D, :], ACT.Relu,
                                             bias=BCOL[:, bias + q:bias + q + 1]).then_inc(SEM["hid_ready"], 1)

            lift(Stage("flags"), psA[:, :], lambda g: lanes[:, ds(Q * P * g, Q * P)])
            root(stat[:, 1, :], stat[:, 0, :])
            root(dinv[:, :], dinv[:, :])
            act.wait_ge(const_in, 14 * 16)
            lift_mlp(Stage("L0mlp"), 2, 0)
            root(stat[:, 1, :], stat[:, 0, :])

            t = Stage("L1")

            def lift_attrs(half, at):
                act.wait_ge(SEM["ea_flipped"], at)
                half %= 2
                nc.scalar.activation(EA[:, half, U * DE:U * DE + 2 * P], psA[:, 0:2 * P], ACT.Copy)\
                  .then_inc(SEM["ea_lifted"], 1)

            def relu(half, at):
                act.wait_ge(SEM["summed"], at)
                nc.scalar.activation(G[:, half, :, 0:D], G[:, half, :, 0:D], ACT.Relu).then_inc(SEM["rows_ready"], 1)

            lift_attrs(0, t.base["ea_flipped"] + 1)

            def attr_round(it, slots):
                for j in slots:
                    lift_attrs(j + 1, UN * it + (t.base["ea_flipped"] + j + 2))
                    relu(j, 2 * UN * it + (t.base["summed"] + 2 * j + 2))

            with act.Fori(0, ROUNDS - 1) as it:
                attr_round(it, range(UN))
            attr_round(ROUNDS - 1, range(UN - 1))
            relu(UN - 1, t.end["summed"])

            lift_mlp(Stage("L1mlp"), 1, 2)
            root(HOT[:, 0, 1, 0:D], HOT[:, 0, 1, 0:D])
            for name in ["in"] + [f"gcn{l}" for l in range(LAYERS)] + ["out"]:
                if name == "in":
                    root(stat[:, 1, :], stat[:, 0, :])
                lift(Stage(name), psA[0:D, :], lambda g: zT[0:D, :])
            root(stat[:, 1, :], stat[:, 0, :])
            for l in range(LAYERS):
                lift(Stage(f"gat{l}"), psA[0:D, :], lambda g: zT[0:D, :])
                t = Stage(f"attend{l}")

                def logits(slot, it, n):
                    act.wait_ge(SEM["hot_read"], 8 * it + (t.base["hot_read"] + n + 1))
                    act.wait_ge(SEM["d_product"], 8 * it + (t.base["d_product"] + n))
                    nc.scalar.activation(ST[:, 0:4, :], psA[:, :].rearrange("p (a b) -> p a b", a=4), ACT.Copy)
                    nc.scalar.activation(ST[:, 4:8, :], psB[:, :].rearrange("p (a b) -> p a b", a=4), ACT.Copy)\
                      .then_inc(SEM["st_ready"], 1)
                    act.wait_ge(SEM["d_product"], 8 * it + (t.base["d_product"] + n + 1))
                    part = U * PARTS * HEADS
                    nc.scalar.activation(DL[:, slot // BG, slot % BG * part:(slot % BG + 1) * part],
                                         psC[:, 0:part], ACT.Copy).then_inc(SEM["d_copied"], 1)

                def exps(half, it):
                    act.wait_ge(SEM["exponent"], 4 * it + (t.base["exponent"] + 2 * half + 1))
                    nc.scalar.activation(WB[:, :, :], SB3, ACT.Exp)
                    nc.scalar.activation(G[:, BG * half:BG * (half + 1), :, D:WT].rearrange("p s k h -> p (s k) h"),
                                         SB3, ACT.Exp).then_inc(SEM["exp_made"], 1)
                    act.wait_ge(SEM["exponent"], 4 * it + (t.base["exponent"] + 2 * half + 2))
                    nc.scalar.activation(lone[0:1, 4:8], lone[0:1, 4:8], ACT.Exp).then_inc(SEM["exp_made"], 1)

                for q in range(BG):
                    logits(q, 0, q)

                def batch(it, half, more=True):
                    exps(half, it)
                    for q in range(BG if more else 0):
                        logits(BG * (1 - half) + q, it, BG * (half + 1) + q)

                with act.Fori(0, BATCHES // 2 - 1) as it:
                    batch(it, 0)
                    batch(it, 1)
                batch(BATCHES // 2 - 1, 0)
                batch(BATCHES // 2 - 1, 1, more=False)

        @block.tensor
        def _(pe):
            for name, value in START.items():
                if name != "acc_step":
                    pe.sem_inc(SEM[name], value)
            given = [0]

            def give(ins):
                given[0] += 1
                ins.then_inc(setup_product, 1)
            pe.wait_ge(setup_operand, 1)
            nc.tensor.matmul(psA[0:NB, 0:1], cnt[0:EP, 0:NB], ones[0:EP, 0:1], start=True, stop=True)
            give(nc.tensor.matmul(psA[0:NB, 1:2], cnt[0:EP, 1:NB + 1], ones[0:EP, 0:1], start=True, stop=True))
            pe.wait_ge(setup_operand, 2)
            give(nc.tensor.matmul(psA[0:NB, 2:3], upper[:, :], plan[0:NB, 3:4], start=True, stop=True))
            pe.wait_ge(setup_operand, 3)
            give(nc.tensor.matmul(psA[0:NB, 3:4], step_of[:, :], plan[0:NB, 5:6], start=True, stop=True))
            pe.wait_ge(setup_operand, 4)
            quarter = STEPS // 4
            for c in range(4):
                part = ind[0:NB, c * quarter:(c + 1) * quarter]
                nc.tensor.matmul(sums[c // 2][:, c % 2, 0:quarter], edge_dv[:, :], part, start=True, stop=True)
                last = nc.tensor.matmul((psA, psB, psC, psD)[c][:, 0:quarter], ones[0:NB, :], part, start=True, stop=True)
            give(last)
            pe.wait_ge(setup_operand, 5)
            pe.wait_ge(weights_in, (8 + P // DE) * 16)
            for n, w in enumerate(TURNED):
                last = nc.tensor.transpose(psA[0:D, n * D:(n + 1) * D], WTS[:, w, :], ident[0:D, 0:D])
            give(last)
            pe.wait_ge(setup_operand, 6)
            for c in range(KC):
                part = slice(c % 4 * P, (c % 4 + 1) * P)
                nc.tensor.transpose(sums[c // 8][:, c // 4 % 2, part], win_f[0][:, c * P:(c + 1) * P], ident[:, :])
                last = nc.tensor.transpose((psA, psB, psC, psD)[c // 4][:, part], win_f[1][:, c * P:(c + 1) * P], ident[:, :])
            give(last)
            for n in range(2):
                pe.wait_ge(setup_operand, 7 + n)
                for c in range(4):
                    last = nc.tensor.matmul(sums[c // 2][:, c % 2, 0:quarter], edge_of[:, :],
                                            dabs[:, c * quarter:(c + 1) * quarter], start=True, stop=True)
                give(last)

            def flip_blocks(t, g):
                pe.wait_ge(SEM["staged"], g + (t.base["staged"] + 1))
                pe.wait_ge(SEM["lifted"], g + t.base["lifted"])
                for q in range(Q):
                    last = nc.tensor.transpose(psA[0:D, q * P:(q + 1) * P], zb[:, q * D:(q + 1) * D], ident[:, :])
                last.then_inc(SEM["flipped"], 1)
                pe.wait_ge(SEM["lifted"], g + (t.base["lifted"] + 1))

            def dense_stage(t, w):
                with pe.Fori(0, NG) as g:
                    flip_blocks(t, g)
                    pe.wait_ge(SEM["taken"], g + t.base["taken"])
                    for q in range(Q):
                        last = nc.tensor.matmul(psD[:, q * D:(q + 1) * D], zT[0:D, q * P:(q + 1) * P], WTS[:, w, :],
                                                start=True, stop=True)
                    last.then_inc(SEM["made"], 1)

            def mlp_stage(t, halves, w1, w2):
                with pe.Fori(0, NG) as g:
                    flip_blocks(t, g)
                    pe.wait_ge(SEM["hid_ready"], halves * g + t.base["hid_ready"])
                    for h in range(halves):
                        nc.tensor.matmul((psB, psC)[h][0:D, :], WTS[:, w1 + h, :], zT[0:D, :],
                                         start=True, stop=True).then_inc(SEM["hid_product"], 1)
                    pe.wait_ge(SEM["hid_ready"], halves * g + (t.base["hid_ready"] + halves))
                    pe.wait_ge(SEM["taken"], g + t.base["taken"])
                    for q in range(Q):
                        for h in range(halves):
                            last = nc.tensor.matmul(psD[:, q * D:(q + 1) * D], hid[0:D, h, q * P:(q + 1) * P],
                                                    WTS[:, w2 + h, :], start=(h == 0), stop=(h == halves - 1))
                    last.then_inc(SEM["made"], 1)

            def segment_group(t, it, unroll, n, hot, slot, width):
                bank = sums[n % 2]
                pe.wait_ge(SEM["acc_step"], unroll * U * it + (t.base["acc_step"] + U * (n - 1)))
                for k in range(U):
                    last = nc.tensor.matmul(bank[:, k // 4, k % 4 * width:(k % 4 + 1) * width],
                                            HOT[:, hot, k, :], G[:, slot, k, 0:width], start=True, stop=True)
                last.then_inc(SEM["seg_done"], 1)

            def sum_stage(t, width, gathered=False):
                with pe.Fori(0, ROUNDS) as it:
                    for j in range(UN):
                        pe.wait_ge(SEM["hot_built"], UN * it + (t.base["hot_built"] + j + 1))
                        if gathered:
                            pe.wait_ge(t.gathered[j], 16 * U * it + 16 * U)
                        else:
                            pe.wait_ge(SEM["rows_ready"], UN * it + (t.base["rows_ready"] + j + 1))
                        segment_group(t, it, UN, j, j % 2, j, width)

            t = Stage("flags")
            with pe.Fori(0, JG) as g:
                pe.wait_ge(SEM["staged"], g + (t.base["staged"] + 1))
                pe.wait_ge(SEM["lifted"], g + t.base["lifted"])
                for q in range(Q):
                    last = nc.tensor.transpose(psA[:, q * P:(q + 1) * P], zb[:, q * P:(q + 1) * P], ident[:, :])
                last.then_inc(SEM["flipped"], 1)

            sum_stage(Stage("L0"), D + 1)
            mlp_stage(Stage("L0mlp"), 2, W_L0A, W_L0C)

            t = Stage("L1")

            def attr_product(half, attr_at, g1, g0):
                half %= 2
                pe.wait_ge(SEM[f"attr_in{half}"], attr_at)
                pe.wait_ge(SEM["ea_lifted"], t.base["ea_lifted"] + g0)
                for q in range(2):
                    last = nc.tensor.transpose(psA[:, q * P:(q + 1) * P], EA[:, half, q * P:(q + 1) * P], ident[:, :])
                last.then_inc(SEM["ea_flipped"], 1)
                pe.wait_ge(SEM["ea_lifted"], t.base["ea_lifted"] + g1)
                pe.wait_ge(SEM["summed"], t.base["summed"] + g0 * 2)
                for q in range(2):
                    nc.tensor.matmul((psB, psC)[q][:, 0:4 * D], EA[:, half, U * DE + q * P:U * DE + (q + 1) * P],
                                     WE[:, :, :].rearrange("p a b -> p (a b)"), start=True, stop=True)\
                      .then_inc(SEM["ea_product"], 1)

            def attr_round(it, slots):
                for j in slots:
                    nxt = j + 1
                    attr_product(nxt, 16 * U * UN // 2 * it + (t.base[f"attr_in{nxt % 2}"] + 16 * U * (nxt // 2 + 1)),
                                 UN * it + nxt + 1, UN * it + nxt)
                    relu_sum(it, j)

            def relu_sum(it, j):
                pe.wait_ge(SEM["hot_built"], UN * it + (t.base["hot_built"] + j + 1))
                pe.wait_ge(SEM["rows_ready"], UN * it + (t.base["rows_ready"] + j + 1))
                segment_group(t, it, UN, j, j % 2, j, D)

            attr_product(0, t.base["attr_in0"] + 16 * U, 1, 0)
            with pe.Fori(0, ROUNDS - 1) as it:
                attr_round(it, range(UN))
            attr_round(ROUNDS - 1, range(UN - 1))
            relu_sum(ROUNDS - 1, UN - 1)

            mlp_stage(Stage("L1mlp"), 1, W_L11, W_L12)
            for n in range(2):
                pe.wait_ge(feature_sums, 1 + n)
                nc.tensor.matmul(psB[:, n * D:(n + 1) * D], ones[:, :], HOT[:, 0, n, 0:D],
                                 start=True, stop=True).then_inc(feature_totals, 1)
            dense_stage(Stage("in"), W_IN)
            for l in range(LAYERS):
                dense_stage(Stage(f"gcn{l}"), W_GCN + l)
                sum_stage(Stage(f"gcnsum{l}"), D, gathered=True)
            dense_stage(Stage("out"), W_OUT)
            for l in range(LAYERS):
                dense_stage(Stage(f"gat{l}"), W_GAT + l)
                t2 = Stage(f"attend{l}")

                def flip_hot(slot, it, n):
                    pe.wait_ge(SEM["hot_built"], 8 * it + (t2.base["hot_built"] + n + 1))
                    pe.wait_ge(SEM["st_ready"], 8 * it + (t2.base["st_ready"] + n))
                    for k in range(U):
                        last = nc.tensor.transpose((psA, psB)[k // 4][:, k % 4 * P:(k % 4 + 1) * P],
                                                   HOT[:, slot, k, :], ident[:, :])
                    last.then_inc(SEM["hot_read"], 1)

                def logits(it, n):
                    b = blocks(8 * U * it + U * n, U, PE)
                    pe.wait_ge(SEM["st_ready"], 8 * it + (t2.base["st_ready"] + n + 1))
                    pe.wait_ge(SEM["d_copied"], 8 * it + (t2.base["d_copied"] + n))
                    part = PARTS * HEADS
                    for k in range(U):
                        last = nc.tensor.matmul(psC[:, k * part:(k + 1) * part], ST[:, k, :],
                                                DDP[:, ds(b[k], 1), :, :].rearrange("p b s h -> p (b s h)"),
                                                start=True, stop=True)
                    last.then_inc(SEM["d_product"], 1)

                def reply(it, half, n):
                    pe.wait_ge(SEM["lane_ask"], 2 * LANE_ASKS * it + (t2.base["lane_ask"] + LANE_ASKS * half + n + 1))
                    if n == 0:
                        last = nc.tensor.transpose(psD[:, 0:P], SB[:, :], ident[:, :])
                    elif n == 1:
                        last = nc.tensor.matmul(psD[:, P:2 * P + HEADS], ones[:, :], LW[:, 2, :], start=True, stop=True)
                    elif n == 2:
                        last = nc.tensor.matmul(psD[:, P:2 * P], ones[:, :], LW[:, 2, 0:P], start=True, stop=True)
                    elif n == 3:
                        last = nc.tensor.transpose(psD[:, 2 * P:3 * P], LW[:, 0, 0:P], ident[:, :])
                    else:
                        last = nc.tensor.matmul(psD[:, 3 * P:3 * P + HEADS], HOT[0:1, BG * half, 0, :],
                                                lone[0:1, 4:8], start=True, stop=True)
                    last.then_inc(SEM["lane_reply"], 1)

                for q in range(BG):
                    flip_hot(q, 0, q)
                    logits(0, q)
                for n in range(HEAD_ASKS):
                    reply(0, 0, n)

                def batch(it, half, more=True):
                    nxt, other = (it + half, 1 - half) if more else (None, None)

                    def add_edges(q):
                        n = BG * half + q
                        pe.wait_ge(SEM["rows_ready"], 8 * it + (t2.base["rows_ready"] + n + 1))
                        segment_group(t2, it, 8, n, n, n, WT)

                    def flip_next(q):
                        if more:
                            flip_hot(BG * other + q, it, BG * (half + 1) + q)

                    def logits_next(q):
                        if more:
                            logits(it, BG * (half + 1) + q)

                    def reply_next(n):
                        if more:
                            reply(nxt, other, n)

                    reply(it, half, HEAD_ASKS)
                    add_edges(0)
                    flip_next(0)
                    add_edges(1)
                    logits_next(0)
                    flip_next(1)
                    reply_next(0)
                    add_edges(2)
                    logits_next(1)
                    flip_next(2)
                    reply_next(1)
                    reply_next(2)
                    add_edges(3)
                    logits_next(2)
                    flip_next(3)
                    reply_next(3)
                    logits_next(3)

                with pe.Fori(0, BATCHES // 2 - 1) as it:
                    batch(it, 0)
                    batch(it, 1)
                batch(BATCHES // 2 - 1, 0)
                batch(BATCHES // 2 - 1, 1, more=False)

        @block.vector
        def _(dve):
            done = [0]
            v = nc.vector

            def link(ins):
                done[0] += 1
                ins.then_inc(chain, 1)
                dve.wait_ge(chain, done[0])

            asked = [0]

            def ask(ins):
                asked[0] += 1
                ins.then_inc(setup_operand, 1)
                dve.wait_ge(setup_product, asked[0])

            v.memset(X[:, FULL:NBP, :], 0.0).then_inc(consts_done, 1)
            link(v.memset(ones[:, :], 1.0))
            v.memset(WE[:, :, :], 0.0).then_inc(consts_done, 1)
            v.memset(ACC[:, :, :], 0.0).then_inc(SEM["acc_step"], START["acc_step"])
            dve.wait_ge(SEM["acc_step"], START["acc_step"])
            link(v.memset(plan[:, :], 0.0))
            dve.wait_ge(iota_done, 3)
            link(v.tensor_scalar(ident[:, :], iota_row[:, :], iota_col[:, 0:1], None, ALU.is_equal))
            link(v.tensor_scalar(upper[:, :], iota_row[0:NB, 0:NB], iota_col[0:NB, 0:1], None, ALU.is_gt))
            link(v.tensor_scalar(plan[0:P, 0:1], iota_col[:, 0:1], 1.0, None, ALU.add))
            link(v.tensor_scalar(step_of[:, :], iota_row[0:NB, 0:NB], plan[0:NB, 0:1], None, ALU.is_equal))
            link(v.tensor_tensor(step_of[:, :], ident[0:NB, 0:NB], step_of[:, :], ALU.subtract))
            link(v.tensor_scalar(valid[:, :], iota_col[:, 0:1], float(REST), None, ALU.is_lt))

            dve.wait_ge(dst_in, 16)
            link(v.tensor_copy(dst_f, dst_i))
            link(v.memset(cnt[:, 0:1], 0.0))
            link(v.memset(cnt[:, NB:NB + 1], float(EF)))
            for b in range(1, NB):
                link(v.tensor_scalar(less, dst_f, float(b * P), None, ALU.is_lt, ALU.add, accum_out=cnt[0:EP, b:b + 1]))
            ask(v.memset(plan[:, 7:8], 0.0))
            link(v.tensor_copy(plan[0:NB, 1:3], psA[0:NB, 0:2]))
            link(v.tensor_copy(tiles_i[0:NB, 0:1], plan[0:NB, 1:2]))
            link(v.tensor_scalar(tiles_i[0:NB, 1:2], plan[0:NB, 2:3], float(P - 1), None, ALU.add))
            link(v.tensor_scalar(tiles_i[0:NB, 0:2], tiles_i[0:NB, 0:2], P.bit_length() - 1, None,
                                 ALU.logical_shift_right))
            link(v.tensor_tensor(plan[0:NB, 3:4], tiles_i[0:NB, 1:2], tiles_i[0:NB, 0:1], ALU.subtract))
            link(v.tensor_tensor(plan[0:NB, 6:7], plan[0:NB, 2:3], plan[0:NB, 1:2], ALU.is_gt))
            ask(v.tensor_tensor(plan[0:NB, 3:4], plan[0:NB, 3:4], plan[0:NB, 6:7], ALU.mult))
            link(v.tensor_copy(plan[0:NB, 4:5], psA[0:NB, 2:3]))
            ask(v.tensor_tensor(plan[0:NB, 5:6], tiles_i[0:NB, 0:1], plan[0:NB, 4:5], ALU.subtract))
            link(v.tensor_copy(plan[0:NB, 6:7], psA[0:NB, 3:4]))
            link(v.tensor_scalar(edge_dv[:, :], ones[0:NB, :], plan[0:NB, 6:7], None, ALU.mult))
            ask(v.tensor_scalar(ind[0:NB, :], iota_k[0:NB, :], plan[0:NB, 4:5], None, ALU.is_ge))
            quarter = STEPS // 4
            for c in range(4):
                part = slice(c * quarter, (c + 1) * quarter)
                link(v.tensor_tensor(first[:, part], iota_k[:, part], sums[c // 2][:, c % 2, 0:quarter], ALU.add))
                link(v.tensor_scalar(block_of[:, part], (psA, psB, psC, psD)[c][:, 0:quarter], -1.0, None, ALU.add))
            by_chunk = [a.rearrange("p (c k) -> p c k", k=P) for a in (ind, keep)]
            link(v.tensor_scalar(ind, first, float(ET - 1), None, ALU.min))
            link(v.tensor_tensor(by_chunk[1], by_chunk[0], ident[:, :].unsqueeze(1).broadcast_to([P, KC, P]), ALU.mult))
            link(v.tensor_reduce(stat[:, 0, 0:KC], by_chunk[1], AX.X, ALU.add))
            v.tensor_copy(row_i[:, :], stat[:, 0, 0:KC]).then_inc(plan_ready, 1)
            link(v.tensor_scalar(first, first, float(P), None, ALU.mult))
            link(v.tensor_scalar(ind, first, float(E - P), None, ALU.min))
            v.tensor_copy(EB[32:33, :], ind[32:33, :])
            v.tensor_copy(EB[64:65, :], block_of[64:65, :]).then_inc(plan_ready, 1)
            link(v.tensor_tensor(keep, first, ind, ALU.subtract))
            link(v.tensor_scalar(keep, keep, iota_col[:, 0:1], None, ALU.is_le))
            ask(v.memset(plan[:, 7:8], 0.0))
            link(v.tensor_copy(WTS[:, W_IN:W_OUT + 1, :], psA[0:D, 0:5 * D].rearrange("p (w d) -> p w d", w=5)))

            roots = [0]

            def root(ins):
                roots[0] += 1
                ins.then_inc(var_ready, 1)
                dve.wait_ge(root_ready, roots[0])

            def over_blocks(vec):
                return vec.broadcast_to([P, NBP, D])

            def over_features(col):
                return col.unsqueeze(2).broadcast_to([P, NBP, D])

            def normalise():
                link(v.tensor_reduce(stat[:, 0, :], X[:, :, :], AX.X, ALU.add))
                link(v.tensor_scalar(stat[:, 0, :], stat[:, 0, :], 1.0 / D, None, ALU.mult))
                link(v.tensor_tensor(H[:, :, :], X[:, :, :], over_features(stat[:, 0, :]), ALU.subtract))
                link(v.tensor_tensor(ACCF, H[:, :, :], H[:, :, :], ALU.mult))
                link(v.tensor_reduce(stat[:, 0, :], ACCF, AX.X, ALU.add))
                root(v.tensor_scalar(stat[:, 0, :], stat[:, 0, :], 1.0 / D, LN_EPS, ALU.mult, ALU.add))
                link(v.reciprocal(stat[:, 0, :], stat[:, 1, :]))
                link(v.scalar_tensor_tensor(H[:, :, :], H[:, :, :], 0.0, over_features(stat[:, 0, :]), ALU.max, ALU.mult))

            dve.wait_ge(windows_in, 2 * KC * 16)
            link(v.tensor_copy(win_f[0], win_i[0]))
            ask(v.tensor_copy(win_f[1], win_i[1]))
            for c in range(0, STEPS, 512):
                n = min(512, STEPS - c)
                part = slice(c, c + n)
                link(v.tensor_copy(IDX[:, part], sums[c // 1024][:, c // 512 % 2, 0:n]))
                got = (psA, psB, psC, psD)[c // 512][:, 0:n]
                link(v.tensor_copy(dabs[:, part], got))
                link(v.scalar_tensor_tensor(first[:, part], block_of[:, part], -float(P), got, ALU.mult, ALU.add))
                link(v.scalar_tensor_tensor(first[:, part], first[:, part], 1.0, keep[:, part], ALU.add, ALU.mult))
                link(v.tensor_scalar(REL[:, part], first[:, part], -1.0, None, ALU.add))
            link(v.tensor_scalar(OUT[:, :], keep, -1.0, BIG, ALU.add, ALU.mult))
            v.memset(plan[:, 7:8], 0.0).then_inc(z_ready, 1)

            for n, to in enumerate((begins, ends)):
                ask(v.tensor_scalar(edge_of[:, :], ones[:, :], ident[:, n * (P - 1):n * (P - 1) + 1], None, ALU.mult))
                for c in range(4):
                    link(v.tensor_copy(to[:, c * quarter:(c + 1) * quarter], sums[c // 2][:, c % 2, 0:quarter]))
            dve.wait_ge(SEM["lifted"], Stage("flags").end["lifted"])
            by_batch = lanes.rearrange("p (b e) -> p b e", e=P)
            link(v.memset(CUT[:, :, :], 0.0))
            link(v.tensor_tensor(CUT[:, :, 1:P], by_batch[:, :, 1:P], by_batch[:, :, 0:P - 1], ALU.not_equal))
            link(v.tensor_scalar(CUT[:, :, 1:P], CUT[:, :, 1:P], -BIG, None, ALU.mult))
            brk = [ACC_flat[:, n * STEPS:(n + 1) * STEPS] for n in range(1, 3)]
            link(v.tensor_tensor(brk[0], begins, ends, ALU.not_equal))
            link(v.memset(brk[1][:, 0:1], 1.0))
            link(v.tensor_tensor(brk[1][:, 1:STEPS], begins[:, 1:STEPS], ends[:, 0:STEPS - 1], ALU.not_equal))
            link(v.tensor_scalar(JOIN[:, :], brk[1][0:1, 0:STEPS:BT], -1.0, 1.0, ALU.mult, ALU.add))
            link(v.tensor_tensor_scan(ends, brk[1], brk[0], 0.0, ALU.add, ALU.add))
            link(v.tensor_tensor(begins, ends, brk[0], ALU.subtract))
            own = [stat[:, n, :] for n in range(2)]
            every = lanes.rearrange("p (b t h) -> p b t h", t=BT, h=HEADS)
            eye = ident[:, :].rearrange("p (t h) -> p t h", h=HEADS).unsqueeze(1).broadcast_to([P, BATCHES, BT, HEADS])
            counts = [a.rearrange("p (b t) -> p b t", t=BT).unsqueeze(3).broadcast_to([P, BATCHES, BT, HEADS])
                      for a in (begins, ends)]
            for n in range(2):
                link(v.tensor_tensor(every, counts[n], eye, ALU.mult))
                link(v.tensor_reduce(own[n][:, 0:BATCHES], by_batch, AX.X, ALU.add))
            head_i = chained[:, 0:P].bitcast(i32)
            same = chained[:, P:2 * P]
            side = chained[:, 2 * P:3 * P]
            head_f = chained[:, 3 * P:4 * P]
            dve.wait_ge(heads_in, 2)
            link(v.tensor_scalar(head_i, heads[:, 0:P], HEADS - 1, None, ALU.bitwise_and))
            link(v.tensor_copy(head_f, head_i))
            link(v.tensor_scalar(head_i[:, 0:1], heads[:, P:P + 1], HEADS - 1, None, ALU.bitwise_and))
            link(v.tensor_copy(lone[:, 0:1], head_i[:, 0:1]))
            link(v.tensor_scalar(same, head_f, lone[:, 0:1], None, ALU.is_equal))
            for n, (to, order) in enumerate(((FORE[:, :, 0:P], ALU.is_lt), (AFT[:, :, :], ALU.is_gt))):
                link(v.tensor_scalar(side, iota_row[:, :], iota_col[:, 0:1], None, order))
                link(v.tensor_tensor(side, side, same, ALU.mult))
                mine = own[n][:, 0:BATCHES].unsqueeze(2).broadcast_to([P, BATCHES, P])
                link(v.tensor_tensor(every, counts[1 - n], mine.rearrange("p b (t h) -> p b t h", h=HEADS), ALU.is_equal))
                link(v.tensor_tensor(by_batch, by_batch, side.unsqueeze(1).broadcast_to([P, BATCHES, P]), ALU.mult))
                link(v.tensor_scalar(to, by_batch, -1.0, BIG, ALU.add, ALU.mult))
            prior = lanes[:, 0:BATCHES * HEADS].rearrange("p (b h) -> p b h", h=HEADS)
            link(v.memset(prior, 0.0))
            link(v.tensor_tensor(prior[:, 1:BATCHES, :],
                                 ends[:, BT - 1:STEPS - 1:BT].unsqueeze(2).broadcast_to([P, BATCHES - 1, HEADS]),
                                 own[0][:, 1:BATCHES].unsqueeze(2).broadcast_to([P, BATCHES - 1, HEADS]), ALU.is_equal))
            link(v.tensor_tensor(prior, prior, same[:, 0:HEADS].unsqueeze(1).broadcast_to([P, BATCHES, HEADS]), ALU.mult))
            link(v.tensor_scalar(FORE[:, :, P:P + HEADS], prior, -1.0, BIG, ALU.add, ALU.mult))

            dve.wait_ge(x_in, 32)
            dve.wait_ge(const_in, 14 * 16)
            normalise()
            link(v.memset(ACC[:, :, :], 0.0))
            link(v.memset(G[:, :, :, :], 1.0))
            v.memset(plan[:, 7:8], 0.0).then_inc(table_ready, 1)

            def build_hot(half, k):
                v.tensor_tensor(HOT[:, half, :, :], iota_row[:, :].unsqueeze(1).broadcast_to([P, U, P]),
                                REL[:, ds(k, U)].unsqueeze(2).broadcast_to([P, U, P]), ALU.is_equal)\
                 .then_inc(SEM["hot_built"], 1)

            def add_up(t, it, unroll, n, width):
                b = blocks(unroll * U * it + U * n, U, DVE)
                dve.wait_ge(SEM["seg_done"], unroll * it + (t.base["seg_done"] + n + 1))
                for k in range(U):
                    to = ACC[:, ds(b[k], 1), 0:width].squeeze(1)
                    v.tensor_tensor(to, to, sums[n % 2][:, k // 4, k % 4 * width:(k % 4 + 1) * width], ALU.add)\
                     .then_inc(SEM["acc_step"], 1)
                    dve.wait_ge(SEM["acc_step"], unroll * U * it + (t.base["acc_step"] + U * n + k + 1))

            def sum_stage(t, width, prepare):
                def ready(it, j):
                    dve.wait_ge(SEM["seg_done"], UN * it + (freed(t, 2) + j + 1))
                    build_hot(j % 2, UN * U * it + U * j)
                    if prepare:
                        prepare(it, j)

                def turn(it, slots):
                    for j in slots:
                        if j < UN - 1:
                            ready(it, j + 1)
                        else:
                            ready(it + 1, 0)
                        add_up(t, it, UN, j, width)
                ready(0, 0)
                with dve.Fori(0, ROUNDS - 1) as it:
                    turn(it, range(UN))
                turn(ROUNDS - 1, range(UN - 1))
                add_up(t, ROUNDS - 1, UN, UN - 1, width)

            def take(t, use):
                with dve.Fori(0, NG) as g:
                    dve.wait_ge(SEM["made"], g + (t.base["made"] + 1))
                    use(g, psD[:, 0:Q * D].rearrange("p (b d) -> p b d", b=Q)).then_inc(SEM["taken"], 1)
                dve.wait_ge(SEM["taken"], t.end["taken"])

            def z_is_ready():
                v.memset(plan[:, 7:8], 0.0).then_inc(z_ready, 1)

            t0 = Stage("L0")

            def add_attr(it, j):
                half = j % 2
                dve.wait_ge(t0.gathered[j], 16 * U * it + 16 * U)
                dve.wait_ge(SEM[f"attr_in{half}"],
                            16 * U * UN // 2 * it + (t0.base[f"attr_in{half}"] + 16 * U * (j // 2 + 1)))
                v.tensor_tensor(G[:, j, :, 0:D], G[:, j, :, 0:D],
                                EA[:, half, :].rearrange("p (k d) -> p k d", k=U), ALU.add)\
                 .then_inc(SEM["rows_ready"], 1)
            sum_stage(t0, D + 1, add_attr)
            root(v.tensor_scalar(dinv[:, :], ACC[:, :, D], 1.0, None, ALU.add))
            link(v.reciprocal(dinv[:, :], dinv[:, :]))
            z_is_ready()
            link(v.tensor_scalar(epsp[:, :], epsp[:, :], 1.0, None, ALU.add))
            link(v.scalar_tensor_tensor(X[:, :, :], H[:, :, :], epsp[:, 0:1], X[:, :, :], ALU.mult, ALU.add))
            link(v.tensor_tensor(X[:, :, :], X[:, :, :], over_blocks(row(R_L0B2)), ALU.add))
            take(Stage("L0mlp"), lambda g, p: v.tensor_tensor(X[:, ds(Q * g, Q), :], p, X[:, ds(Q * g, Q), :], ALU.add))
            normalise()

            link(v.tensor_tensor(ACCF, H[:, :, :], over_blocks(row(R_BE)), ALU.add))
            v.memset(plan[:, 7:8], 0.0).then_inc(table_ready, 1)
            dve.wait_ge(table_stored, 32)
            link(v.tensor_copy(ACCF, H[:, :, :]))
            t1 = Stage("L1")

            def add_product(it, j):
                dve.wait_ge(t1.gathered[j], 16 * U * it + 16 * U)
                for q in range(2):
                    dve.wait_ge(SEM["ea_product"], 2 * UN * it + (t1.base["ea_product"] + 2 * j + q + 1))
                    v.tensor_tensor(G[:, j, 4 * q:4 * q + 4, 0:D], G[:, j, 4 * q:4 * q + 4, 0:D],
                                    (psB, psC)[q][:, 0:4 * D].rearrange("p (k d) -> p k d", k=4), ALU.add)\
                     .then_inc(SEM["summed"], 1)
            sum_stage(t1, D, add_product)
            z_is_ready()
            take(Stage("L1mlp"), lambda g, p: v.tensor_tensor(
                H[:, ds(Q * g, Q), :], p, row(R_L1B2).broadcast_to([P, Q, D]), ALU.add))
            hot0, hot1 = HOT[:, 0, 0, 0:D], HOT[:, 0, 1, 0:D]
            by_feature = H[:, 0:NB, :].rearrange("p b d -> p d b")
            link(v.tensor_scalar(H[:, NB - 1, :], H[:, NB - 1, :], valid[:, 0:1], None, ALU.mult))
            v.tensor_reduce(hot0, by_feature, AX.X, ALU.add).then_inc(feature_sums, 1)
            dve.wait_ge(feature_totals, 1)
            link(v.tensor_scalar(hot0, psB[:, 0:D], 1.0 / N, None, ALU.mult))
            link(v.tensor_tensor(H[:, :, :], H[:, :, :], over_blocks(HOT[:, 0, 0:1, 0:D]), ALU.subtract))
            link(v.tensor_scalar(H[:, NB - 1, :], H[:, NB - 1, :], valid[:, 0:1], None, ALU.mult))
            link(v.tensor_tensor(ACCF, H[:, :, :], H[:, :, :], ALU.mult))
            v.tensor_reduce(hot1, ACC[:, 0:NB, 0:D].rearrange("p b d -> p d b"), AX.X, ALU.add).then_inc(feature_sums, 1)
            dve.wait_ge(feature_totals, 2)
            hot2 = HOT[:, 0, 2, 0:D]
            link(v.tensor_scalar(hot2, psB[:, D:2 * D], 1.0 / N, BN_EPS, ALU.mult, ALU.add))
            root(v.tensor_copy(hot1, hot2))
            link(v.reciprocal(hot0, hot1))
            link(v.tensor_tensor(hot0, hot0, ROWS[:, R_GAMMA, :], ALU.mult))
            link(v.tensor_tensor(H[:, :, :], H[:, :, :], over_blocks(HOT[:, 0, 0:1, 0:D]), ALU.mult))
            link(v.tensor_tensor(H[:, :, :], H[:, :, :], over_blocks(row(R_BETA)), ALU.add))
            link(v.scalar_tensor_tensor(X[:, :, :], H[:, :, :], 0.0, X[:, :, :], ALU.max, ALU.add))
            normalise()

            z_is_ready()
            take(Stage("in"), lambda g, p: v.tensor_tensor(
                H[:, ds(Q * g, Q), :], p, row(R_BIN).broadcast_to([P, Q, D]), ALU.add))
            link(v.tensor_scalar(H[:, :, :], H[:, :, :], 0.0, None, ALU.max))
            for l in range(LAYERS):
                z_is_ready()
                take(Stage(f"gcn{l}"), lambda g, p: v.tensor_tensor(
                    ACC[:, ds(Q * g, Q), 0:D], p, dinv[:, ds(Q * g, Q)].unsqueeze(2).broadcast_to([P, Q, D]), ALU.mult))
                v.memset(plan[:, 7:8], 0.0).then_inc(table_ready, 1)
                dve.wait_ge(table_stored, 16 * (3 + l))
                sum_stage(Stage(f"gcnsum{l}"), D, None)
                link(v.tensor_tensor(ACCF, ACCF, over_features(dinv[:, :]), ALU.mult))
                link(v.tensor_tensor(ACCF, ACCF, over_blocks(row(R_GCNB + l)), ALU.add))
                link(v.scalar_tensor_tensor(H[:, :, :], ACCF, 0.0, H[:, :, :], ALU.max, ALU.add))
            z_is_ready()
            link(v.tensor_tensor(X[:, :, :], X[:, :, :], over_blocks(row(R_BOUT)), ALU.add))
            take(Stage("out"), lambda g, p: v.tensor_tensor(X[:, ds(Q * g, Q), :], p, X[:, ds(Q * g, Q), :], ALU.add))
            normalise()

            for l in range(LAYERS):
                z_is_ready()
                take(Stage(f"gat{l}"), lambda g, p: v.tensor_copy(ACC[:, ds(Q * g, Q), 0:D], p))
                for r, to in ((R_ASRC, ACC[:, :, D:WT]), (R_ADST, DD[:, :, :])):
                    link(v.tensor_tensor(H[:, :, :], ACCF, over_blocks(row(r + l)), ALU.mult))
                    link(v.tensor_reduce(to, H[:, :, :].rearrange("p b (h c) -> p b h c", h=HEADS), AX.X, ALU.add))
                v.memset(plan[:, 7:8], 0.0).then_inc(table_ready, 1)
                for s in range(PARTS):
                    link(v.tensor_copy(DDP[:, :, s, :], DD[:, :, :]))
                    if s < PARTS - 1:
                        link(v.tensor_tensor(DD[:, :, :], DD[:, :, :], DDP[:, :, s, :], ALU.subtract))
                dve.wait_ge(table_stored, 16 * (3 + LAYERS + l))
                link(v.memset(ACC[:, :, :], 0.0))
                link(v.memset(lone[:, :], -BIG))
                t = Stage(f"attend{l}")
                leaky = lambda to, of: v.scalar_tensor_tensor(to, of, SLOPE, of, ALU.mult, ALU.max)

                run, scan, diag = LW[:, 0, 0:P], LW[:, 1, 0:P], LW[:, 2, :]
                top, worth = LW[:, 1, 0:P], lone[0:1, 4:8]

                class Lanes:

                    def __init__(self, it, half, steps, asks):
                        self.it, self.half, self.steps, self.asks = it, half, steps, asks

                    def step(self, ins):
                        self.steps += 1
                        ins.then_inc(SEM["lane_step"], 1)

                    def steps_done(self):
                        dve.wait_ge(SEM["lane_step"], 2 * LANE_STEPS * self.it
                                    + (t.base["lane_step"] + LANE_STEPS * self.half + self.steps))

                    def ask(self, ins):
                        self.asks += 1
                        ins.then_inc(SEM["lane_ask"], 1)

                    def reply(self):
                        dve.wait_ge(SEM["lane_reply"], 2 * LANE_ASKS * self.it
                                    + (t.base["lane_reply"] + LANE_ASKS * self.half + self.asks))

                def head(it, half, adds):
                    lanes = Lanes(it, half, 0, 0)
                    step, steps_done, ask_lane, reply = lanes.step, lanes.steps_done, lanes.ask, lanes.reply
                    batch_no = 2 * it + half
                    for q in range(BG):
                        dve.wait_ge(t.gathered[BG * half + q], 16 * U * it + 16 * U)
                    ask_lane(v.tensor_tensor(SB3, G[:, BG * half:BG * (half + 1), :, D:WT].rearrange("p s k h -> p (s k) h"),
                                             OUT[:, ds(BT * batch_no, BT)].unsqueeze(2).broadcast_to([P, BT, HEADS]),
                                             ALU.add))
                    step(v.tensor_copy(cut_now[:, :], CUT[:, ds(batch_no, 1), :].squeeze(1)))
                    step(v.tensor_scalar(diag[:, P:P + HEADS], ident[:, P - HEADS:P], lone[:, 1:2], None, ALU.mult))
                    adds(2)
                    steps_done()
                    reply()
                    step(v.tensor_tensor_scan(run, cut_now[:, 0:P], psD[:, 0:P], -BIG, ALU.add, ALU.max))
                    adds(1)
                    steps_done()
                    ask_lane(v.tensor_scalar(diag[:, 0:P], ident[:, :], run[:, P - 1:P], None, ALU.mult))
                    adds(3)
                    reply()
                    step(v.tensor_tensor(LW[:, 3, :], psD[:, P:2 * P + HEADS],
                                         FORE[:, ds(batch_no, 1), :].squeeze(1), ALU.add))
                    step(v.tensor_copy(worth, psD[0:1, 2 * P:2 * P + HEADS]))
                    adds(1)
                    steps_done()
                    step(v.tensor_reduce(lone[:, 0:1], LW[:, 3, :], AX.X, ALU.max))
                    adds(1)
                    steps_done()
                    step(v.tensor_tensor_scan(run, cut_now[:, 0:P], psD[:, 0:P], lone[:, 0:1], ALU.add, ALU.max))
                    adds(1)
                    steps_done()
                    step(v.tensor_tensor_scan(scan[:, ::-1], cut_now[:, P:0:-1], run[:, ::-1], -BIG, ALU.add, ALU.max))
                    step(v.tensor_copy(lone[:, 1:2], run[:, P - 1:P]))
                    adds(1)
                    steps_done()
                    ask_lane(v.tensor_scalar(diag[:, 0:P], ident[:, :], scan[:, 0:1], None, ALU.mult))
                    adds(4)
                    reply()
                    step(v.tensor_tensor(LW[:, 3, 0:P], psD[:, P:2 * P], AFT[:, ds(batch_no, 1), :].squeeze(1), ALU.add))
                    adds(1)
                    steps_done()
                    step(v.tensor_reduce(lone[:, 0:1], LW[:, 3, 0:P], AX.X, ALU.max))
                    adds(1)
                    steps_done()
                    ask_lane(v.tensor_tensor_scan(run[:, ::-1], cut_now[:, P:0:-1], run[:, ::-1], lone[:, 0:1],
                                                  ALU.add, ALU.max))
                    assert (lanes.steps, lanes.asks) == (HEAD_STEPS, HEAD_ASKS)

                def tail(it, half):
                    lanes = Lanes(it, half, HEAD_STEPS, HEAD_ASKS)
                    step, steps_done, ask_lane, reply = lanes.step, lanes.steps_done, lanes.ask, lanes.reply
                    batch_no = 2 * it + half
                    d_logit = LW[:, 3, 0:P]
                    dve.wait_ge(SEM["d_copied"], 8 * it + (t.base["d_copied"] + BG * half + BG))
                    step(v.tensor_reduce(d_logit.rearrange("p (t h) -> p t h", h=HEADS),
                                         DL[:, half, :].rearrange("p (t s h) -> p t h s", s=PARTS, h=HEADS),
                                         AX.X, ALU.add))
                    steps_done()
                    step(v.tensor_tensor(SB[:, :], SB[:, :], d_logit, ALU.add))
                    step(v.tensor_tensor(worth, worth, d_logit[0:1, 0:HEADS], ALU.add))
                    reply()
                    step(v.tensor_tensor(top, psD[:, 2 * P:3 * P], d_logit, ALU.add))
                    steps_done()
                    step(leaky(SB[:, :], SB[:, :]))
                    step(leaky(worth, worth))
                    step(leaky(top, top))
                    steps_done()
                    v.tensor_tensor(SB[:, :], SB[:, :], top, ALU.subtract).then_inc(SEM["exponent"], 1)
                    step(v.tensor_tensor(worth, worth, top[0:1, 0:HEADS], ALU.subtract))
                    steps_done()
                    v.tensor_scalar(worth, worth, JOIN[:, ds(batch_no, 1)], None, ALU.mult)\
                     .then_inc(SEM["exponent"], 1)
                    dve.wait_ge(SEM["exp_made"], 4 * it + (t.base["exp_made"] + 2 * half + 2))
                    ask_lane(v.tensor_scalar(worth, worth, -1.0, None, ALU.add))
                    reply()
                    step(v.tensor_scalar(scales[:, :], psD[:, 3 * P:3 * P + HEADS], 1.0, None, ALU.add))
                    b = blocks(2 * BT * it + BT * half, 1, DVE)
                    dve.wait_ge(SEM["acc_step"], 8 * U * it + (t.base["acc_step"] + BT * half))
                    steps_done()
                    node = ACC[:, ds(b[0], 1), :].squeeze(1)
                    sums_of_node = node[:, 0:D].rearrange("p (h c) -> p h c", h=HEADS)
                    step(v.tensor_tensor(sums_of_node, sums_of_node,
                                         scales[:, :].unsqueeze(2).broadcast_to([P, HEADS, C]), ALU.mult))
                    step(v.tensor_tensor(node[:, D:WT], node[:, D:WT], scales[:, :], ALU.mult))
                    assert (lanes.steps, lanes.asks) == (LANE_STEPS, LANE_ASKS)

                def weigh(slot):
                    rows = G[:, slot, :, 0:D].rearrange("p k (h c) -> p k h c", h=HEADS)
                    w = WB[:, slot % BG * U:(slot % BG + 1) * U, :]
                    v.tensor_tensor(rows, rows, w.unsqueeze(3).broadcast_to([P, U, HEADS, C]), ALU.mult)\
                     .then_inc(SEM["rows_ready"], 1)

                class Adds:

                    def __init__(self, it, half):
                        self.it, self.half, self.tile, self.blocks = it, half, 0, None

                    def __call__(self, n):
                        for k in range(self.tile, self.tile + n):
                            group = BG * self.half + k // U
                            if k % U == 0:
                                self.blocks = blocks(8 * U * self.it + U * group, U, DVE)
                                dve.wait_ge(SEM["seg_done"], 8 * self.it + (t.base["seg_done"] + group + 1))
                            if k == 0:
                                dve.wait_ge(SEM["lane_step"], 2 * LANE_STEPS * self.it
                                            + (t.base["lane_step"] + LANE_STEPS * (self.half + 1)))
                            else:
                                dve.wait_ge(SEM["acc_step"], 8 * U * self.it + (t.base["acc_step"] + BT * self.half + k))
                            to = ACC[:, ds(self.blocks[k % U], 1), :].squeeze(1)
                            v.tensor_tensor(to, to, sums[group % 2][:, k % U // 4, k % 4 * WT:(k % 4 + 1) * WT], ALU.add)\
                             .then_inc(SEM["acc_step"], 1)
                        self.tile += n

                def batch(it, half, more=True):
                    tail(it, half)
                    adds = Adds(it, half)

                    def hot_next(q):
                        if more:
                            build_hot(BG * (1 - half) + q, 8 * U * it + U * (BG * (half + 1) + q))
                    weigh(BG * half)
                    weigh(BG * half + 1)
                    hot_next(0)
                    weigh(BG * half + 2)
                    hot_next(1)
                    adds(1)
                    weigh(BG * half + 3)
                    adds(1)
                    hot_next(2)
                    adds(1)
                    hot_next(3)
                    adds(5)
                    if more:
                        head(it + half, 1 - half, adds)
                    adds(BT - adds.tile)

                for q in range(BG):
                    build_hot(q, U * q)
                head(0, 0, lambda n: None)
                with dve.Fori(0, BATCHES // 2 - 1) as it:
                    batch(it, 0)
                    batch(it, 1)
                batch(BATCHES // 2 - 1, 0)
                batch(BATCHES // 2 - 1, 1, more=False)
                dve.wait_ge(SEM["acc_step"], t.end["acc_step"])
                link(v.tensor_scalar(ACC[:, :, D:WT], ACC[:, :, D:WT], 1e-16, None, ALU.add))
                link(v.reciprocal(ACC[:, :, D:WT], ACC[:, :, D:WT]))
                for h in range(HEADS):
                    part = ACC[:, :, h * C:(h + 1) * C]
                    link(v.tensor_tensor(part, part, ACC[:, :, D + h:D + h + 1].broadcast_to([P, NBP, C]), ALU.mult))
                link(v.tensor_tensor(ACCF, ACCF, over_blocks(row(R_GATB + l)), ALU.add))
                if l < LAYERS - 1:
                    link(v.tensor_scalar(H[:, :, :], ACCF, 0.0, None, ALU.max))
            v.scalar_tensor_tensor(X[:, :, :], ACCF, 0.0, X[:, :, :], ALU.max, ALU.add).then_inc(result_ready, 1)


_INS = ["x", "src", "dst", "edge_attr_32", "edge_attr_96", "L0_gnn_W1", "L0_gnn_b1", "L0_gnn_W2", "L0_gnn_b2",
        "L0_gnn_eps", "L1_gnn_We", "L1_gnn_be", "L1_gnn_W1", "L1_gnn_b1", "L1_gnn_W2", "L1_gnn_b2", "L1_gnn_gamma",
        "L1_gnn_beta", "L2_gnn_W_in", "L2_gnn_b_in", "L2_gnn_gcn_W", "L2_gnn_gcn_b", "L2_gnn_W_out", "L2_gnn_b_out",
        "L3_gnn_W", "L3_gnn_att_src", "L3_gnn_att_dst", "L3_gnn_bias"]


def kernel(**inputs):
    import numpy as _np
    import concourse.bacc as _bacc
    from concourse import mybir as _mybir
    from concourse.bass_utils import run_bass_kernel_spmd as _run

    nc = _bacc.Bacc("TRN2", target_bir_lowering=False, num_devices=1)
    arrays, args = {}, []
    for name in _INS:
        a = _np.ascontiguousarray(inputs[name])
        arrays[f"in_{name}_dram"] = a
        args.append(nc.dram_tensor(f"in_{name}_dram", a.shape, _mybir.dt.from_np(a.dtype), kind="ExternalInput").ap())
    shape = arrays["in_x_dram"].shape
    result = nc.dram_tensor("out_0_dram", shape, _mybir.dt.float32, kind="ExternalOutput").ap()
    gnn_kernel(nc, *args, result)
    r = _run(nc, [arrays], core_ids=[0])
    return r.results[0]["out_0_dram"]
```

```python
import concourse.bass as bass
from concourse import mybir
from contextlib import ExitStack


def gnn_kernel(nc, x, src, dst, edge_attr_32, edge_attr_96, L0_W1, L0_b1, L0_W2, L0_b2, L0_eps,
               L1_We, L1_be, L1_W1, L1_b1, L1_W2, L1_b2, L1_gamma, L1_beta,
               L2_W_in, L2_b_in, L2_gcn_W, L2_gcn_b, L2_W_out, L2_b_out,
               L3_W, L3_att_src, L3_att_dst, L3_bias, out):
    f32, i32, bf16 = mybir.dt.float32, mybir.dt.int32, mybir.dt.bfloat16
    ALU, ACT, AX = mybir.AluOpType, mybir.ActivationFunctionType, mybir.AxisListType
    DVE, PE, SP, ACTE = (mybir.EngineType.DVE, mybir.EngineType.PE, mybir.EngineType.SP,
                         mybir.EngineType.Activation)
    ds = bass.ds

    P = 128
    N, D = x.shape
    E = src.shape[0]
    DE = edge_attr_32.shape[1]
    LAYERS, HEADS, C = L3_att_src.shape
    WT = D + HEADS
    NB = -(-N // P)
    Q = 4
    NG = -(-NB // Q)
    NBP = NG * Q
    FULL = N // P
    REST = N - FULL * P
    U = 8
    BT = P // HEADS
    TILES = -(-(-(-E // P) + NB) // BT) * BT
    STEPS = -(-TILES // P) * P
    GROUPS = TILES // U
    ITERS = GROUPS // 2
    UN = 4
    ROUNDS = GROUPS // UN
    BATCHES = TILES // BT
    BG = BT // U
    BIG = 1.0e30
    LN_EPS = BN_EPS = 1e-5
    SLOPE = 0.2
    PARTS = 3
    EP = max(d for d in range(1, P + 1) if E % d == 0)
    EF = E // EP
    ET = -(-E // P)
    REM = E - (ET - 1) * P
    KC = -(-STEPS // P)
    assert BATCHES % 2 == 0 and GROUPS % UN == 0 and UN == BG == 4 and STEPS <= 4 * 512 and 0 < REM < P

    ctx = ExitStack()
    with ctx:
        def sb(name, shape, dt=f32):
            return ctx.enter_context(nc.sbuf_tensor("sb_" + name, shape, dt))

        def sem(name):
            return ctx.enter_context(nc.semaphore(name))

        def dram(name, shape, dt):
            return nc.dram_tensor(name, shape, dt, kind="Internal").ap()

        table = dram("feature_table", [NBP * P, D], f32)
        gat_table = dram("attention_table", [NBP * P, WT], f32)
        src_rows = dram("src_rows", [ET, P], i32)
        dst_rows = dram("dst_rows", [ET, P], i32)

        X = sb("X", [P, NBP, D])
        H = sb("H", [P, NBP, D])
        ACC = sb("ACC", [P, NBP, WT])
        CUT = sb("CUT", [P, BATCHES, P + 1], bf16)
        FORE = sb("FORE", [P, BATCHES, P + HEADS], bf16)
        AFT = sb("AFT", [P, BATCHES, P], bf16)
        JOIN = sb("JOIN", [1, BATCHES])
        IDX = sb("IDX", [P, STEPS], i32)
        REL = sb("REL", [P, STEPS], bf16)
        OUT = sb("OUT", [P, STEPS], bf16)
        EB = sb("EB", [65, STEPS], i32)
        HOT = sb("HOT", [P, 8, U, P])
        G = sb("G", [P, 8, U, WT])
        EA = sb("EA", [P, 2, U * D])
        NOW = sb("NOW", [P, 2, BT], i32)
        SB = sb("SB", [P, P])
        LW = sb("LW", [P, 4, P + HEADS])
        WB = sb("WB", [P, BT, HEADS])
        scales = sb("scales", [P, HEADS])
        cut_now = sb("cut_now", [P, P + 1], bf16)
        lone = sb("lone", [P, 8])
        iota_row = sb("iota_row", [P, P])
        iota_col = sb("iota_col", [P, 1])
        ident = sb("ident", [P, P])
        ones = sb("ones", [P, P])
        WTS = sb("WTS", [D, 14, D])
        WE = sb("WE", [P, P // DE, D])
        ROWS = sb("ROWS", [P, 7 + 4 * LAYERS, D])
        BCOL = sb("BCOL", [D, 3])
        DD = sb("DD", [P, NBP, HEADS])
        DDP = sb("DDP", [P, NBP, PARTS, HEADS], bf16)
        dinv = sb("dinv", [P, NBP])
        stat = sb("stat", [P, 2, NBP])
        epsp = sb("epsp", [P, 1])
        valid = sb("valid", [P, 1])
        plan = sb("plan", [P, 8])
        tiles_i = sb("tiles_i", [P, 3], i32)
        row_i = sb("row_i", [P, KC], i32)
        H_flat = H[:, :, :].rearrange("p b d -> p (b d)")
        ACC_flat = ACC[:, :, :].rearrange("p b d -> p (b d)")
        G_flat = G[:, :, :, :].rearrange("p s k d -> p (s k d)")
        HOT_flat = HOT[:, :, :, :].rearrange("p s k n -> p (s k n)")
        EA_flat = EA[:, :, :].rearrange("p a b -> p (a b)")
        ST = EA_flat[:, 0:U * P // 2].bitcast(bf16).rearrange("p (k e) -> p k e", k=U)
        DL = EA_flat[:, U * P // 2:U * P // 2 + 2 * PARTS * P].rearrange("p (b a) -> p b a", b=2)
        spare = 2 * STEPS
        zb, zT, hid = (G_flat[:, spare + n * 1024:spare + (n + 1) * 1024].rearrange("p (q a) -> p q a", q=2)
                       for n in range(3))
        assert NG % 2 == 1 and spare + 3 * 1024 <= 8 * U * WT and 4 * STEPS + P // BT * P <= 8 * U * P
        win_i = [H_flat[:, n * STEPS:(n + 1) * STEPS].bitcast(i32) for n in range(2)]
        win_f = [H_flat[:, 2 * STEPS:3 * STEPS], G_flat[:, 0:STEPS]]
        ind = dabs = ACC_flat[:, 0:STEPS]
        first = ACC_flat[:, STEPS:2 * STEPS]
        keep = ACC_flat[:, 2 * STEPS:3 * STEPS]
        block_of = G_flat[:, STEPS:2 * STEPS]
        begins, ends, chained = (H_flat[:, n * STEPS:(n + 1) * STEPS] for n in range(3))
        starts = HOT_flat[:, 0:STEPS]
        by_tile = HOT_flat[:, STEPS:STEPS + TILES].rearrange("p (b t) -> p b t", t=BT)
        by_tile16 = HOT_flat[:, 2 * STEPS:3 * STEPS].bitcast(bf16)[:, 0:TILES].rearrange("p (b t) -> p b t", t=BT)
        lane_of = HOT_flat[:, 4 * STEPS:4 * STEPS + P // BT * P].rearrange("p (q l) -> p q l", l=P)
        iota_k = HOT_flat[:, 3 * STEPS:4 * STEPS]
        dst_i = HOT_flat[0:EP, 0:EF].bitcast(i32)
        dst_block = HOT_flat[0:EP, EF:2 * EF].bitcast(bf16)[:, 0:EF]
        upper = HOT_flat[0:NB, 2 * EF:2 * EF + P][:, 0:NB]
        step_of = HOT_flat[0:NB, 2 * EF + P:2 * EF + 2 * P][:, 0:NB]
        edge_dv = HOT_flat[0:NB, 2 * EF + 2 * P:2 * EF + 3 * P]
        cnt = HOT_flat[:, 2 * EF + 3 * P:2 * EF + 3 * P + NB + 1]
        assert 2 * EF + 4 * P <= 3 * STEPS and NB < P
        less = ACC_flat[0:EP, 0:EF].bitcast(bf16)[:, 0:EF]
        ACCF = ACC[:, :, 0:D]
        SB3 = SB[:, :].rearrange("p (t h) -> p t h", h=HEADS)
        lane_no = EA_flat[:, 0:2 * P].bitcast(i32)
        edge_of = EA_flat[:, 2 * P:3 * P]

        sums = [ctx.enter_context(nc.psum_tensor(f"sums{j}", [P, 2, 512], f32)) for j in range(2)]
        psA, psB, psC, psD = (ctx.enter_context(nc.psum_tensor(f"ps{c}", [P, 512], f32)) for c in "ABCD")

        def row(n):
            return ROWS[:, n:n + 1, :]
        R_L0B2, R_BE, R_L1B2, R_GAMMA, R_BETA, R_BIN, R_BOUT = range(7)
        R_GCNB, R_GATB, R_ASRC, R_ADST = 7, 7 + LAYERS, 7 + 2 * LAYERS, 7 + 3 * LAYERS
        W_L0A, W_L0B, W_L0C, W_L0D, W_L11, W_L12, W_IN, W_GCN, W_OUT = 0, 1, 2, 3, 4, 5, 6, 7, 10
        W_GAT = 11
        TURNED = [W_IN, W_GCN, W_GCN + 1, W_GCN + 2, W_OUT]

        x_in, dst_in, const_in, weights_in = sem("x_in"), sem("dst_in"), sem("const_in"), sem("weights_in")
        iota_done, consts_done = sem("iota_done"), sem("consts_done")
        setup_operand, setup_product = sem("setup_operand"), sem("setup_product")
        plan_ready = sem("plan_ready")
        rows_in, windows_in = sem("rows_in"), sem("windows_in")
        chain = sem("chain")
        var_ready, root_ready = sem("var_ready"), sem("root_ready")
        table_ready, table_stored = sem("table_ready"), sem("table_stored")
        feature_sums, feature_totals = sem("feature_sums"), sem("feature_totals")
        lane_no_ready = sem("lane_no_ready")
        idx_seen = sem("idx_seen")
        cuts_product, cuts_copied = sem("cuts_product"), sem("cuts_copied")
        CUTS = [(q, c) for q in range(P // BT) for c in range(0, KC, 4)]
        result_ready, out_done = sem("result_ready"), sem("out_done")

        NAMES = ["idx_ready", "attr_in0", "attr_in1", "hot_built", "rows_ready",
                 "seg_done", "acc_step", "ea_flipped", "ea_lifted", "ea_product", "summed",
                 "hot_read", "st_ready", "d_product", "d_copied",
                 "lane_step", "lane_ask", "lane_reply", "exponent", "exp_made",
                 "prepared", "staged", "flipped", "lifted", "hid_product", "hid_ready", "made", "taken", "scored", "hop_step"]
        SEM = {n: sem(n) for n in NAMES}
        START = {"seg_done": 8, "acc_step": 2 * U, "flipped": 2, "made": 2} | {n: 1 for n in (
            "lifted", "taken", "hid_ready", "ea_lifted", "summed", "st_ready", "d_product",
            "d_copied")}
        LANE_STEPS, LANE_ASKS = 22, 5
        HEAD_STEPS, HEAD_ASKS = 11, 4
        gather = {"idx_ready": GROUPS // 2}
        segment = {"hot_built": GROUPS, "seg_done": GROUPS, "acc_step": TILES}
        attrs = {"attr_in0": ITERS * U * 16, "attr_in1": ITERS * U * 16, "rows_ready": GROUPS}
        dense = {n: NG for n in ("prepared", "staged", "flipped", "lifted", "made", "taken")}
        MOVES = {
            "sum_attr": gather | segment | attrs,
            "sum_relu": gather | segment | attrs | {"ea_flipped": GROUPS, "ea_lifted": GROUPS,
                                                    "ea_product": 2 * GROUPS, "summed": 2 * GROUPS},
            "sum": gather | segment,
            "attend": segment | {"idx_ready": BATCHES, "rows_ready": GROUPS, "lane_step": LANE_STEPS * BATCHES,
                                 "lane_ask": LANE_ASKS * BATCHES, "lane_reply": LANE_ASKS * BATCHES,
                                 "exponent": 2 * BATCHES, "exp_made": 2 * BATCHES}
                      | {n: GROUPS for n in ("hot_read", "st_ready", "d_product", "d_copied")},
            "dense": dense,
            "scores": dense | {"scored": NG},
            "hop": dense | {"hop_step": 2 * NG},
            "mlp1": dense | {"hid_product": NG, "hid_ready": NG},
            "mlp2": dense | {"hid_product": 2 * NG, "hid_ready": 2 * NG},
        }
        PLAN = [("L0", "sum_attr"), ("L0mlp", "mlp2"), ("L1", "sum_relu"),
                ("L1mlp", "mlp1"), ("in", "dense")]
        for l in range(LAYERS):
            PLAN += [(f"gcn{l}", "hop" if l else "dense"), (f"gcnsum{l}", "sum")]
        PLAN += [("out", "hop")]
        for l in range(LAYERS):
            PLAN += [(f"gat{l}", "scores"), (f"attend{l}", "attend")]

        STORED = [16, 32] + [32 + 16 * NG * (n + 1) for n in range(2 * LAYERS)]

        AHEAD = 3
        assert (NG - AHEAD) % 2 == 0

        def in_pairs(engine, body):
            with engine.Fori(0, NG // 2) as pair:
                body(2 * pair, 0)
                body(2 * pair + 1, 1)
            body(NG - 1, 0)

        GATHERED = {name: [sem(f"gathered{slot}_{name}") for slot in range(UN if kind != "attend" else 8)]
                    for name, kind in PLAN if "idx_ready" in MOVES[kind]}

        class Stage:
            def __init__(self, name):
                n = [a for a, _ in PLAN].index(name)
                self.base = {s: START.get(s, 0) + sum(MOVES[k].get(s, 0) for _, k in PLAN[:n]) for s in NAMES}
                self.gathered = GATHERED.get(name)
                self.end = {s: self.base[s] + MOVES[PLAN[n][1]].get(s, 0) for s in NAMES}

        def freed(t, slots):
            return t.base["seg_done"] - slots

        def firsts(k, n, engine):
            return nc.values_load_multi_w_load_instructions(
                EB[32:33, ds(k, n)], engines=(engine,), min_val=0, max_val=E - P,
                skip_runtime_bounds_check_because="the plan clips them")[1]

        def blocks(k, n, engine):
            return nc.values_load_multi_w_load_instructions(
                EB[64:65, ds(k, n)], engines=(engine,), min_val=0, max_val=NB - 1,
                skip_runtime_bounds_check_because="the plan clips them")[1]

        block = ctx.enter_context(nc.Block())

        @block.sync
        def _(sp):
            for to, of in ((src_rows, src), (dst_rows, dst)):
                sp.dma_start(to[0:ET - 1, :], of[0:(ET - 1) * P].rearrange("(r e) -> r e", e=P)).then_inc(rows_in, 16)
            sp.dma_start(src_rows[ET - 1:ET, :], src[E - P:E].unsqueeze(0)).then_inc(rows_in, 16)
            sp.dma_start(dst_rows[ET - 1:ET, P - REM:P], dst[E - REM:E].unsqueeze(0)).then_inc(rows_in, 16)
            with nc.allow_non_contiguous_dma(reason="one number, repeated"):
                sp.dma_start(dst_rows[ET - 1, 0:P - REM].unsqueeze(1),
                             dst[E - REM:E - REM + 1].partition_broadcast(P - REM)).then_inc(rows_in, 16)
            sp.dma_start(dst_i, dst.rearrange("(p f) -> p f", p=EP)).then_inc(dst_in, 16)
            sp.dma_start(X[:, 0:FULL, :], x[0:FULL * P, :].rearrange("(b p) d -> p b d", p=P)).then_inc(x_in, 16)
            sp.wait_ge(consts_done, 2)
            sp.dma_start(X[0:REST, FULL, :], x[FULL * P:N, :]).then_inc(x_in, 16)
            vectors = [(R_L0B2, L0_b2), (R_BE, L1_be), (R_L1B2, L1_b2), (R_GAMMA, L1_gamma),
                       (R_BETA, L1_beta), (R_BIN, L2_b_in), (R_BOUT, L2_b_out)]
            for n, v in vectors:
                sp.dma_start(ROWS[:, n, :], v.partition_broadcast(P)).then_inc(const_in, 16)
            for n, m in [(R_GCNB, L2_gcn_b), (R_GATB, L3_bias),
                         (R_ASRC, L3_att_src.rearrange("l h c -> l (h c)")),
                         (R_ADST, L3_att_dst.rearrange("l h c -> l (h c)"))]:
                sp.dma_start(ROWS[:, n:n + LAYERS, :], m.partition_broadcast(P)).then_inc(const_in, 16)
            sp.dma_start(epsp[:, :], L0_eps.partition_broadcast(P)).then_inc(const_in, 16)
            with nc.allow_non_contiguous_dma(reason="three short columns"):
                sp.dma_start(BCOL[:, 0:2], L0_b1.rearrange("(q d) -> d q", q=2)).then_inc(const_in, 16)
                sp.dma_start(BCOL[:, 2:3], L1_b1.rearrange("(d a) -> d a", a=1)).then_inc(const_in, 16)
            sp.dma_start(WTS[:, W_L0A:W_L0B + 1, :], L0_W1.rearrange("k (q n) -> k q n", q=2)).then_inc(weights_in, 16)
            sp.dma_start(WTS[:, W_L0C:W_L0D + 1, :], L0_W2.rearrange("(q k) n -> k q n", q=2)).then_inc(weights_in, 16)
            sp.dma_start(WTS[:, W_L11, :], L1_W1).then_inc(weights_in, 16)
            sp.dma_start(WTS[:, W_L12, :], L1_W2).then_inc(weights_in, 16)
            sp.dma_start(WTS[:, W_IN, :], L2_W_in).then_inc(weights_in, 16)
            sp.dma_start(WTS[:, W_GCN:W_GCN + LAYERS, :], L2_gcn_W.rearrange("l a b -> a l b")).then_inc(weights_in, 16)
            sp.dma_start(WTS[:, W_OUT, :], L2_W_out).then_inc(weights_in, 16)
            sp.dma_start(WTS[:, W_GAT:W_GAT + LAYERS, :], L3_W.rearrange("l a b -> a l b")).then_inc(weights_in, 16)
            for r in range(P // DE):
                sp.dma_start(WE[r * DE:(r + 1) * DE, r, :], L1_We).then_inc(weights_in, 16)

            tables = [0]

            def store_table(to, of):
                tables[0] += 1
                sp.wait_ge(table_ready, tables[0])
                sp.dma_start(to.rearrange("(b p) d -> p b d", p=P), of).then_inc(table_stored, 16)

            def store_groups(t, to, of):
                by_block = to.rearrange("(b p) d -> p b d", p=P)
                with sp.Fori(0, NG) as g:
                    sp.wait_ge(SEM["taken"], g + (t.base["taken"] + 1))
                    sp.dma_start(by_block[:, ds(Q * g, Q), :], of[:, ds(Q * g, Q), :]).then_inc(table_stored, 16)

            def load_attrs(t, attr, width, freed):
                at, name = t.base[freed], SEM[freed]
                for half in range(2):
                    e = firsts(half * U, U, SP)
                    for n in range(U):
                        sp.dma_start(EA[:, half, n * width:(n + 1) * width],
                                     attr[ds(e[n], P), :]).then_inc(SEM[f"attr_in{half}"], 16)
                with sp.Fori(1, ITERS) as it:
                    e = firsts(2 * U * it, 2 * U, SP)
                    for half in range(2):
                        sp.wait_ge(name, 2 * it + (at + half - 1))
                        for n in range(U):
                            sp.dma_start(EA[:, half, n * width:(n + 1) * width],
                                         attr[ds(e[half * U + n], P), :]).then_inc(SEM[f"attr_in{half}"], 16)

            store_table(table, H[:, :, :])
            load_attrs(Stage("L0"), edge_attr_96, D, "rows_ready")
            store_table(table, ACCF)
            sp.wait_ge(table_stored, STORED[1])
            load_attrs(Stage("L1"), edge_attr_32, DE, "ea_flipped")
            for l in range(LAYERS):
                store_groups(Stage(f"gcn{l}"), table, ACCF)
            for l in range(LAYERS):
                store_groups(Stage(f"gat{l}"), gat_table, ACC)
            sp.wait_ge(result_ready, 1)
            sp.dma_start(out[0:FULL * P, :].rearrange("(b p) d -> p b d", p=P), X[:, 0:FULL, :]).then_inc(out_done, 16)
            sp.dma_start(out[FULL * P:N, :], X[0:REST, FULL, :]).then_inc(out_done, 16)
            sp.wait_ge(out_done, 32)

        @block.gpsimd
        def _(pool):
            nc.gpsimd.iota(iota_row[:, :], [[1, P]], base=0, channel_multiplier=0,
                           allow_small_or_imprecise_dtypes=True).then_inc(iota_done, 1)
            nc.gpsimd.iota(iota_col[:, :], [[0, 1]], base=0, channel_multiplier=1,
                           allow_small_or_imprecise_dtypes=True).then_inc(iota_done, 1)
            nc.gpsimd.iota(lane_no[:, 0:P], [[1, P]], base=0, channel_multiplier=0).then_inc(lane_no_ready, 1)
            nc.gpsimd.iota(lane_no[:, P:P + 1], [[0, 1]], base=0, channel_multiplier=1).then_inc(lane_no_ready, 1)
            nc.gpsimd.iota(iota_k, [[1, STEPS]], base=0, channel_multiplier=0,
                           allow_small_or_imprecise_dtypes=True).then_inc(iota_done, 1)

            pool.wait_ge(rows_in, 5 * 16)
            pool.wait_ge(plan_ready, 2)
            for n, rows in enumerate((src_rows, dst_rows)):
                for c in range(KC):
                    pool.indirect_dma_start(win_i[n][:, c * P:(c + 1) * P], None, rows,
                                            bass.IndirectOffsetOnAxis(ap=row_i[:, c:c + 1], axis=0)).then_inc(windows_in, 16)

            def row_of(to, index, rows, landed):
                pool.indirect_dma_start(to, None, rows, bass.IndirectOffsetOnAxis(ap=index, axis=0)).then_inc(landed, 16)

            def sums_of(t):
                with pool.Fori(0, ROUNDS) as it:
                    for pair in range(UN // 2):
                        pool.wait_ge(SEM["idx_ready"], UN // 2 * it + (t.base["idx_ready"] + pair + 1))
                        pool.sem_inc(idx_seen, 1)
                        for n in range(2 * U):
                            slot = 2 * pair + n // U
                            row_of(G[:, slot, n % U, 0:D], NOW[:, pair, n:n + 1], table, t.gathered[slot])

            def attention_rows(t):
                with pool.Fori(0, BATCHES // 2) as it:
                    for half in range(2):
                        for q in range(BG):
                            pool.wait_ge(SEM["seg_done"], 8 * it + (freed(t, 8) + BG * half + q + 1))
                            if q == 0:
                                pool.wait_ge(SEM["idx_ready"], 2 * it + (t.base["idx_ready"] + half + 1))
                            pool.sem_inc(idx_seen, 1)
                            for n in range(U):
                                row_of(G[:, BG * half + q, n, :], NOW[:, half, q * U + n:q * U + n + 1], gat_table,
                                       t.gathered[BG * half + q])

            def stored(n):
                pool.wait_ge(table_stored, STORED[n])

            def stage_blocks(t, z):
                def stage(g, half):
                    pool.wait_ge(SEM["prepared"], g + (t.base["prepared"] + 1))
                    pool.wait_ge(SEM["flipped"], g + (t.base["flipped"] - 1))
                    pool.tensor_copy(zb[:, half, 0:Q * D].rearrange("p (b d) -> p b d", b=Q),
                                     z[:, ds(Q * g, Q), 0:D]).then_inc(SEM["staged"], 1)
                in_pairs(pool, stage)

            stored(0)
            sums_of(Stage("L0"))
            stage_blocks(Stage("L0mlp"), ACC)
            stored(1)
            sums_of(Stage("L1"))
            stage_blocks(Stage("L1mlp"), ACC)
            stage_blocks(Stage("in"), H)
            for l in range(LAYERS):
                stage_blocks(Stage(f"gcn{l}"), H)
                stored(2 + l)
                sums_of(Stage(f"gcnsum{l}"))
            stage_blocks(Stage("out"), H)
            for l in range(LAYERS):
                stage_blocks(Stage(f"gat{l}"), H)
                stored(2 + LAYERS + l)
                attention_rows(Stage(f"attend{l}"))

        @block.scalar
        def _(act):
            roots = [0]

            def root(to, of):
                roots[0] += 1
                act.wait_ge(var_ready, roots[0])
                nc.scalar.activation(to, of, ACT.Sqrt).then_inc(root_ready, 1)

            def lift(t):
                def copy(g, half):
                    act.wait_ge(SEM["flipped"], g + (t.base["flipped"] + 1))
                    act.wait_ge(SEM["made"], g + (t.base["made"] - 1))
                    nc.scalar.activation(zT[0:D, half, :], psA[0:D, :], ACT.Copy).then_inc(SEM["lifted"], 1)
                in_pairs(act, copy)

            def lift_mlp(t, halves, bias):
                def copy(g, half):
                    act.wait_ge(SEM["flipped"], g + (t.base["flipped"] + 1))
                    nc.scalar.activation(zT[0:D, half, :], psA[0:D, :], ACT.Copy).then_inc(SEM["lifted"], 1)
                    for q in range(halves):
                        act.wait_ge(SEM["hid_product"], halves * g + (t.base["hid_product"] + q + 1))
                        nc.scalar.activation(hid[0:D, q, :], (psB, psC)[q][0:D, :], ACT.Relu,
                                             bias=BCOL[:, bias + q:bias + q + 1]).then_inc(SEM["hid_ready"], 1)
                in_pairs(act, copy)

            for n, (q, c) in enumerate(CUTS):
                act.wait_ge(cuts_product, n + 1)
                to = CUT[:, 4 * c + q:min(4 * (c + 4), BATCHES):4, 0:P]
                nc.scalar.activation(to, (psA, psB, psC, psD)[n % 4][:, 0:to.shape[1] * P].rearrange("p (b e) -> p b e", e=P),
                                     ACT.Copy, scale=-BIG).then_inc(cuts_copied, 1)
            root(stat[:, 1, :], stat[:, 0, :])
            root(dinv[:, :], dinv[:, :])
            act.wait_ge(const_in, 14 * 16)
            lift_mlp(Stage("L0mlp"), 2, 0)
            root(stat[:, 1, :], stat[:, 0, :])

            t = Stage("L1")

            def lift_attrs(half, at):
                act.wait_ge(SEM["ea_flipped"], at)
                nc.scalar.activation(EA[:, half, U * DE:U * DE + 2 * P], psA[:, 0:2 * P], ACT.Copy)\
                  .then_inc(SEM["ea_lifted"], 1)

            def relu(half, at):
                act.wait_ge(SEM["summed"], at)
                nc.scalar.activation(G[:, half, :, 0:D], G[:, half, :, 0:D], ACT.Relu).then_inc(SEM["rows_ready"], 1)

            lift_attrs(0, t.base["ea_flipped"] + 1)

            def attr_round(it, slots):
                for j in slots:
                    lift_attrs((j + 1) % 2, UN * it + (t.base["ea_flipped"] + j + 2))
                    relu(j, 2 * UN * it + (t.base["summed"] + 2 * j + 2))

            with act.Fori(0, ROUNDS - 1) as it:
                attr_round(it, range(UN))
            attr_round(ROUNDS - 1, range(UN - 1))
            relu(UN - 1, t.end["summed"])

            lift_mlp(Stage("L1mlp"), 1, 2)
            root(HOT[:, 0, 1, 0:D], HOT[:, 0, 1, 0:D])
            for name in ["in"] + [f"gcn{l}" for l in range(LAYERS)] + ["out"]:
                if name == "in":
                    root(stat[:, 1, :], stat[:, 0, :])
                lift(Stage(name))
            root(stat[:, 1, :], stat[:, 0, :])
            for l in range(LAYERS):
                lift(Stage(f"gat{l}"))
                t = Stage(f"attend{l}")

                def logits(slot, it, n):
                    act.wait_ge(SEM["hot_read"], 8 * it + (t.base["hot_read"] + n + 1))
                    act.wait_ge(SEM["d_product"], 8 * it + (t.base["d_product"] + n))
                    nc.scalar.activation(ST[:, 0:4, :], psA[:, :].rearrange("p (a b) -> p a b", a=4), ACT.Copy)
                    nc.scalar.activation(ST[:, 4:8, :], psB[:, :].rearrange("p (a b) -> p a b", a=4), ACT.Copy)\
                      .then_inc(SEM["st_ready"], 1)
                    act.wait_ge(SEM["d_product"], 8 * it + (t.base["d_product"] + n + 1))
                    part = U * PARTS * HEADS
                    nc.scalar.activation(DL[:, slot // BG, slot % BG * part:(slot % BG + 1) * part],
                                         psC[:, 0:part], ACT.Copy).then_inc(SEM["d_copied"], 1)

                def exps(half, it):
                    act.wait_ge(SEM["exponent"], 4 * it + (t.base["exponent"] + 2 * half + 1))
                    nc.scalar.activation(WB[:, :, :], SB3, ACT.Exp)
                    nc.scalar.activation(G[:, BG * half:BG * (half + 1), :, D:WT].rearrange("p s k h -> p (s k) h"),
                                         SB3, ACT.Exp).then_inc(SEM["exp_made"], 1)
                    act.wait_ge(SEM["exponent"], 4 * it + (t.base["exponent"] + 2 * half + 2))
                    nc.scalar.activation(lone[0:1, 4:8], lone[0:1, 4:8], ACT.Exp).then_inc(SEM["exp_made"], 1)

                for q in range(BG):
                    logits(q, 0, q)

                def batch(it, half, more=True):
                    exps(half, it)
                    for q in range(BG if more else 0):
                        logits(BG * (1 - half) + q, it, BG * (half + 1) + q)

                with act.Fori(0, BATCHES // 2 - 1) as it:
                    batch(it, 0)
                    batch(it, 1)
                batch(BATCHES // 2 - 1, 0)
                batch(BATCHES // 2 - 1, 1, more=False)

        @block.tensor
        def _(pe):
            for name, value in START.items():
                if name != "acc_step":
                    pe.sem_inc(SEM[name], value)
            given = [0]

            def give(ins):
                given[0] += 1
                ins.then_inc(setup_product, 1)
            pe.wait_ge(setup_operand, 1)
            nc.tensor.matmul(psA[0:NB, 0:1], cnt[0:EP, 0:NB], ones[0:EP, 0:1], start=True, stop=True)
            give(nc.tensor.matmul(psA[0:NB, 1:2], cnt[0:EP, 1:NB + 1], ones[0:EP, 0:1], start=True, stop=True))
            pe.wait_ge(setup_operand, 2)
            give(nc.tensor.matmul(psA[0:NB, 2:3], upper[:, :], plan[0:NB, 3:4], start=True, stop=True))
            pe.wait_ge(setup_operand, 3)
            give(nc.tensor.matmul(psA[0:NB, 3:4], step_of[:, :], plan[0:NB, 5:6], start=True, stop=True))
            pe.wait_ge(setup_operand, 4)
            quarter = STEPS // 4
            for c in range(4):
                part = ind[0:NB, c * quarter:(c + 1) * quarter]
                nc.tensor.matmul(sums[c // 2][:, c % 2, 0:quarter], edge_dv[:, :], part, start=True, stop=True)
                last = nc.tensor.matmul((psA, psB, psC, psD)[c][:, 0:quarter], ones[0:NB, :], part, start=True, stop=True)
            give(last)
            pe.wait_ge(setup_operand, 5)
            pe.wait_ge(weights_in, (8 + P // DE) * 16)
            for n, w in enumerate(TURNED):
                last = nc.tensor.transpose(psA[0:D, n * D:(n + 1) * D], WTS[:, w, :], ident[0:D, 0:D])
            give(last)
            pe.wait_ge(setup_operand, 6)
            for c in range(KC):
                part = slice(c % 4 * P, (c % 4 + 1) * P)
                nc.tensor.transpose(sums[c // 8][:, c // 4 % 2, part], win_f[0][:, c * P:(c + 1) * P], ident[:, :])
                last = nc.tensor.transpose((psA, psB, psC, psD)[c // 4][:, part], win_f[1][:, c * P:(c + 1) * P], ident[:, :])
            give(last)
            for n in range(2):
                pe.wait_ge(setup_operand, 7 + n)
                for c in range(4):
                    last = nc.tensor.matmul(sums[c // 2][:, c % 2, 0:quarter], edge_of[:, :],
                                            dabs[:, c * quarter:(c + 1) * quarter], start=True, stop=True)
                give(last)
            for n, (q, c) in enumerate(CUTS):
                if n >= 4:
                    pe.wait_ge(cuts_copied, n - 3)
                width = min(4, KC - c) * P
                nc.tensor.matmul((psA, psB, psC, psD)[n % 4][:, 0:width], lane_of[:, q, :],
                                 starts[:, c * P:c * P + width], start=True, stop=True).then_inc(cuts_product, 1)
            pe.wait_ge(cuts_copied, len(CUTS))

            def flip_blocks(t, g, half):
                pe.wait_ge(SEM["staged"], g + (t.base["staged"] + 1))
                pe.wait_ge(SEM["lifted"], g + t.base["lifted"])
                for q in range(Q):
                    last = nc.tensor.transpose(psA[0:D, q * P:(q + 1) * P], zb[:, half, q * D:(q + 1) * D], ident[:, :])
                last.then_inc(SEM["flipped"], 1)

            def dense_stage(t, w):
                def product(g, half):
                    pe.wait_ge(SEM["lifted"], g + (t.base["lifted"] + 1))
                    pe.wait_ge(SEM["taken"], g + (t.base["taken"] - 1))
                    for q in range(Q):
                        last = nc.tensor.matmul((psD, psC)[half][:, q * D:(q + 1) * D],
                                                zT[0:D, half, q * P:(q + 1) * P], WTS[:, w, :], start=True, stop=True)
                    last.then_inc(SEM["made"], 1)
                flip_blocks(t, 0, 0)
                with pe.Fori(0, NG // 2) as pair:
                    for half in range(2):
                        flip_blocks(t, 2 * pair + half + 1, 1 - half)
                        product(2 * pair + half, half)
                product(NG - 1, 0)

            def mlp_stage(t, halves, w1, w2):
                def hidden(g, half):
                    pe.wait_ge(SEM["lifted"], g + (t.base["lifted"] + 1))
                    pe.wait_ge(SEM["hid_ready"], halves * g + t.base["hid_ready"])
                    for h in range(halves):
                        nc.tensor.matmul((psB, psC)[h][0:D, :], WTS[:, w1 + h, :], zT[0:D, half, :],
                                         start=True, stop=True).then_inc(SEM["hid_product"], 1)

                def product(g):
                    pe.wait_ge(SEM["hid_ready"], halves * g + (t.base["hid_ready"] + halves))
                    pe.wait_ge(SEM["taken"], g + t.base["taken"])
                    for q in range(Q):
                        for h in range(halves):
                            last = nc.tensor.matmul(psD[:, q * D:(q + 1) * D], hid[0:D, h, q * P:(q + 1) * P],
                                                    WTS[:, w2 + h, :], start=(h == 0), stop=(h == halves - 1))
                    last.then_inc(SEM["made"], 1)
                flip_blocks(t, 0, 0)
                with pe.Fori(0, NG // 2) as pair:
                    for half in range(2):
                        hidden(2 * pair + half, half)
                        flip_blocks(t, 2 * pair + half + 1, 1 - half)
                        product(2 * pair + half)
                hidden(NG - 1, 0)
                product(NG - 1)

            def segment_group(t, it, unroll, n, hot, slot, width):
                bank = sums[n % 2]
                pe.wait_ge(SEM["acc_step"], unroll * U * it + (t.base["acc_step"] + U * (n - 1)))
                for k in range(U):
                    last = nc.tensor.matmul(bank[:, k // 4, k % 4 * width:(k % 4 + 1) * width],
                                            HOT[:, hot, k, :], G[:, slot, k, 0:width], start=True, stop=True)
                last.then_inc(SEM["seg_done"], 1)

            def sum_stage(t, width, gathered=False):
                with pe.Fori(0, ROUNDS) as it:
                    for j in range(UN):
                        pe.wait_ge(SEM["hot_built"], UN * it + (t.base["hot_built"] + j + 1))
                        if gathered:
                            pe.wait_ge(t.gathered[j], 16 * U * it + 16 * U)
                        else:
                            pe.wait_ge(SEM["rows_ready"], UN * it + (t.base["rows_ready"] + j + 1))
                        segment_group(t, it, UN, j, j % 2, j, width)

            sum_stage(Stage("L0"), D + 1)
            mlp_stage(Stage("L0mlp"), 2, W_L0A, W_L0C)

            t = Stage("L1")

            def attr_product(half, attr_at, g1, g0):
                pe.wait_ge(SEM[f"attr_in{half}"], attr_at)
                pe.wait_ge(SEM["ea_lifted"], t.base["ea_lifted"] + g0)
                for q in range(2):
                    last = nc.tensor.transpose(psA[:, q * P:(q + 1) * P], EA[:, half, q * P:(q + 1) * P], ident[:, :])
                last.then_inc(SEM["ea_flipped"], 1)
                pe.wait_ge(SEM["ea_lifted"], t.base["ea_lifted"] + g1)
                pe.wait_ge(SEM["summed"], t.base["summed"] + g0 * 2)
                for q in range(2):
                    nc.tensor.matmul((psB, psC)[q][:, 0:4 * D], EA[:, half, U * DE + q * P:U * DE + (q + 1) * P],
                                     WE[:, :, :].rearrange("p a b -> p (a b)"), start=True, stop=True)\
                      .then_inc(SEM["ea_product"], 1)

            def attr_round(it, slots):
                for j in slots:
                    nxt = j + 1
                    attr_product(nxt % 2, 16 * U * UN // 2 * it + (t.base[f"attr_in{nxt % 2}"] + 16 * U * (nxt // 2 + 1)),
                                 UN * it + nxt + 1, UN * it + nxt)
                    relu_sum(it, j)

            def relu_sum(it, j):
                pe.wait_ge(SEM["hot_built"], UN * it + (t.base["hot_built"] + j + 1))
                pe.wait_ge(SEM["rows_ready"], UN * it + (t.base["rows_ready"] + j + 1))
                segment_group(t, it, UN, j, j % 2, j, D)

            attr_product(0, t.base["attr_in0"] + 16 * U, 1, 0)
            with pe.Fori(0, ROUNDS - 1) as it:
                attr_round(it, range(UN))
            attr_round(ROUNDS - 1, range(UN - 1))
            relu_sum(ROUNDS - 1, UN - 1)

            mlp_stage(Stage("L1mlp"), 1, W_L11, W_L12)
            for n in range(2):
                pe.wait_ge(feature_sums, 1 + n)
                nc.tensor.matmul(psB[:, n * D:(n + 1) * D], ones[:, :], HOT[:, 0, n, 0:D],
                                 start=True, stop=True).then_inc(feature_totals, 1)
            dense_stage(Stage("in"), W_IN)
            for l in range(LAYERS):
                dense_stage(Stage(f"gcn{l}"), W_GCN + l)
                sum_stage(Stage(f"gcnsum{l}"), D, gathered=True)
            dense_stage(Stage("out"), W_OUT)
            for l in range(LAYERS):
                dense_stage(Stage(f"gat{l}"), W_GAT + l)
                t2 = Stage(f"attend{l}")

                def flip_hot(slot, it, n):
                    pe.wait_ge(SEM["hot_built"], 8 * it + (t2.base["hot_built"] + n + 1))
                    pe.wait_ge(SEM["st_ready"], 8 * it + (t2.base["st_ready"] + n))
                    for k in range(U):
                        last = nc.tensor.transpose((psA, psB)[k // 4][:, k % 4 * P:(k % 4 + 1) * P],
                                                   HOT[:, slot, k, :], ident[:, :])
                    last.then_inc(SEM["hot_read"], 1)

                def logits(it, n):
                    b = blocks(8 * U * it + U * n, U, PE)
                    pe.wait_ge(SEM["st_ready"], 8 * it + (t2.base["st_ready"] + n + 1))
                    pe.wait_ge(SEM["d_copied"], 8 * it + (t2.base["d_copied"] + n))
                    part = PARTS * HEADS
                    for k in range(U):
                        last = nc.tensor.matmul(psC[:, k * part:(k + 1) * part], ST[:, k, :],
                                                DDP[:, ds(b[k], 1), :, :].rearrange("p b s h -> p (b s h)"),
                                                start=True, stop=True)
                    last.then_inc(SEM["d_product"], 1)

                def reply(it, half, n):
                    pe.wait_ge(SEM["lane_ask"], 2 * LANE_ASKS * it + (t2.base["lane_ask"] + LANE_ASKS * half + n + 1))
                    if n == 0:
                        last = nc.tensor.transpose(psD[:, 0:P], SB[:, :], ident[:, :])
                    elif n == 1:
                        last = nc.tensor.matmul(psD[:, P:2 * P + HEADS], ones[:, :], LW[:, 2, :], start=True, stop=True)
                    elif n == 2:
                        last = nc.tensor.matmul(psD[:, P:2 * P], ones[:, :], LW[:, 2, 0:P], start=True, stop=True)
                    elif n == 3:
                        last = nc.tensor.transpose(psD[:, 2 * P:3 * P], LW[:, 0, 0:P], ident[:, :])
                    else:
                        last = nc.tensor.matmul(psD[:, 3 * P:3 * P + HEADS], HOT[0:1, BG * half, 0, :],
                                                lone[0:1, 4:8], start=True, stop=True)
                    last.then_inc(SEM["lane_reply"], 1)

                for q in range(BG):
                    flip_hot(q, 0, q)
                    logits(0, q)
                for n in range(HEAD_ASKS):
                    reply(0, 0, n)

                def batch(it, half, more=True):
                    nxt, other = (it + half, 1 - half) if more else (None, None)

                    def add_edges(q):
                        n = BG * half + q
                        pe.wait_ge(SEM["rows_ready"], 8 * it + (t2.base["rows_ready"] + n + 1))
                        segment_group(t2, it, 8, n, n, n, WT)

                    def flip_next(q):
                        if more:
                            flip_hot(BG * other + q, it, BG * (half + 1) + q)

                    def logits_next(q):
                        if more:
                            logits(it, BG * (half + 1) + q)

                    def reply_next(n):
                        if more:
                            reply(nxt, other, n)

                    reply(it, half, HEAD_ASKS)
                    add_edges(0)
                    flip_next(0)
                    add_edges(1)
                    logits_next(0)
                    flip_next(1)
                    reply_next(0)
                    add_edges(2)
                    logits_next(1)
                    flip_next(2)
                    reply_next(1)
                    reply_next(2)
                    add_edges(3)
                    logits_next(2)
                    flip_next(3)
                    reply_next(3)
                    logits_next(3)

                with pe.Fori(0, BATCHES // 2 - 1) as it:
                    batch(it, 0)
                    batch(it, 1)
                batch(BATCHES // 2 - 1, 0)
                batch(BATCHES // 2 - 1, 1, more=False)

        @block.vector
        def _(dve):
            done = [0]
            v = nc.vector

            def link(ins):
                done[0] += 1
                ins.then_inc(chain, 1)
                dve.wait_ge(chain, done[0])

            asked = [0]

            def ask(ins):
                asked[0] += 1
                ins.then_inc(setup_operand, 1)
                dve.wait_ge(setup_product, asked[0])

            v.memset(X[:, FULL:NBP, :], 0.0).then_inc(consts_done, 1)
            link(v.memset(ones[:, :], 1.0))
            v.memset(WE[:, :, :], 0.0).then_inc(consts_done, 1)
            v.memset(ACC[:, :, :], 0.0).then_inc(SEM["acc_step"], START["acc_step"])
            dve.wait_ge(SEM["acc_step"], START["acc_step"])
            link(v.memset(plan[:, :], 0.0))
            dve.wait_ge(iota_done, 3)
            link(v.tensor_scalar(ident[:, :], iota_row[:, :], iota_col[:, 0:1], None, ALU.is_equal))
            link(v.tensor_scalar(upper[:, :], iota_row[0:NB, 0:NB], iota_col[0:NB, 0:1], None, ALU.is_gt))
            link(v.tensor_scalar(plan[0:P, 0:1], iota_col[:, 0:1], 1.0, None, ALU.add))
            link(v.tensor_scalar(step_of[:, :], iota_row[0:NB, 0:NB], plan[0:NB, 0:1], None, ALU.is_equal))
            link(v.tensor_tensor(step_of[:, :], ident[0:NB, 0:NB], step_of[:, :], ALU.subtract))
            link(v.tensor_scalar(valid[:, :], iota_col[:, 0:1], float(REST), None, ALU.is_lt))

            dve.wait_ge(dst_in, 16)
            link(v.tensor_scalar(dst_i, dst_i, P.bit_length() - 1, None, ALU.logical_shift_right))
            link(v.tensor_copy(dst_block, dst_i))
            link(v.memset(cnt[:, 0:1], 0.0))
            link(v.memset(cnt[:, NB:NB + 1], float(EF)))
            for b in range(1, NB):
                link(v.tensor_scalar(less, dst_block, float(b), None, ALU.is_lt, ALU.add, accum_out=cnt[0:EP, b:b + 1]))
            ask(v.memset(plan[:, 7:8], 0.0))
            link(v.tensor_copy(plan[0:NB, 1:3], psA[0:NB, 0:2]))
            link(v.tensor_copy(tiles_i[0:NB, 0:1], plan[0:NB, 1:2]))
            link(v.tensor_scalar(tiles_i[0:NB, 1:2], plan[0:NB, 2:3], float(P - 1), None, ALU.add))
            link(v.tensor_scalar(tiles_i[0:NB, 0:2], tiles_i[0:NB, 0:2], P.bit_length() - 1, None,
                                 ALU.logical_shift_right))
            link(v.tensor_tensor(plan[0:NB, 3:4], tiles_i[0:NB, 1:2], tiles_i[0:NB, 0:1], ALU.subtract))
            link(v.tensor_tensor(plan[0:NB, 6:7], plan[0:NB, 2:3], plan[0:NB, 1:2], ALU.is_gt))
            ask(v.tensor_tensor(plan[0:NB, 3:4], plan[0:NB, 3:4], plan[0:NB, 6:7], ALU.mult))
            link(v.tensor_copy(plan[0:NB, 4:5], psA[0:NB, 2:3]))
            ask(v.tensor_tensor(plan[0:NB, 5:6], tiles_i[0:NB, 0:1], plan[0:NB, 4:5], ALU.subtract))
            link(v.tensor_copy(plan[0:NB, 6:7], psA[0:NB, 3:4]))
            link(v.tensor_scalar(edge_dv[:, :], ones[0:NB, :], plan[0:NB, 6:7], None, ALU.mult))
            ask(v.tensor_scalar(ind[0:NB, :], iota_k[0:NB, :], plan[0:NB, 4:5], None, ALU.is_ge))
            quarter = STEPS // 4
            for c in range(4):
                part = slice(c * quarter, (c + 1) * quarter)
                link(v.tensor_tensor(first[:, part], iota_k[:, part], sums[c // 2][:, c % 2, 0:quarter], ALU.add))
                link(v.tensor_scalar(block_of[:, part], (psA, psB, psC, psD)[c][:, 0:quarter], -1.0, None, ALU.add))
            by_chunk = [a.rearrange("p (c k) -> p c k", k=P) for a in (ind, keep)]
            link(v.tensor_scalar(ind, first, float(ET - 1), None, ALU.min))
            link(v.tensor_tensor(by_chunk[1], by_chunk[0], ident[:, :].unsqueeze(1).broadcast_to([P, KC, P]), ALU.mult))
            link(v.tensor_reduce(stat[:, 0, 0:KC], by_chunk[1], AX.X, ALU.add))
            v.tensor_copy(row_i[:, :], stat[:, 0, 0:KC]).then_inc(plan_ready, 1)
            link(v.tensor_scalar(first, first, float(P), None, ALU.mult))
            link(v.tensor_scalar(ind, first, float(E - P), None, ALU.min))
            v.tensor_copy(EB[32:33, :], ind[32:33, :])
            v.tensor_copy(EB[64:65, :], block_of[64:65, :]).then_inc(plan_ready, 1)
            link(v.tensor_tensor(keep, first, ind, ALU.subtract))
            link(v.tensor_scalar(keep, keep, iota_col[:, 0:1], None, ALU.is_le))
            ask(v.memset(plan[:, 7:8], 0.0))
            link(v.tensor_copy(WTS[:, W_IN:W_OUT + 1, :], psA[0:D, 0:5 * D].rearrange("p (w d) -> p w d", w=5)))

            roots = [0]

            def root(ins):
                roots[0] += 1
                ins.then_inc(var_ready, 1)
                dve.wait_ge(root_ready, roots[0])

            def over_blocks(vec):
                return vec.broadcast_to([P, NBP, D])

            def over_features(col):
                return col.unsqueeze(2).broadcast_to([P, NBP, D])

            def normalise():
                link(v.tensor_reduce(stat[:, 0, :], X[:, :, :], AX.X, ALU.add))
                link(v.tensor_scalar(stat[:, 0, :], stat[:, 0, :], 1.0 / D, None, ALU.mult))
                link(v.tensor_tensor(H[:, :, :], X[:, :, :], over_features(stat[:, 0, :]), ALU.subtract))
                link(v.tensor_tensor(ACCF, H[:, :, :], H[:, :, :], ALU.mult))
                link(v.tensor_reduce(stat[:, 0, :], ACCF, AX.X, ALU.add))
                root(v.tensor_scalar(stat[:, 0, :], stat[:, 0, :], 1.0 / D, LN_EPS, ALU.mult, ALU.add))
                link(v.reciprocal(stat[:, 0, :], stat[:, 1, :]))
                link(v.scalar_tensor_tensor(H[:, :, :], H[:, :, :], 0.0, over_features(stat[:, 0, :]), ALU.max, ALU.mult))

            dve.wait_ge(windows_in, 2 * KC * 16)
            link(v.tensor_copy(win_f[0], win_i[0]))
            ask(v.tensor_copy(win_f[1], win_i[1]))
            for c in range(0, STEPS, 512):
                n = min(512, STEPS - c)
                part = slice(c, c + n)
                link(v.tensor_copy(IDX[:, part], sums[c // 1024][:, c // 512 % 2, 0:n]))
                got = (psA, psB, psC, psD)[c // 512][:, 0:n]
                link(v.tensor_copy(dabs[:, part], got))
                link(v.scalar_tensor_tensor(first[:, part], block_of[:, part], -float(P), got, ALU.mult, ALU.add))
                link(v.scalar_tensor_tensor(first[:, part], first[:, part], 1.0, keep[:, part], ALU.add, ALU.mult))
                link(v.tensor_scalar(REL[:, part], first[:, part], -1.0, None, ALU.add))
            link(v.tensor_scalar(OUT[:, :], keep, -1.0, BIG, ALU.add, ALU.mult))
            by_row = [a.rearrange("p (c e) -> p c e", e=P) for a in (win_f[1], starts)]
            v.memset(by_row[1][:, :, 0:1], 0.0)
            v.memset(CUT[:, :, 0:1], 0.0)
            v.memset(CUT[:, :, P:P + 1], 0.0)
            v.tensor_copy(lane_of.rearrange("p q (t h) -> p (q t) h", h=HEADS),
                          ident[:, :].unsqueeze(2).broadcast_to([P, P, HEADS]))
            link(v.tensor_tensor(by_row[1][:, :, 1:P], by_row[0][:, :, 1:P], by_row[0][:, :, 0:P - 1], ALU.not_equal))

            for n, to in enumerate((begins, ends)):
                ask(v.tensor_scalar(edge_of[:, :], ones[:, :], ident[:, n * (P - 1):n * (P - 1) + 1], None, ALU.mult))
                for c in range(4):
                    link(v.tensor_copy(to[:, c * quarter:(c + 1) * quarter], sums[c // 2][:, c % 2, 0:quarter]))
            brk = [ACC_flat[:, n * STEPS:(n + 1) * STEPS] for n in range(1, 3)]
            link(v.tensor_tensor(brk[0], begins, ends, ALU.not_equal))
            link(v.memset(brk[1][:, 0:1], 1.0))
            link(v.tensor_tensor(brk[1][:, 1:STEPS], begins[:, 1:STEPS], ends[:, 0:STEPS - 1], ALU.not_equal))
            link(v.tensor_scalar(JOIN[:, :], brk[1][0:1, 0:TILES:BT], -1.0, 1.0, ALU.mult, ALU.add))
            link(v.tensor_tensor_scan(ends, brk[1], brk[0], 0.0, ALU.add, ALU.add))
            link(v.tensor_tensor(begins, ends, brk[0], ALU.subtract))
            own = [stat[:, n, :] for n in range(2)]
            tile_of = chained[:, 5 * P:5 * P + BT]
            link(v.tensor_reduce(tile_of, ident[:, :].rearrange("p (t h) -> p t h", h=HEADS), AX.X, ALU.add))
            counts = [a[:, 0:TILES].rearrange("p (b t) -> p b t", t=BT) for a in (begins, ends)]
            for n in range(2):
                link(v.tensor_tensor(by_tile, counts[n], tile_of.unsqueeze(1).broadcast_to([P, BATCHES, BT]), ALU.mult))
                link(v.tensor_reduce(own[n][:, 0:BATCHES], by_tile, AX.X, ALU.add))
            head_i = chained[:, 0:P].bitcast(i32)
            same = chained[:, P:2 * P]
            side = chained[:, 2 * P:3 * P]
            head_f = chained[:, 3 * P:4 * P]
            side16 = chained[:, 4 * P:5 * P].bitcast(bf16)[:, 0:P]
            dve.wait_ge(lane_no_ready, 2)
            link(v.tensor_scalar(head_i, lane_no[:, 0:P], HEADS - 1, None, ALU.bitwise_and))
            link(v.tensor_copy(head_f, head_i))
            link(v.tensor_scalar(head_i[:, 0:1], lane_no[:, P:P + 1], HEADS - 1, None, ALU.bitwise_and))
            link(v.tensor_copy(lone[:, 0:1], head_i[:, 0:1]))
            link(v.tensor_scalar(same, head_f, lone[:, 0:1], None, ALU.is_equal))
            for n, (to, order) in enumerate(((FORE[:, :, 0:P], ALU.is_lt), (AFT[:, :, :], ALU.is_gt))):
                link(v.tensor_scalar(side, iota_row[:, :], iota_col[:, 0:1], None, order))
                link(v.tensor_tensor(side, side, same, ALU.mult))
                link(v.tensor_scalar(side16, side, -1.0, BIG, ALU.add, ALU.mult))
                link(v.tensor_tensor(by_tile, counts[1 - n], own[n][:, 0:BATCHES].unsqueeze(2).broadcast_to([P, BATCHES, BT]),
                                     ALU.is_equal))
                link(v.tensor_scalar(by_tile16, by_tile, -1.0, BIG, ALU.add, ALU.mult))
                link(v.tensor_tensor(to.rearrange("p b (t h) -> p b t h", h=HEADS),
                                     by_tile16.unsqueeze(3).broadcast_to([P, BATCHES, BT, HEADS]),
                                     side16.rearrange("p (t h) -> p t h", h=HEADS).unsqueeze(1)
                                     .broadcast_to([P, BATCHES, BT, HEADS]), ALU.min))
            prior = HOT_flat[:, STEPS:STEPS + BATCHES * HEADS].rearrange("p (b h) -> p b h", h=HEADS)
            link(v.memset(prior, 0.0))
            link(v.tensor_tensor(prior[:, 1:BATCHES, :],
                                 ends[:, BT - 1:TILES - 1:BT].unsqueeze(2).broadcast_to([P, BATCHES - 1, HEADS]),
                                 own[0][:, 1:BATCHES].unsqueeze(2).broadcast_to([P, BATCHES - 1, HEADS]), ALU.is_equal))
            link(v.tensor_tensor(prior, prior, same[:, 0:HEADS].unsqueeze(1).broadcast_to([P, BATCHES, HEADS]), ALU.mult))
            link(v.tensor_scalar(FORE[:, :, P:P + HEADS], prior, -1.0, BIG, ALU.add, ALU.mult))

            dve.wait_ge(x_in, 32)
            dve.wait_ge(const_in, 14 * 16)
            normalise()
            v.memset(G[:, 0:UN, :, D:D + 1], 1.0).then_inc(table_ready, 1)
            link(v.memset(ACC[:, :, :], 0.0))

            def build_hot(half, k):
                v.tensor_tensor(HOT[:, half, :, :], iota_row[:, :].unsqueeze(1).broadcast_to([P, U, P]),
                                REL[:, ds(k, U)].unsqueeze(2).broadcast_to([P, U, P]), ALU.is_equal)\
                 .then_inc(SEM["hot_built"], 1)

            def add_up(t, it, unroll, n, width):
                b = blocks(unroll * U * it + U * n, U, DVE)
                dve.wait_ge(SEM["seg_done"], unroll * it + (t.base["seg_done"] + n + 1))
                for k in range(U):
                    to = ACC[:, ds(b[k], 1), 0:width].squeeze(1)
                    v.tensor_tensor(to, to, sums[n % 2][:, k // 4, k % 4 * width:(k % 4 + 1) * width], ALU.add)\
                     .then_inc(SEM["acc_step"], 1)
                    dve.wait_ge(SEM["acc_step"], unroll * U * it + (t.base["acc_step"] + U * n + k + 1))

            def sum_stage(t, width, prepare):
                def ready(it, j):
                    dve.wait_ge(SEM["seg_done"], UN * it + (freed(t, 2) + j + 1))
                    build_hot(j % 2, UN * U * it + U * j)
                    if prepare:
                        prepare(it, j)

                def sources(it, pair):
                    v.tensor_copy(NOW[:, pair, 0:2 * U], IDX[:, ds(UN * U * it + 2 * U * pair, 2 * U)])\
                     .then_inc(SEM["idx_ready"], 1)

                def turn(it, slots):
                    for j in slots:
                        if j < UN - 1:
                            ready(it, j + 1)
                        else:
                            ready(it + 1, 0)
                        add_up(t, it, UN, j, width)
                        if j % 2 and len(slots) == UN:
                            sources(it + 1, j // 2)
                for pair in range(UN // 2):
                    sources(0, pair)
                ready(0, 0)
                with dve.Fori(0, ROUNDS - 1) as it:
                    turn(it, range(UN))
                turn(ROUNDS - 1, range(UN - 1))
                add_up(t, ROUNDS - 1, UN, UN - 1, width)

            def take(t, use, banks=(psD, psC), prepare=None):
                def use_group(g, half):
                    dve.wait_ge(SEM["made"], g + (t.base["made"] + 1))
                    use(g, banks[half][:, 0:Q * D].rearrange("p (b d) -> p b d", b=Q)).then_inc(SEM["taken"], 1)

                def prepare_group(g):
                    ins = prepare(g)
                    ins.then_inc(SEM["prepared"], 1)

                if not prepare:
                    v.memset(plan[:, 7:8], 0.0).then_inc(SEM["prepared"], NG)
                    in_pairs(dve, use_group)
                else:
                    for g in range(AHEAD):
                        prepare_group(g)
                    with dve.Fori(0, (NG - AHEAD) // 2) as pair:
                        for half in range(2):
                            prepare_group(2 * pair + half + AHEAD)
                            use_group(2 * pair + half, half)
                    for g in range(NG - AHEAD, NG):
                        use_group(g, g % 2)
                dve.wait_ge(SEM["taken"], t.end["taken"])

            t0 = Stage("L0")

            def add_attr(it, j):
                half = j % 2
                dve.wait_ge(t0.gathered[j], 16 * U * it + 16 * U)
                dve.wait_ge(SEM[f"attr_in{half}"],
                            16 * U * UN // 2 * it + (t0.base[f"attr_in{half}"] + 16 * U * (j // 2 + 1)))
                v.tensor_tensor(G[:, j, :, 0:D], G[:, j, :, 0:D],
                                EA[:, half, :].rearrange("p (k d) -> p k d", k=U), ALU.add)\
                 .then_inc(SEM["rows_ready"], 1)
            sum_stage(t0, D + 1, add_attr)
            root(v.tensor_scalar(dinv[:, :], ACC[:, :, D], 1.0, None, ALU.add))
            link(v.reciprocal(dinv[:, :], dinv[:, :]))
            link(v.tensor_scalar(epsp[:, :], epsp[:, :], 1.0, None, ALU.add))
            link(v.scalar_tensor_tensor(X[:, :, :], H[:, :, :], epsp[:, 0:1], X[:, :, :], ALU.mult, ALU.add))
            link(v.tensor_tensor(X[:, :, :], X[:, :, :], over_blocks(row(R_L0B2)), ALU.add))
            take(Stage("L0mlp"), lambda g, p: v.tensor_tensor(X[:, ds(Q * g, Q), :], p, X[:, ds(Q * g, Q), :], ALU.add),
                 banks=(psD, psD))
            normalise()

            link(v.tensor_tensor(ACCF, H[:, :, :], over_blocks(row(R_BE)), ALU.add))
            v.memset(plan[:, 7:8], 0.0).then_inc(table_ready, 1)
            dve.wait_ge(table_stored, STORED[1])
            link(v.tensor_copy(ACCF, H[:, :, :]))
            t1 = Stage("L1")

            def add_product(it, j):
                dve.wait_ge(t1.gathered[j], 16 * U * it + 16 * U)
                for q in range(2):
                    dve.wait_ge(SEM["ea_product"], 2 * UN * it + (t1.base["ea_product"] + 2 * j + q + 1))
                    v.tensor_tensor(G[:, j, 4 * q:4 * q + 4, 0:D], G[:, j, 4 * q:4 * q + 4, 0:D],
                                    (psB, psC)[q][:, 0:4 * D].rearrange("p (k d) -> p k d", k=4), ALU.add)\
                     .then_inc(SEM["summed"], 1)
            sum_stage(t1, D, add_product)
            take(Stage("L1mlp"), lambda g, p: v.tensor_tensor(
                H[:, ds(Q * g, Q), :], p, row(R_L1B2).broadcast_to([P, Q, D]), ALU.add), banks=(psD, psD))
            hot0, hot1 = HOT[:, 0, 0, 0:D], HOT[:, 0, 1, 0:D]
            by_feature = H[:, 0:NB, :].rearrange("p b d -> p d b")
            link(v.tensor_scalar(H[:, NB - 1, :], H[:, NB - 1, :], valid[:, 0:1], None, ALU.mult))
            v.tensor_reduce(hot0, by_feature, AX.X, ALU.add).then_inc(feature_sums, 1)
            dve.wait_ge(feature_totals, 1)
            link(v.tensor_scalar(hot0, psB[:, 0:D], 1.0 / N, None, ALU.mult))
            link(v.tensor_tensor(H[:, :, :], H[:, :, :], over_blocks(HOT[:, 0, 0:1, 0:D]), ALU.subtract))
            link(v.tensor_scalar(H[:, NB - 1, :], H[:, NB - 1, :], valid[:, 0:1], None, ALU.mult))
            link(v.tensor_tensor(ACCF, H[:, :, :], H[:, :, :], ALU.mult))
            v.tensor_reduce(hot1, ACC[:, 0:NB, 0:D].rearrange("p b d -> p d b"), AX.X, ALU.add).then_inc(feature_sums, 1)
            dve.wait_ge(feature_totals, 2)
            hot2 = HOT[:, 0, 2, 0:D]
            link(v.tensor_scalar(hot2, psB[:, D:2 * D], 1.0 / N, BN_EPS, ALU.mult, ALU.add))
            root(v.tensor_copy(hot1, hot2))
            link(v.reciprocal(hot0, hot1))
            link(v.tensor_tensor(hot0, hot0, ROWS[:, R_GAMMA, :], ALU.mult))
            link(v.tensor_tensor(H[:, :, :], H[:, :, :], over_blocks(HOT[:, 0, 0:1, 0:D]), ALU.mult))
            link(v.tensor_tensor(H[:, :, :], H[:, :, :], over_blocks(row(R_BETA)), ALU.add))
            link(v.scalar_tensor_tensor(X[:, :, :], H[:, :, :], 0.0, X[:, :, :], ALU.max, ALU.add))
            normalise()

            take(Stage("in"), lambda g, p: v.tensor_tensor(
                H[:, ds(Q * g, Q), :], p, row(R_BIN).broadcast_to([P, Q, D]), ALU.add))

            def prepare_hop(l, t):
                def prepare(g):
                    part = ds(Q * g, Q)
                    into, agg = H[:, part, :], ACC[:, part, 0:D]
                    if l == 0:
                        return v.tensor_scalar(into, into, 0.0, None, ALU.max)

                    def hop_step(ins, n):
                        ins.then_inc(SEM["hop_step"], 1)
                        dve.wait_ge(SEM["hop_step"], 2 * g + (t.base["hop_step"] + n))
                    hop_step(v.tensor_tensor(agg, agg, dinv[:, part].unsqueeze(2).broadcast_to([P, Q, D]), ALU.mult), 1)
                    hop_step(v.tensor_tensor(agg, agg, row(R_GCNB + l - 1).broadcast_to([P, Q, D]), ALU.add), 2)
                    return v.scalar_tensor_tensor(into, agg, 0.0, into, ALU.max, ALU.add)
                return prepare

            for l in range(LAYERS):
                t = Stage(f"gcn{l}")
                take(t, lambda g, p: v.tensor_tensor(
                    ACC[:, ds(Q * g, Q), 0:D], p, dinv[:, ds(Q * g, Q)].unsqueeze(2).broadcast_to([P, Q, D]), ALU.mult),
                    prepare=prepare_hop(l, t))
                dve.wait_ge(table_stored, STORED[2 + l])
                sum_stage(Stage(f"gcnsum{l}"), D, None)
            link(v.tensor_tensor(X[:, :, :], X[:, :, :], over_blocks(row(R_BOUT)), ALU.add))
            t = Stage("out")
            take(t, lambda g, p: v.tensor_tensor(X[:, ds(Q * g, Q), :], p, X[:, ds(Q * g, Q), :], ALU.add),
                 prepare=prepare_hop(LAYERS, t))
            normalise()

            for l in range(LAYERS):
                score = Stage(f"gat{l}")

                def attend_to(g, p):
                    part = ds(Q * g, Q)
                    by_head = [H[:, part, :], HOT_flat[:, 0:Q * D].rearrange("p (b d) -> p b d", b=Q)]
                    dve.wait_ge(SEM["taken"], g + score.base["taken"])
                    v.tensor_copy(ACC[:, part, 0:D], p)
                    for n, r in enumerate((R_ASRC, R_ADST)):
                        last = v.tensor_tensor(by_head[n], p, row(r + l).broadcast_to([P, Q, D]), ALU.mult)
                    last.then_inc(SEM["scored"], 1)
                    dve.wait_ge(SEM["scored"], g + (score.base["scored"] + 1))
                    for n, to in enumerate((ACC[:, part, D:WT], DD[:, part, :])):
                        last = v.tensor_reduce(to, by_head[n].rearrange("p b (h c) -> p b h c", h=HEADS), AX.X, ALU.add)
                    return last
                take(score, attend_to)
                for s in range(PARTS):
                    link(v.tensor_copy(DDP[:, :, s, :], DD[:, :, :]))
                    if s < PARTS - 1:
                        link(v.tensor_tensor(DD[:, :, :], DD[:, :, :], DDP[:, :, s, :], ALU.subtract))
                dve.wait_ge(table_stored, STORED[2 + LAYERS + l])

                def sources(it, half):
                    v.tensor_copy(NOW[:, half, :], IDX[:, ds(2 * BT * it + BT * half, BT)])\
                     .then_inc(SEM["idx_ready"], 1)
                for half in range(2):
                    sources(0, half)
                link(v.memset(ACC[:, :, :], 0.0))
                dve.wait_ge(cuts_copied, len(CUTS))
                link(v.memset(lone[:, :], -BIG))
                t = Stage(f"attend{l}")
                leaky = lambda to, of: v.scalar_tensor_tensor(to, of, SLOPE, of, ALU.mult, ALU.max)

                run, scan, diag = LW[:, 0, 0:P], LW[:, 1, 0:P], LW[:, 2, :]
                top, worth = LW[:, 1, 0:P], lone[0:1, 4:8]

                class Lanes:

                    def __init__(self, it, half, steps, asks):
                        self.it, self.half, self.steps, self.asks = it, half, steps, asks

                    def step(self, ins):
                        self.steps += 1
                        ins.then_inc(SEM["lane_step"], 1)

                    def steps_done(self):
                        dve.wait_ge(SEM["lane_step"], 2 * LANE_STEPS * self.it
                                    + (t.base["lane_step"] + LANE_STEPS * self.half + self.steps))

                    def ask(self, ins):
                        self.asks += 1
                        ins.then_inc(SEM["lane_ask"], 1)

                    def reply(self):
                        dve.wait_ge(SEM["lane_reply"], 2 * LANE_ASKS * self.it
                                    + (t.base["lane_reply"] + LANE_ASKS * self.half + self.asks))

                def head(it, half, adds):
                    lanes = Lanes(it, half, 0, 0)
                    step, steps_done, ask_lane, reply = lanes.step, lanes.steps_done, lanes.ask, lanes.reply
                    batch_no = 2 * it + half
                    for q in range(BG):
                        dve.wait_ge(t.gathered[BG * half + q], 16 * U * it + 16 * U)
                    ask_lane(v.tensor_tensor(SB3, G[:, BG * half:BG * (half + 1), :, D:WT].rearrange("p s k h -> p (s k) h"),
                                             OUT[:, ds(BT * batch_no, BT)].unsqueeze(2).broadcast_to([P, BT, HEADS]),
                                             ALU.add))
                    step(v.tensor_copy(cut_now[:, :], CUT[:, ds(batch_no, 1), :].squeeze(1)))
                    step(v.tensor_scalar(diag[:, P:P + HEADS], ident[:, P - HEADS:P], lone[:, 1:2], None, ALU.mult))
                    adds(2)
                    steps_done()
                    reply()
                    step(v.tensor_tensor_scan(run, cut_now[:, 0:P], psD[:, 0:P], -BIG, ALU.add, ALU.max))
                    adds(1)
                    steps_done()
                    ask_lane(v.tensor_scalar(diag[:, 0:P], ident[:, :], run[:, P - 1:P], None, ALU.mult))
                    adds(3)
                    reply()
                    step(v.tensor_tensor(LW[:, 3, :], psD[:, P:2 * P + HEADS],
                                         FORE[:, ds(batch_no, 1), :].squeeze(1), ALU.add))
                    step(v.tensor_copy(worth, psD[0:1, 2 * P:2 * P + HEADS]))
                    adds(1)
                    steps_done()
                    step(v.tensor_reduce(lone[:, 0:1], LW[:, 3, :], AX.X, ALU.max))
                    adds(1)
                    steps_done()
                    step(v.tensor_tensor_scan(run, cut_now[:, 0:P], psD[:, 0:P], lone[:, 0:1], ALU.add, ALU.max))
                    adds(1)
                    steps_done()
                    step(v.tensor_tensor_scan(scan[:, ::-1], cut_now[:, P:0:-1], run[:, ::-1], -BIG, ALU.add, ALU.max))
                    step(v.tensor_copy(lone[:, 1:2], run[:, P - 1:P]))
                    adds(1)
                    steps_done()
                    ask_lane(v.tensor_scalar(diag[:, 0:P], ident[:, :], scan[:, 0:1], None, ALU.mult))
                    adds(4)
                    reply()
                    step(v.tensor_tensor(LW[:, 3, 0:P], psD[:, P:2 * P], AFT[:, ds(batch_no, 1), :].squeeze(1), ALU.add))
                    adds(1)
                    steps_done()
                    step(v.tensor_reduce(lone[:, 0:1], LW[:, 3, 0:P], AX.X, ALU.max))
                    adds(1)
                    steps_done()
                    ask_lane(v.tensor_tensor_scan(run[:, ::-1], cut_now[:, P:0:-1], run[:, ::-1], lone[:, 0:1],
                                                  ALU.add, ALU.max))
                    assert (lanes.steps, lanes.asks) == (HEAD_STEPS, HEAD_ASKS)

                def tail(it, half):
                    lanes = Lanes(it, half, HEAD_STEPS, HEAD_ASKS)
                    step, steps_done, ask_lane, reply = lanes.step, lanes.steps_done, lanes.ask, lanes.reply
                    batch_no = 2 * it + half
                    d_logit = LW[:, 3, 0:P]
                    dve.wait_ge(SEM["d_copied"], 8 * it + (t.base["d_copied"] + BG * half + BG))
                    step(v.tensor_reduce(d_logit.rearrange("p (t h) -> p t h", h=HEADS),
                                         DL[:, half, :].rearrange("p (t s h) -> p t h s", s=PARTS, h=HEADS),
                                         AX.X, ALU.add))
                    steps_done()
                    step(v.tensor_tensor(SB[:, :], SB[:, :], d_logit, ALU.add))
                    step(v.tensor_tensor(worth, worth, d_logit[0:1, 0:HEADS], ALU.add))
                    reply()
                    step(v.tensor_tensor(top, psD[:, 2 * P:3 * P], d_logit, ALU.add))
                    steps_done()
                    step(leaky(SB[:, :], SB[:, :]))
                    step(leaky(worth, worth))
                    step(leaky(top, top))
                    steps_done()
                    v.tensor_tensor(SB[:, :], SB[:, :], top, ALU.subtract).then_inc(SEM["exponent"], 1)
                    step(v.tensor_tensor(worth, worth, top[0:1, 0:HEADS], ALU.subtract))
                    steps_done()
                    v.tensor_scalar(worth, worth, JOIN[:, ds(batch_no, 1)], None, ALU.mult)\
                     .then_inc(SEM["exponent"], 1)
                    dve.wait_ge(SEM["exp_made"], 4 * it + (t.base["exp_made"] + 2 * half + 2))
                    ask_lane(v.tensor_scalar(worth, worth, -1.0, None, ALU.add))
                    reply()
                    step(v.tensor_scalar(scales[:, :], psD[:, 3 * P:3 * P + HEADS], 1.0, None, ALU.add))
                    b = blocks(2 * BT * it + BT * half, 1, DVE)
                    dve.wait_ge(SEM["acc_step"], 8 * U * it + (t.base["acc_step"] + BT * half))
                    steps_done()
                    node = ACC[:, ds(b[0], 1), :].squeeze(1)
                    sums_of_node = node[:, 0:D].rearrange("p (h c) -> p h c", h=HEADS)
                    step(v.tensor_tensor(sums_of_node, sums_of_node,
                                         scales[:, :].unsqueeze(2).broadcast_to([P, HEADS, C]), ALU.mult))
                    step(v.tensor_tensor(node[:, D:WT], node[:, D:WT], scales[:, :], ALU.mult))
                    assert (lanes.steps, lanes.asks) == (LANE_STEPS, LANE_ASKS)

                def weigh(slot):
                    rows = G[:, slot, :, 0:D].rearrange("p k (h c) -> p k h c", h=HEADS)
                    w = WB[:, slot % BG * U:(slot % BG + 1) * U, :]
                    v.tensor_tensor(rows, rows, w.unsqueeze(3).broadcast_to([P, U, HEADS, C]), ALU.mult)\
                     .then_inc(SEM["rows_ready"], 1)

                class Adds:

                    def __init__(self, it, half):
                        self.it, self.half, self.tile, self.blocks = it, half, 0, None

                    def __call__(self, n):
                        for k in range(self.tile, self.tile + n):
                            group = BG * self.half + k // U
                            if k % U == 0:
                                self.blocks = blocks(8 * U * self.it + U * group, U, DVE)
                                dve.wait_ge(SEM["seg_done"], 8 * self.it + (t.base["seg_done"] + group + 1))
                            if k == 0:
                                dve.wait_ge(SEM["lane_step"], 2 * LANE_STEPS * self.it
                                            + (t.base["lane_step"] + LANE_STEPS * (self.half + 1)))
                            else:
                                dve.wait_ge(SEM["acc_step"], 8 * U * self.it + (t.base["acc_step"] + BT * self.half + k))
                            to = ACC[:, ds(self.blocks[k % U], 1), :].squeeze(1)
                            v.tensor_tensor(to, to, sums[group % 2][:, k % U // 4, k % 4 * WT:(k % 4 + 1) * WT], ALU.add)\
                             .then_inc(SEM["acc_step"], 1)
                        self.tile += n

                def batch(it, half, more=True, last=False):
                    tail(it, half)
                    if not last:
                        sources(it + 1, half)
                    adds = Adds(it, half)

                    def hot_next(q):
                        if more:
                            build_hot(BG * (1 - half) + q, 8 * U * it + U * (BG * (half + 1) + q))
                    weigh(BG * half)
                    weigh(BG * half + 1)
                    hot_next(0)
                    weigh(BG * half + 2)
                    hot_next(1)
                    adds(1)
                    weigh(BG * half + 3)
                    adds(1)
                    hot_next(2)
                    adds(1)
                    hot_next(3)
                    adds(5)
                    if more:
                        head(it + half, 1 - half, adds)
                    adds(BT - adds.tile)

                for q in range(BG):
                    build_hot(q, U * q)
                head(0, 0, lambda n: None)
                with dve.Fori(0, BATCHES // 2 - 1) as it:
                    batch(it, 0)
                    batch(it, 1)
                batch(BATCHES // 2 - 1, 0, last=True)
                batch(BATCHES // 2 - 1, 1, more=False, last=True)
                dve.wait_ge(SEM["acc_step"], t.end["acc_step"])
                link(v.tensor_scalar(ACC[:, :, D:WT], ACC[:, :, D:WT], 1e-16, None, ALU.add))
                link(v.reciprocal(ACC[:, :, D:WT], ACC[:, :, D:WT]))
                for h in range(HEADS):
                    part = ACC[:, :, h * C:(h + 1) * C]
                    link(v.tensor_tensor(part, part, ACC[:, :, D + h:D + h + 1].broadcast_to([P, NBP, C]), ALU.mult))
                link(v.tensor_tensor(ACCF, ACCF, over_blocks(row(R_GATB + l)), ALU.add))
                if l < LAYERS - 1:
                    link(v.tensor_scalar(H[:, :, :], ACCF, 0.0, None, ALU.max))
            v.scalar_tensor_tensor(X[:, :, :], ACCF, 0.0, X[:, :, :], ALU.max, ALU.add).then_inc(result_ready, 1)


_INS = ["x", "src", "dst", "edge_attr_32", "edge_attr_96", "L0_gnn_W1", "L0_gnn_b1", "L0_gnn_W2", "L0_gnn_b2",
        "L0_gnn_eps", "L1_gnn_We", "L1_gnn_be", "L1_gnn_W1", "L1_gnn_b1", "L1_gnn_W2", "L1_gnn_b2", "L1_gnn_gamma",
        "L1_gnn_beta", "L2_gnn_W_in", "L2_gnn_b_in", "L2_gnn_gcn_W", "L2_gnn_gcn_b", "L2_gnn_W_out", "L2_gnn_b_out",
        "L3_gnn_W", "L3_gnn_att_src", "L3_gnn_att_dst", "L3_gnn_bias"]


def kernel(**inputs):
    import numpy as _np
    import concourse.bacc as _bacc
    from concourse import mybir as _mybir
    from concourse.bass_utils import run_bass_kernel_spmd as _run

    nc = _bacc.Bacc("TRN2", target_bir_lowering=False, num_devices=1)
    arrays, args = {}, []
    for name in _INS:
        a = _np.ascontiguousarray(inputs[name])
        arrays[f"in_{name}_dram"] = a
        args.append(nc.dram_tensor(f"in_{name}_dram", a.shape, _mybir.dt.from_np(a.dtype), kind="ExternalInput").ap())
    shape = arrays["in_x_dram"].shape
    result = nc.dram_tensor("out_0_dram", shape, _mybir.dt.float32, kind="ExternalOutput").ap()
    gnn_kernel(nc, *args, result)
    r = _run(nc, [arrays], core_ids=[0])
    return r.results[0]["out_0_dram"]
```
